# Optimizing a Trainium2 kernel written in Bass

```python
import numpy as np
import jax
import jax.numpy as jnp

def _softmax(x, axis=-1):
    return jax.nn.softmax(x, axis=axis)

def _gelu(x):
    return jax.nn.gelu(x, approximate=True)

def _silu(x):
    return jax.nn.silu(x)

def _sigmoid(x):
    return jax.nn.sigmoid(x)

def _layernorm(x, axis=-1, eps=1e-05):
    m = jnp.mean(x, axis=axis, keepdims=True)
    v = jnp.var(x, axis=axis, keepdims=True)
    return (x - m) / jnp.sqrt(v + eps)

def _scatter_add(tgt, idx, src, axis=0):
    return tgt.at[idx].add(src)

def _segment_sum(src, seg, n):
    return jax.ops.segment_sum(src, seg, n)
kernel_name = 'mk_macaron_d2_jaxref_r8_6a3c23'

def setup_inputs(seed: int=0):
    np.random.seed(seed)
    _w = jnp.asarray

    def _L0_attn_setup():
        import jax, jax.numpy as jnp
        import numpy as np
        Q_DIM = 512
        N_HEADS = 32
        HEAD_DIM = 128
        INNER = N_HEADS * HEAD_DIM
        EPS = 1e-06

        def rms_norm(x, w):
            xf = x.astype(jnp.float32)
            var = jnp.mean(xf * xf, axis=-1, keepdims=True)
            return (w.astype(jnp.float32) * xf * jax.lax.rsqrt(var + EPS)).astype(x.dtype)
        key = jax.random.key(seed)
        ks = jax.random.split(key, 12)
        s = 1.0 / np.sqrt(Q_DIM)
        return {'hidden_states': jax.random.normal(ks[0], (2, 256, Q_DIM), dtype=jnp.float32), 'Wq': jax.random.normal(ks[1], (Q_DIM, INNER), dtype=jnp.float32) * s, 'bq': jnp.zeros((INNER,), dtype=jnp.float32), 'Wk': jax.random.normal(ks[2], (Q_DIM, INNER), dtype=jnp.float32) * s, 'bk': jnp.zeros((INNER,), dtype=jnp.float32), 'Wv': jax.random.normal(ks[3], (Q_DIM, INNER), dtype=jnp.float32) * s, 'bv': jnp.zeros((INNER,), dtype=jnp.float32), 'Wo': jax.random.normal(ks[4], (INNER, Q_DIM), dtype=jnp.float32) * s, 'bo': jnp.zeros((Q_DIM,), dtype=jnp.float32), 'gq': jnp.ones((INNER,), dtype=jnp.float32), 'gk': jnp.ones((INNER,), dtype=jnp.float32)}
    _L0_attn_in = _L0_attn_setup()

    def _L0_ffn_setup():
        import jax, jax.numpy as jnp
        import numpy as np
        M = 512
        K = 512

        def _make_2to4_mask(key, shape):
            scores = jax.random.normal(key, shape)
            g = scores.reshape(shape[0], shape[1] // 4, 4)
            rank = jnp.argsort(jnp.argsort(-jnp.abs(g), axis=-1), axis=-1)
            return (rank < 2).reshape(shape).astype(jnp.float32)
        key = jax.random.key(seed)
        k_x, k_w12, k_b12, k_w3, k_b3, k_m = jax.random.split(key, 6)
        x = jax.random.normal(k_x, (4, 256, K), dtype=jnp.float32)
        w12_dense = jax.random.normal(k_w12, (2 * M, K), dtype=jnp.float32) * (1.0 / np.sqrt(K))
        mask12 = _make_2to4_mask(k_m, (2 * M, K))
        w12 = w12_dense * mask12
        b12 = jax.random.normal(k_b12, (2 * M,), dtype=jnp.float32) * 0.01
        w3 = jax.random.normal(k_w3, (M, M), dtype=jnp.float32) * (1.0 / np.sqrt(M))
        b3 = jax.random.normal(k_b3, (M,), dtype=jnp.float32) * 0.01
        return {'x': x, 'w12': w12, 'b12': b12, 'w3': w3, 'b3': b3}
    _L0_ffn_in = _L0_ffn_setup()

    def _L1_attn_setup():
        import jax, jax.numpy as jnp
        import numpy as np
        B, S, HID = (2, 512, 512)
        H, HKV, D = (32, 8, 128)
        G = H // HKV
        EPS = 1e-06

        def _reference_tuple_inner(hidden_states, Wq, bq, Wk, bk, Wv, bv, Wo, M, z):
            b, s, _ = hidden_states.shape
            q = (hidden_states @ Wq.T + bq).reshape(b, s, H, D)
            k = (hidden_states @ Wk.T + bk).reshape(b, s, HKV, D)
            v = (hidden_states @ Wv.T + bv).reshape(b, s, HKV, D)
            sig_q = jax.nn.elu(q) + 1.0
            sig_k = jax.nn.elu(k) + 1.0
            q_sel = sig_q[:, :, ::G, :]
            num = jnp.einsum('bshd,hde->bshe', q_sel, M)
            den = jnp.einsum('bshd,hd->bsh', q_sel, z)[..., None] + EPS
            retrieved = num / den
            out_heads = jnp.repeat(retrieved, G, axis=2)
            output = out_heads.reshape(b, s, H * D) @ Wo.T
            M_new = M + jnp.einsum('bshd,bshe->hde', sig_k, v)
            z_new = z + sig_k.sum(axis=(0, 1))
            return (output, M_new, z_new)
        key = jax.random.key(seed)
        ks = jax.random.split(key, 10)
        s = 0.02
        return {'hidden_states': jax.random.normal(ks[0], (B, S, HID), jnp.float32), 'Wq': jax.random.normal(ks[1], (H * D, HID), jnp.float32) * s, 'bq': jnp.zeros((H * D,), jnp.float32), 'Wk': jax.random.normal(ks[2], (HKV * D, HID), jnp.float32) * s, 'bk': jnp.zeros((HKV * D,), jnp.float32), 'Wv': jax.random.normal(ks[3], (HKV * D, HID), jnp.float32) * s, 'bv': jnp.zeros((HKV * D,), jnp.float32), 'Wo': jax.random.normal(ks[4], (HID, H * D), jnp.float32) * s, 'M': jax.random.normal(ks[5], (HKV, D, D), jnp.float32), 'z': jax.random.uniform(ks[6], (HKV, D), jnp.float32) * 100.0 + 1.0}
    _L1_attn_in = _L1_attn_setup()

    def _L1_ffn_setup():
        import jax, jax.numpy as jnp
        import numpy as np
        HIDDEN = 512
        INTER = 1376

        def _ternary_quantize(w):
            scale = jnp.mean(jnp.abs(w))
            return jnp.clip(jnp.round(w / scale), -1.0, 1.0) * scale
        key = jax.random.key(seed)
        kx, kg, ku, kd = jax.random.split(key, 4)
        x = jax.random.normal(kx, (2, 256, HIDDEN), dtype=jnp.float32)
        w_gate = _ternary_quantize(jax.random.normal(kg, (INTER, HIDDEN), dtype=jnp.float32) * 0.02)
        w_up = _ternary_quantize(jax.random.normal(ku, (INTER, HIDDEN), dtype=jnp.float32) * 0.02)
        w_down = _ternary_quantize(jax.random.normal(kd, (HIDDEN, INTER), dtype=jnp.float32) * 0.02)
        return {'x': x, 'w_gate': w_gate, 'w_up': w_up, 'w_down': w_down}
    _L1_ffn_in = _L1_ffn_setup()
    _d = {'L0_attn_hidden_states': _L0_attn_in['hidden_states'], 'L0_attn_Wq': _L0_attn_in['Wq'], 'L0_attn_bq': _L0_attn_in['bq'], 'L0_attn_Wk': _L0_attn_in['Wk'], 'L0_attn_bk': _L0_attn_in['bk'], 'L0_attn_Wv': _L0_attn_in['Wv'], 'L0_attn_bv': _L0_attn_in['bv'], 'L0_attn_Wo': _L0_attn_in['Wo'], 'L0_attn_bo': _L0_attn_in['bo'], 'L0_attn_gq': _L0_attn_in['gq'], 'L0_attn_gk': _L0_attn_in['gk'], 'L0_ffn_w12': _L0_ffn_in['w12'], 'L0_ffn_b12': _L0_ffn_in['b12'], 'L0_ffn_w3': _L0_ffn_in['w3'], 'L0_ffn_b3': _L0_ffn_in['b3'], 'L1_attn_Wq': _L1_attn_in['Wq'], 'L1_attn_bq': _L1_attn_in['bq'], 'L1_attn_Wk': _L1_attn_in['Wk'], 'L1_attn_bk': _L1_attn_in['bk'], 'L1_attn_Wv': _L1_attn_in['Wv'], 'L1_attn_bv': _L1_attn_in['bv'], 'L1_attn_Wo': _L1_attn_in['Wo'], 'L1_attn_M': _L1_attn_in['M'], 'L1_attn_z': _L1_attn_in['z'], 'L1_ffn_w_gate': _L1_ffn_in['w_gate'], 'L1_ffn_w_up': _L1_ffn_in['w_up'], 'L1_ffn_w_down': _L1_ffn_in['w_down']}
    _x0 = _d['L0_attn_hidden_states']
    _d['L0_attn_hidden_states'] = jax.random.normal(jax.random.fold_in(jax.random.key(seed), 1), (1, 1024, 512), dtype=_x0.dtype)
    del _x0
    return _d

def reference(L0_attn_hidden_states, L0_attn_Wq, L0_attn_bq, L0_attn_Wk, L0_attn_bk, L0_attn_Wv, L0_attn_bv, L0_attn_Wo, L0_attn_bo, L0_attn_gq, L0_attn_gk, L0_ffn_w12, L0_ffn_b12, L0_ffn_w3, L0_ffn_b3, L1_attn_Wq, L1_attn_bq, L1_attn_Wk, L1_attn_bk, L1_attn_Wv, L1_attn_bv, L1_attn_Wo, L1_attn_M, L1_attn_z, L1_ffn_w_gate, L1_ffn_w_up, L1_ffn_w_down):

    def _L0_attn_ref(hidden_states, Wq, bq, Wk, bk, Wv, bv, Wo, bo, gq, gk):
        import jax, jax.numpy as jnp
        import numpy as np
        Q_DIM = 512
        N_HEADS = 32
        HEAD_DIM = 128
        INNER = N_HEADS * HEAD_DIM
        EPS = 1e-06

        def rms_norm(x, w):
            xf = x.astype(jnp.float32)
            var = jnp.mean(xf * xf, axis=-1, keepdims=True)
            return (w.astype(jnp.float32) * xf * jax.lax.rsqrt(var + EPS)).astype(x.dtype)
        B, S, _ = hidden_states.shape
        q = hidden_states @ Wq + bq
        k = hidden_states @ Wk + bk
        v = hidden_states @ Wv + bv
        q = rms_norm(q, gq)
        k = rms_norm(k, gk)
        q = q.reshape(B, S, N_HEADS, HEAD_DIM).transpose(0, 2, 1, 3)
        k = k.reshape(B, S, N_HEADS, HEAD_DIM).transpose(0, 2, 1, 3)
        v = v.reshape(B, S, N_HEADS, HEAD_DIM).transpose(0, 2, 1, 3)
        scale = 1.0 / np.sqrt(HEAD_DIM)
        attn = jnp.einsum('bhqd,bhkd->bhqk', q.astype(jnp.float32), k.astype(jnp.float32)) * scale
        attn = jax.nn.softmax(attn, axis=-1)
        out = jnp.einsum('bhqk,bhkd->bhqd', attn, v.astype(jnp.float32))
        out = out.transpose(0, 2, 1, 3).reshape(B, S, INNER).astype(hidden_states.dtype)
        return out @ Wo + bo

    def _L0_ffn_ref(x, w12, b12, w3, b3):
        import jax, jax.numpy as jnp
        import numpy as np
        M = 512
        K = 512

        def _make_2to4_mask(key, shape):
            scores = jax.random.normal(key, shape)
            g = scores.reshape(shape[0], shape[1] // 4, 4)
            rank = jnp.argsort(jnp.argsort(-jnp.abs(g), axis=-1), axis=-1)
            return (rank < 2).reshape(shape).astype(jnp.float32)
        x12 = jnp.einsum('bsk,mk->bsm', x, w12) + b12
        x1, x2 = jnp.split(x12, 2, axis=-1)
        x4 = jax.nn.silu(x1) * x2
        return jnp.einsum('bsm,nm->bsn', x4, w3) + b3

    def _L1_attn_ref(hidden_states, Wq, bq, Wk, bk, Wv, bv, Wo, M, z):
        import jax, jax.numpy as jnp
        import numpy as np
        B, S, HID = (2, 512, 512)
        H, HKV, D = (32, 8, 128)
        G = H // HKV
        EPS = 1e-06

        def _reference_tuple_inner(hidden_states, Wq, bq, Wk, bk, Wv, bv, Wo, M, z):
            b, s, _ = hidden_states.shape
            q = (hidden_states @ Wq.T + bq).reshape(b, s, H, D)
            k = (hidden_states @ Wk.T + bk).reshape(b, s, HKV, D)
            v = (hidden_states @ Wv.T + bv).reshape(b, s, HKV, D)
            sig_q = jax.nn.elu(q) + 1.0
            sig_k = jax.nn.elu(k) + 1.0
            q_sel = sig_q[:, :, ::G, :]
            num = jnp.einsum('bshd,hde->bshe', q_sel, M)
            den = jnp.einsum('bshd,hd->bsh', q_sel, z)[..., None] + EPS
            retrieved = num / den
            out_heads = jnp.repeat(retrieved, G, axis=2)
            output = out_heads.reshape(b, s, H * D) @ Wo.T
            M_new = M + jnp.einsum('bshd,bshe->hde', sig_k, v)
            z_new = z + sig_k.sum(axis=(0, 1))
            return (output, M_new, z_new)
        return _reference_tuple_inner(hidden_states, Wq, bq, Wk, bk, Wv, bv, Wo, M, z)[0]

    def _L1_ffn_ref(x, w_gate, w_up, w_down):
        import jax, jax.numpy as jnp
        import numpy as np
        HIDDEN = 512
        INTER = 1376

        def _ternary_quantize(w):
            scale = jnp.mean(jnp.abs(w))
            return jnp.clip(jnp.round(w / scale), -1.0, 1.0) * scale
        xf = x.astype(jnp.float32) / 128.0
        gate = jnp.einsum('bsh,ih->bsi', xf, w_gate)
        up = jnp.einsum('bsh,ih->bsi', xf, w_up)
        inter = jax.nn.silu(gate) * up
        inter_q = jnp.trunc(jnp.clip(inter * 128.0, -128.0, 127.0)).astype(jnp.int8)
        down = jnp.einsum('bsi,hi->bsh', inter_q.astype(jnp.float32), w_down)
        out = jnp.trunc(jnp.clip(down * 128.0, -128.0, 127.0)).astype(jnp.int8)
        return out
    x = L0_attn_hidden_states
    x = x + 0.5 * _L0_ffn_ref(_layernorm(x, axis=-1), L0_ffn_w12, L0_ffn_b12, L0_ffn_w3, L0_ffn_b3)
    x = x + _L0_attn_ref(_layernorm(x, axis=-1), L0_attn_Wq, L0_attn_bq, L0_attn_Wk, L0_attn_bk, L0_attn_Wv, L0_attn_bv, L0_attn_Wo, L0_attn_bo, L0_attn_gq, L0_attn_gk)
    x = x + 0.5 * _L0_ffn_ref(_layernorm(x, axis=-1), L0_ffn_w12, L0_ffn_b12, L0_ffn_w3, L0_ffn_b3)
    x = x + 0.5 * _L1_ffn_ref(_layernorm(x, axis=-1), L1_ffn_w_gate, L1_ffn_w_up, L1_ffn_w_down)
    x = x + _L1_attn_ref(_layernorm(x, axis=-1), L1_attn_Wq, L1_attn_bq, L1_attn_Wk, L1_attn_bk, L1_attn_Wv, L1_attn_bv, L1_attn_Wo, L1_attn_M, L1_attn_z)
    x = x + 0.5 * _L1_ffn_ref(_layernorm(x, axis=-1), L1_ffn_w_gate, L1_ffn_w_up, L1_ffn_w_down)
    return x

_drawn_inputs = setup_inputs


def setup_inputs(seed=0):
    import zlib

    import numpy as np

    out = dict(_drawn_inputs(seed))
    spreads = {'L0_attn_bq': (0.0, 0.424),
     'L0_attn_bk': (0.0, 0.8),
     'L0_attn_bv': (0.0, 0.1),
     'L0_attn_bo': (0.0, 0.1),
     'L0_attn_gq': (1.0, 0.584),
     'L0_attn_gk': (1.0, 0.582),
     'L1_attn_bq': (0.0, 2.0),
     'L1_attn_bk': (0.0, 0.1),
     'L1_attn_bv': (0.0, 0.1)}
    factors = {'L0_ffn_b12': 8.0,
     'L0_ffn_b3': 3.872,
     'L1_attn_Wq': 188.672,
     'L1_attn_Wo': 64.0,
     'L1_attn_M': 64.0,
     'L1_attn_z': 200.0}
    for name, (base, spread) in spreads.items():
        noise = np.random.default_rng([zlib.crc32(name.encode()), seed]).standard_normal(out[name].shape)
        drawn = base * np.exp(spread * noise) if base else spread * noise
        out[name] = jnp.asarray(drawn.astype(out[name].dtype))
    for name, factor in factors.items():
        out[name] = (out[name] * factor).astype(out[name].dtype)
    return out
```

```python
from contextlib import ExitStack

import concourse.bass as bass
from concourse import mybir

F32 = mybir.dt.float32
F32R = mybir.dt.float32r
ALU = mybir.AluOpType
ACT = mybir.ActivationFunctionType
AX = mybir.AxisListType

P = 128
TOK = 1024
DM = 512
NT = TOK // P
KB = DM // P
HALF = 512
NH = TOK // HALF
LN_EPS = 1e-5
RMS_EPS = 1e-6

HEADS = 32
HD = 128
INNER = HEADS * HD
GROUP = HALF // HD
NGROUPS = HEADS // GROUP

M0 = 512
MB0 = M0 // P

INTER = 1376
IB = (INTER + P - 1) // P
QSCALE = 128.0
ROUND = float(2 ** 23)

KVH = 8
REP = HEADS // KVH
MZ = HD + 2
RET_EPS = 1e-6


def wait(eng, sem, value):
    if isinstance(value, int) and value <= 0:
        return
    eng.wait_ge(sem, value)


class Core:

    def __init__(self, nc, ctx):
        self.nc = nc
        self.sems = []
        self.cols_in = ctx.enter_context(nc.semaphore("cols_in"))
        self.x = ctx.enter_context(nc.sbuf_tensor("x", [P, NT, DM], F32))
        self.ident = ctx.enter_context(nc.sbuf_tensor("ident", [P, P], F32))
        self.ones = ctx.enter_context(nc.sbuf_tensor("ones", [P, P], F32))
        self.ps = [ctx.enter_context(nc.psum_tensor(f"ps{i}", [P, 2 * HALF], F32)) for i in range(4)]

    def open_attention(self, ctx):
        nc = self.nc
        self.rms = ctx.enter_context(nc.sbuf_tensor("rms", [P, TOK + NT], F32))
        self.cols = {n: ctx.enter_context(nc.sbuf_tensor(f"col_{n}", [P, HEADS], F32))
                     for n in ("bq", "bk", "bv", "gq", "gk")}

    def semaphore(self, ctx, name):
        s = ctx.enter_context(self.nc.semaphore(name))
        self.sems.append(s)
        return s

    def open_block(self, ctx):
        nc, ctx_sems, self.sems = self.nc, self.sems, []

        def clear():
            nums = sorted(s.num for s in ctx_sems)
            starts = [n for n in nums if n - 1 not in nums]
            ends = [n + 1 for n in nums if n + 1 not in nums]
            with nc.Block() as block:
                @block.gpsimd
                def _(pool):
                    for a, b in zip(starts, ends):
                        nc.gpsimd.sem_clear(range(a, b))

        ctx.callback(clear)
        return ctx.enter_context(nc.Block())

    def bank(self, b):
        return self.ps[b // 2][:, (b % 2) * HALF:(b % 2 + 1) * HALF]


class LayerNorm:

    def __init__(self, core, ctx, tag):
        nc = core.nc
        self.core, self.nc = core, nc

        def sb(name, shape, dt=F32):
            return ctx.enter_context(nc.sbuf_tensor(f"{tag}_ln_{name}", shape, dt))

        def sem(name):
            return core.semaphore(ctx, f"{tag}_ln_{name}")

        self.stats = sb("stats", [P, NT, 6])
        self.meanvar = sb("meanvar", [P, NT, 2])
        self.var = sb("var", [P, NT])
        self.sd = sb("sd", [P, NT])
        self.r0 = sb("r0", [P, NT])
        self.corr = sb("corr", [P, NT])
        self.rstd = sb("rstd", [P, NT])
        self.xn = sb("xn", [P, 2, DM])
        self.hi = sb("xT_hi", [P, KB, TOK], F32R)
        self.lo = sb("xT_lo", [P, KB, TOK], F32R)
        self.s_stats, self.s_aggr, self.s_small = sem("stats_done"), sem("aggr_done"), sem("small_done")
        self.s_sd, self.s_xn, self.s_T = sem("sd_done"), sem("xn_done"), sem("transposed")
        self.s_hi, self.s_lo = sem("hi_done"), sem("lo_done")

    def statistics(self, v):
        nc = self.nc
        for t in range(NT):
            nc.vector.bn_stats(out=self.stats[:, t, :], in_=self.core.x[:, t, :]).then_inc(self.s_stats, 1)
        for t in range(NT):
            v.wait_ge(self.s_stats, t + 1)
            nc.vector.bn_aggr(out=self.meanvar[:, t, :], in_=self.stats[:, t, :]).then_inc(self.s_aggr, 1)
        v.wait_ge(self.s_aggr, NT)
        nc.vector.tensor_scalar_add(self.var[:], self.meanvar[:, :, 1], LN_EPS).then_inc(self.s_small, 1)

    def normalise(self, v):
        nc = self.nc
        v.wait_ge(self.s_sd, 1)
        nc.vector.reciprocal(self.r0[:], self.sd[:]).then_inc(self.s_small, 1)
        v.wait_ge(self.s_small, 2)
        nc.vector.tensor_tensor(self.corr[:], self.var[:], self.r0[:], ALU.mult).then_inc(self.s_small, 1)
        v.wait_ge(self.s_small, 3)
        nc.vector.tensor_tensor(self.corr[:], self.corr[:], self.r0[:], ALU.mult).then_inc(self.s_small, 1)
        v.wait_ge(self.s_small, 4)
        nc.vector.tensor_scalar(self.corr[:], self.corr[:], -0.5, 1.5, ALU.mult, ALU.add).then_inc(self.s_small, 1)
        v.wait_ge(self.s_small, 5)
        nc.vector.tensor_tensor(self.rstd[:], self.r0[:], self.corr[:], ALU.mult).then_inc(self.s_small, 1)
        v.wait_ge(self.s_small, 6)
        for t in range(NT):
            if t >= 2:
                v.wait_ge(self.s_T, t - 1)
            nc.vector.tensor_scalar(self.xn[:, t % 2, :], self.core.x[:, t, :], self.meanvar[:, t, 0:1],
                                    self.rstd[:, t:t + 1], ALU.subtract, ALU.mult).then_inc(self.s_xn, 1)
            if t >= 1:
                self._lo(v, t - 1)
        self._lo(v, NT - 1)

    def _psum(self, t):
        return self.core.bank(6 + t % 2).rearrange("p (k n) -> p k n", k=KB)

    def _lo(self, v, t):
        v.wait_ge(self.s_hi, t + 1)
        self.nc.vector.tensor_tensor(self.lo[:, :, t * P:(t + 1) * P], self._psum(t),
                                     self.hi[:, :, t * P:(t + 1) * P], ALU.subtract).then_inc(self.s_lo, 1)

    def sqrt(self, act):
        act.wait_ge(self.s_small, 1)
        self.nc.scalar.activation(self.sd[:], self.var[:], ACT.Sqrt).then_inc(self.s_sd, 1)

    def hi_parts(self, act):
        for t in range(NT):
            act.wait_ge(self.s_T, t + 1)
            self.nc.scalar.activation(self.hi[:, :, t * P:(t + 1) * P], self._psum(t), ACT.Copy)\
                .then_inc(self.s_hi, 1)

    def transposes(self, pe):
        for t in range(NT):
            pe.wait_ge(self.s_xn, t + 1)
            if t >= 2:
                pe.wait_ge(self.s_lo, t - 1)
            for k in range(KB):
                last = self.nc.tensor.transpose(self._psum(t)[:, k, :],
                                                self.xn[:, t % 2, k * P:(k + 1) * P], self.core.ident[:])
            last.then_inc(self.s_T, 1)

    def ready(self, pe, half):
        pe.wait_ge(self.s_lo, (half + 1) * NT // NH)


def product(nc, out, pairs):
    terms = []
    for (sh, sl), (mh, ml) in pairs:
        terms.append((sh, mh))
        if ml is not None:
            terms.append((sh, ml))
        if sl is not None:
            terms.append((sl, mh))
    for n, (s, m) in enumerate(terms):
        last = nc.tensor.matmul(out, s, m, start=(n == 0), stop=(n == len(terms) - 1))
    return last


def setup_block(core, ins):
    nc = core.nc
    with ExitStack() as ctx:
        loaded = core.semaphore(ctx, "setup_loaded")
        made = core.semaphore(ctx, "setup_made")
        block = core.open_block(ctx)

        @block.sync
        def _(sp):
            sp.dma_start(core.x[:], ins["x"].rearrange("(t p) d -> p t d", p=P)).then_inc(loaded, 16)
            sp.wait_ge(loaded, 16)

        @block.gpsimd
        def _(pool):
            nc.gpsimd.memset(core.ones[:], 1.0)
            nc.gpsimd.memset(core.ident[:], 0.0).then_inc(made, 1)
            pool.wait_ge(made, 1)
            nc.gpsimd.affine_select(out=core.ident[:], in_=core.ident[:], compare_op=ALU.not_equal, fill=1.0,
                                    base=0, pattern=[[-1, P]], channel_multiplier=1)


def ffn0_block(core, ins, tag):
    nc = core.nc
    x = core.x
    with ExitStack() as ctx:
        def sb(name, shape, dt=F32):
            return ctx.enter_context(nc.sbuf_tensor(f"{tag}_{name}", shape, dt))

        def sem(name):
            return core.semaphore(ctx, f"{tag}_{name}")

        ln = LayerNorm(core, ctx, tag)
        w12 = sb("w12", [P, KB, 2 * M0])
        w12_hi, w12_lo = sb("w12_hi", [P, KB, 2 * M0], F32R), sb("w12_lo", [P, KB, 2 * M0], F32R)
        w3 = sb("w3", [P, MB0, DM])
        w3_hi, w3_lo = sb("w3_hi", [P, MB0, DM], F32R), sb("w3_lo", [P, MB0, DM], F32R)
        b12 = sb("b12", [P, 2 * MB0])
        b3 = sb("b3", [P, DM])
        sig = sb("sig", [P, 2, HALF])
        gated = sb("gated", [P, 2, HALF])
        h = sb("h", [P, 2, HALF])
        h_hi, h_lo = sb("h_hi", [P, MB0, TOK], F32R), sb("h_lo", [P, MB0, TOK], F32R)
        w12_in = [sem(f"w12_in{k}") for k in range(KB)]
        w3_in, bias_in, b3_in = sem("w3_in"), sem("bias_in"), sem("b3_in")
        w12_hi_done, w12_lo_done = sem("w12_hi_done"), sem("w12_lo_done")
        w3_hi_done, w3_lo_done = sem("w3_hi_done"), sem("w3_lo_done")
        up_done, sig_done, gated_done, h_done = sem("up_done"), sem("sig_done"), sem("gated_done"), sem("h_done")
        h_hi_done, h_lo_done = sem("h_hi_done"), sem("h_lo_done")
        biased, down_done, added = sem("biased"), sem("down_done"), sem("added")
        block = core.open_block(ctx)
        units = [(th, mb) for th in range(NH) for mb in range(MB0)]

        def tok(th):
            return slice(th * HALF, (th + 1) * HALF)

        @block.sync
        def _(sp):
            for k in range(KB):
                sp.dma_start(w12[:, k, :], ins["w12T"][:, k, :]).then_inc(w12_in[k], 16)
            sp.dma_start(b12[:], ins["b12T"]).then_inc(bias_in, 16)
            sp.dma_start(w3[:], ins["w3T"]).then_inc(w3_in, 16)
            sp.dma_start(b3[:], ins["b3"].partition_broadcast(P)).then_inc(b3_in, 16)

        @block.gpsimd
        def _(pool):
            pool.wait_ge(w3_in, 16)
            pool.wait_ge(w3_hi_done, 1)
            nc.gpsimd.tensor_tensor(w3_lo[:], w3[:], w3_hi[:], ALU.subtract).then_inc(w3_lo_done, 1)
            pool.wait_ge(b3_in, 16)
            nc.gpsimd.tensor_scalar(b3[:], b3[:], 0.5, None, ALU.mult).then_inc(biased, 1)
            pool.wait_ge(biased, 1)
            for t in range(NT):
                pool.wait_ge(ln.s_xn, t + 1)
                nc.gpsimd.tensor_tensor(x[:, t, :], x[:, t, :], b3[:], ALU.add).then_inc(biased, 1)

        @block.vector
        def _(v):
            ln.statistics(v)
            ln.normalise(v)
            for k in range(KB):
                v.wait_ge(w12_hi_done, k + 1)
                nc.vector.tensor_tensor(w12_lo[:, k, :], w12[:, k, :], w12_hi[:, k, :], ALU.subtract)\
                    .then_inc(w12_lo_done, 1)
            v.wait_ge(bias_in, 16)
            for u, (th, mb) in enumerate(units):
                x1, x2 = core.bank(2 * (u % 2)), core.bank(2 * (u % 2) + 1)
                v.wait_ge(sig_done, u + 1)
                nc.vector.scalar_tensor_tensor(out=gated[:, u % 2, :], in0=x1, scalar=b12[:, mb:mb + 1],
                                               in1=sig[:, u % 2, :], op0=ALU.add, op1=ALU.mult)\
                    .then_inc(gated_done, 1)
                v.wait_ge(gated_done, u + 1)
                wait(v, h_lo_done, u - 1)
                nc.vector.scalar_tensor_tensor(out=h[:, u % 2, :], in0=x2, scalar=b12[:, MB0 + mb:MB0 + mb + 1],
                                               in1=gated[:, u % 2, :], op0=ALU.add, op1=ALU.mult)\
                    .then_inc(h_done, 1)
            for t in range(NT):
                v.wait_ge(down_done, t + 1)
                v.wait_ge(biased, t + 2)
                nc.vector.scalar_tensor_tensor(out=x[:, t, :], in0=core.bank(4 + t % 2), scalar=0.5,
                                               in1=x[:, t, :], op0=ALU.mult, op1=ALU.add).then_inc(added, 1)

        @block.scalar
        def _(act):
            ln.sqrt(act)
            for k in range(KB):
                act.wait_ge(w12_in[k], 16)
                nc.scalar.activation(w12_hi[:, k, :], w12[:, k, :], ACT.Copy).then_inc(w12_hi_done, 1)
            ln.hi_parts(act)
            act.wait_ge(w3_in, 16)
            nc.scalar.activation(w3_hi[:], w3[:], ACT.Copy).then_inc(w3_hi_done, 1)
            act.wait_ge(bias_in, 16)

            def split(u):
                th, mb = units[u]
                act.wait_ge(h_done, u + 1)
                nc.scalar.activation(h_hi[:, mb, tok(th)], h[:, u % 2, :], ACT.Copy).then_inc(h_hi_done, 1)

            for u, (th, mb) in enumerate(units):
                act.wait_ge(up_done, u + 1)
                wait(act, gated_done, u - 1)
                nc.scalar.activation(sig[:, u % 2, :], core.bank(2 * (u % 2)), ACT.Sigmoid,
                                     bias=b12[:, mb:mb + 1]).then_inc(sig_done, 1)
                if u >= 1:
                    split(u - 1)
            split(len(units) - 1)

        @block.gpsimd
        def _(pool):
            for u, (th, mb) in enumerate(units):
                pool.wait_ge(h_hi_done, u + 1)
                nc.gpsimd.tensor_tensor(h_lo[:, mb, tok(th)], h[:, u % 2, :], h_hi[:, mb, tok(th)], ALU.subtract)\
                    .then_inc(h_lo_done, 1)

        @block.tensor
        def _(pe):
            ln.transposes(pe)
            pe.wait_ge(w12_lo_done, KB)
            for u, (th, mb) in enumerate(units):
                ln.ready(pe, th)
                wait(pe, h_done, u - 1)
                for part in range(2):
                    c = (part * MB0 + mb) * P
                    last = product(nc, core.bank(2 * (u % 2) + part), [
                        ((w12_hi[:, k, c:c + P], w12_lo[:, k, c:c + P]),
                         (ln.hi[:, k, tok(th)], ln.lo[:, k, tok(th)])) for k in range(KB)])
                last.then_inc(up_done, 1)
            pe.wait_ge(w3_lo_done, 1)
            for t in range(NT):
                pe.wait_ge(h_lo_done, MB0 * (1 + t * P // HALF))
                wait(pe, added, t - 1)
                s = slice(t * P, (t + 1) * P)
                product(nc, core.bank(4 + t % 2), [
                    ((h_hi[:, m, s], h_lo[:, m, s]), (w3_hi[:, m, :], w3_lo[:, m, :])) for m in range(MB0)])\
                    .then_inc(down_done, 1)


def qkv_block(core, ins, scratch):
    nc = core.nc
    with ExitStack() as ctx:
        def sb(name, shape, dt=F32):
            return ctx.enter_context(nc.sbuf_tensor(f"qkv_{name}", shape, dt))

        def sem(name):
            return core.semaphore(ctx, f"qkv_{name}")

        Q, K, V = range(3)
        UNITS = 8
        ln = LayerNorm(core, ctx, "qkv")
        w = [sb(f"w{t}", [P, KB, HALF]) for t in range(3)]
        w_hi = [sb(f"w{t}_hi", [P, KB, HALF], F32R) for t in range(3)]
        w_lo = [sb(f"w{t}_lo", [P, KB, HALF], F32R) for t in range(3)]
        res = [sb(f"res{i}", [P, HALF]) for i in range(4)]
        sq = sb("sq", [P, 2, HALF])
        acc = [sb(f"acc{t}", [P, TOK]) for t in (Q, K)]
        ms = sb("ms", [P, TOK + NT])
        sd = sb("sd", [P, TOK + NT])
        r0 = sb("r0", [P, TOK + NT])
        w_in = [sem(f"w_in{t}") for t in range(3)]
        w_hi_done, w_lo_done, proj_done, res_done = (sem(n) for n in
                                                     ("w_hi_done", "w_lo_done", "proj_done", "res_done"))
        stored = [sem(f"stored{i}") for i in range(4)]
        sq_done, acc_done, sums_done, ms_done, sd_done, rms_done = (
            sem(n) for n in ("sq_done", "acc_done", "sums_done", "ms_done", "sd_done", "rms_done"))
        block = core.open_block(ctx)
        weights = [ins["Wq"], ins["Wk"], ins["Wv"]]
        bias = [core.cols["bq"], core.cols["bk"]]

        def groups(eng, body):
            body(0)
            with eng.Fori(1, NGROUPS - 1) as g:
                body(g)
            body(NGROUPS - 1)

        def is_last(g):
            return isinstance(g, int) and g == NGROUPS - 1

        @block.sync
        def _(sp):
            def load(g, t):
                wait(sp, w_hi_done, (g - 1) * 3 + t + 1)
                wait(sp, w_lo_done, (g - 1) * 3 + t + 1)
                sp.dma_start(w[t][:], weights[t][bass.ds(g, 1)].rearrange("a p k n -> p (a k) n"))\
                    .then_inc(w_in[t], 16)

            load(0, Q)
            for n in core.cols:
                sp.dma_start(core.cols[n][:], ins[n]).then_inc(core.cols_in, 16)
            load(0, K)

            def body(g):
                for t in (Q, K, V):
                    if t == Q:
                        load(g, V)
                    elif not is_last(g):
                        load(g + 1, t - 1)
                    for u in range(UNITS):
                        sp.wait_ge(res_done, g * 24 + t * UNITS + u + 1)
                        if t == V:
                            dst = scratch["v"][bass.ds(g * GROUP, GROUP), :, u, :].rearrange("h p d -> p h d")
                            src = res[u % 4][:].rearrange("p (h d) -> p h d", h=GROUP)
                        else:
                            dst = scratch["qk"[t]][bass.ds(g * GROUP + u // 2, 1), :,
                                                   (u % 2) * HALF:(u % 2 + 1) * HALF]\
                                .rearrange("a p n -> p (a n)")
                            src = res[u % 4][:]
                        sp.dma_start(dst, src).then_inc(stored[u % 4], 16)

            groups(sp, body)
            for i in range(4):
                sp.wait_ge(stored[i], NGROUPS * 6 * 16)

        @block.scalar
        def _(act):
            def split(n, t, g):
                act.wait_ge(w_in[t], (g + 1) * 16)
                wait(act, proj_done, (n - 2) * UNITS)
                nc.scalar.activation(w_hi[t][:], w[t][:], ACT.Copy).then_inc(w_hi_done, 1)

            ln.sqrt(act)
            split(0, Q, 0)
            ln.hi_parts(act)

            def body(g):
                for t in (Q, K, V):
                    n = g * 3 + t
                    if t < V:
                        split(n + 1, t + 1, g)
                    elif not is_last(g):
                        split(n + 1, Q, g + 1)
                    for u in range(UNITS):
                        if t == V:
                            continue
                        m = g * 16 + t * UNITS + u
                        act.wait_ge(res_done, n * UNITS + u + 1)
                        wait(act, acc_done, m + 2 - 1)
                        nc.scalar.activation(sq[:, u % 2, :], res[u % 4][:], ACT.Square).then_inc(sq_done, 1)

            groups(act, body)
            act.wait_ge(ms_done, 2)
            nc.scalar.activation(sd[:], ms[:], ACT.Sqrt).then_inc(sd_done, 1)

        @block.vector
        def _(v):
            def split(n, t):
                v.wait_ge(w_hi_done, n + 1)
                nc.vector.tensor_tensor(w_lo[t][:], w[t][:], w_hi[t][:], ALU.subtract).then_inc(w_lo_done, 1)

            ln.statistics(v)
            split(0, Q)
            ln.normalise(v)
            v.wait_ge(core.cols_in, 16 * len(core.cols))

            def body(g):
                for t in (Q, K, V):
                    n = g * 3 + t
                    if t < V or not is_last(g):
                        split(n + 1, (t + 1) % 3)
                    for u in range(UNITS):
                        v.wait_ge(proj_done, n * UNITS + u + 1)
                        wait(v, stored[u % 4], (g * 6 + t * 2 + u // 4) * 16)
                        wait(v, sq_done, g * 16 + max(min(t * UNITS + u - 3, 16), 0))
                        if t == V:
                            nc.vector.tensor_copy(res[u % 4][:], core.bank(u % 4)).then_inc(res_done, 1)
                        else:
                            nc.vector.tensor_scalar(res[u % 4][:], core.bank(u % 4),
                                                    bias[t][:, bass.ds(g * GROUP + u // 2, 1)], None, ALU.add)\
                                .then_inc(res_done, 1)

            groups(v, body)
            v.wait_ge(sums_done, 1)
            nc.vector.tensor_scalar(ms[:, 0:TOK], core.ps[2][:], 1.0 / INNER, RMS_EPS, ALU.mult, ALU.add)\
                .then_inc(ms_done, 1)
            nc.vector.tensor_scalar(ms[:, TOK:TOK + NT], core.bank(6)[:, 0:NT], 1.0 / INNER, RMS_EPS,
                                    ALU.mult, ALU.add).then_inc(ms_done, 1)
            v.wait_ge(sd_done, 1)
            nc.vector.reciprocal(r0[:], sd[:]).then_inc(rms_done, 1)
            v.wait_ge(rms_done, 1)
            nc.vector.tensor_tensor(sd[:], ms[:], r0[:], ALU.mult).then_inc(rms_done, 1)
            v.wait_ge(rms_done, 2)
            nc.vector.tensor_tensor(sd[:], sd[:], r0[:], ALU.mult).then_inc(rms_done, 1)
            v.wait_ge(rms_done, 3)
            nc.vector.tensor_scalar(sd[:], sd[:], -0.5, 1.5, ALU.mult, ALU.add).then_inc(rms_done, 1)
            v.wait_ge(rms_done, 4)
            nc.vector.tensor_tensor(core.rms[:], r0[:], sd[:], ALU.mult).then_inc(rms_done, 1)
            v.wait_ge(rms_done, 5)
            nc.vector.tensor_scalar(core.rms[:, TOK:TOK + NT], core.rms[:, TOK:TOK + NT], float(HD) ** -0.5, None,
                                    ALU.mult)

        @block.gpsimd
        def _(pool):
            for t in (Q, K):
                nc.gpsimd.memset(acc[t][:], 0.0).then_inc(acc_done, 1)
            pool.wait_ge(acc_done, 2)

            def body(g):
                for t in (Q, K):
                    for u in range(UNITS):
                        m = g * 16 + t * UNITS + u
                        pool.wait_ge(sq_done, m + 1)
                        pool.wait_ge(acc_done, m + 2)
                        part = acc[t][:, (u % 2) * HALF:(u % 2 + 1) * HALF]
                        nc.gpsimd.tensor_tensor(part, part, sq[:, u % 2, :], ALU.add).then_inc(acc_done, 1)

            groups(pool, body)

        @block.tensor
        def _(pe):
            ln.transposes(pe)

            def sums():
                pe.wait_ge(acc_done, 2 + NGROUPS * 16)
                for th in range(NH):
                    nc.tensor.matmul(core.bank(4 + th), core.ones[:], acc[K][:, th * HALF:(th + 1) * HALF],
                                     start=True, stop=True)
                for t in range(NT):
                    last = nc.tensor.matmul(core.bank(6)[:, t:t + 1], acc[Q][:, t * P:(t + 1) * P],
                                            core.ones[:, 0:1], start=True, stop=True)
                last.then_inc(sums_done, 1)

            def body(g):
                for t in (Q, K, V):
                    n = g * 3 + t
                    pe.wait_ge(w_lo_done, n + 1)
                    for u in range(UNITS):
                        if isinstance(g, int) and g == 0 and t == Q and u == 0:
                            ln.ready(pe, NH - 1)
                        wait(pe, res_done, n * UNITS + u - 3)
                        if t == V:
                            s = slice(u * P, (u + 1) * P)
                            pairs = [((ln.hi[:, k, s], ln.lo[:, k, s]), (w_hi[t][:, k, :], w_lo[t][:, k, :]))
                                     for k in range(KB)]
                        else:
                            c = slice(u // 2 * HD, (u // 2 + 1) * HD)
                            s = slice((u % 2) * HALF, (u % 2 + 1) * HALF)
                            pairs = [((w_hi[t][:, k, c], w_lo[t][:, k, c]), (ln.hi[:, k, s], ln.lo[:, k, s]))
                                     for k in range(KB)]
                        product(nc, core.bank(u % 4), pairs).then_inc(proj_done, 1)
                        if is_last(g) and t == V and u == 3:
                            sums()

            groups(pe, body)


def attention_block(core, ins, scratch):
    nc = core.nc
    x = core.x
    T_LAG, PV_LAG, OUT_LAG, WO_LAG = 2, 6, 10, 11
    BODY = 2 * NT
    STEPS = HEADS * NT
    with ExitStack() as ctx:
        def sb(name, shape, dt=F32):
            return ctx.enter_context(nc.sbuf_tensor(f"at_{name}", shape, dt))

        def sem(name):
            return core.semaphore(ctx, f"at_{name}")

        def pair(name, shape):
            return [(sb(f"{name}{i}_hi", shape, F32R), sb(f"{name}{i}_lo", shape, F32R)) for i in range(2)]

        k_raw, q_raw, v_raw = sb("k_raw", [P, TOK]), sb("q_raw", [P, TOK]), sb("v_raw", [P, NT, HD])
        o_raw, bo = sb("o_raw", [P, DM]), sb("bo", [P, DM])
        kn = sb("kn", [P, TOK])
        k2, q2, v2 = pair("k", [P, TOK]), pair("q", [P, TOK]), pair("v", [P, NT, HD])
        o2 = pair("o", [P, DM])
        pT2 = pair("pT", [P, NT, HALF])
        y2 = pair("y", [P, HALF])
        y = sb("y", [P, HALF])
        probs = [sb(f"probs{i}", [P, TOK]) for i in range(4)]
        maxes, nbias, sums, rsums = (sb(n, [P, 4]) for n in ("maxes", "nbias", "sums", "rsums"))
        k_in, q_in, v_in, o_in, bo_in = (sem(f"{n}_in") for n in ("k", "q", "v", "o", "bo"))
        kn_done = sem("kn_done")
        k_hi, k_lo, q_hi, q_lo, v_hi, v_lo, o_hi, o_lo = (
            sem(f"{n}_done") for n in ("k_hi", "k_lo", "q_hi", "q_lo", "v_hi", "v_lo", "o_hi", "o_lo"))
        s_scores, s_max, s_bias, s_exp, s_rsum, s_norm = (
            sem(n) for n in ("scores_done", "max_done", "bias_done", "exp_done", "rsum_done", "norm_done"))
        s_T, s_pT_hi, s_pT_lo = sem("transposed"), sem("pT_hi_done"), sem("pT_lo_done")
        s_pv, s_y, s_y_hi, s_y_lo = sem("pv_done"), sem("y_done"), sem("y_hi_done"), sem("y_lo_done")
        s_wo, s_added, s_bo = sem("wo_done"), sem("added"), sem("bo_added")
        block = core.open_block(ctx)
        rk, rq = core.rms[:, 0:TOK], core.rms[:, TOK:TOK + NT]
        gq, gk, bv = core.cols["gq"], core.cols["gk"], core.cols["bv"]
        T_BANKS, PV_BANK, WO_BANK = core.ps[2], 6, 7

        def scores(l):
            return core.ps[l % 2]

        def steps(eng, step, before_loop=None):
            for l in range(BODY):
                step(0, l)
            with eng.Fori(1, STEPS // BODY - 1) as i:
                for l in range(BODY):
                    step(i, l)
            for l in range(BODY):
                step(STEPS // BODY - 1, l)
            for l in range(WO_LAG):
                step(STEPS // BODY, l)

        def exists(i, l, lag=0):
            return not isinstance(i, int) or 0 <= BODY * i + l - lag < STEPS

        def lagging(i, l, lag):
            m = (l - lag) % BODY
            return (BODY // 4 * i + (l - lag) // 4), (m // 4) % 2, m // NT, m % 4

        def next_head(i, l):
            h = 2 * i + l // NT + 1
            return h, (l // NT + 1) % 2, not isinstance(h, int) or h < HEADS

        @block.sync
        def _(sp):
            def load(dst, src, h, arrived):
                sp.dma_start(dst, src[bass.ds(h, 1)].rearrange("a p n -> p (a n)")).then_inc(arrived, 16)

            def head(h):
                wait(sp, kn_done, h)
                load(k_raw[:], scratch["k"], h, k_in)
                wait(sp, q_lo, h)
                load(q_raw[:], scratch["q"], h, q_in)
                wait(sp, v_lo, h)
                wait(sp, v_hi, h)
                load(v_raw[:].rearrange("p t d -> p (t d)"), scratch["v_flat"], h, v_in)
                wait(sp, o_lo, h)
                wait(sp, o_hi, h)
                load(o_raw[:], ins["Wo"], h, o_in)

            sp.dma_start(bo[:], ins["bo"].partition_broadcast(P)).then_inc(bo_in, 16)
            head(0)
            with sp.Fori(1, HEADS) as h:
                head(h)

        @block.gpsimd
        def _(pool):
            def part_lo(dst, a, b, done, count, arrived):
                pool.wait_ge(arrived, count)
                nc.gpsimd.tensor_tensor(dst, a, b, ALU.subtract).then_inc(done, 1)

            def k_part(h, hp):
                part_lo(k2[hp][1][:], kn[:], k2[hp][0][:], k_lo, h + 1, k_hi)

            def v_part(h, hp):
                part_lo(v2[hp][1][:], v_raw[:], v2[hp][0][:], v_lo, h + 1, v_hi)

            k_part(0, 0)
            pool.wait_ge(bo_in, 16)
            for t in range(NT):
                nc.gpsimd.tensor_tensor(x[:, t, :], x[:, t, :], bo[:], ALU.add).then_inc(s_bo, 1)

            def step(i, l):
                p = BODY * i + l
                if exists(i, l):
                    pool.wait_ge(s_rsum, p + 1)
                    nc.gpsimd.tensor_tensor(probs[l % 4][:], probs[l % 4][:],
                                            rsums[:, l % 4:l % 4 + 1].broadcast_to([P, TOK]), ALU.mult)\
                        .then_inc(s_norm, 1)
                h, hp, there = next_head(i, l)
                if l % NT == 1 and there:
                    k_part(h, hp)
                if l % NT == 7 and there:
                    v_part(h, hp)
                if l == 0 and isinstance(i, int) and i == 0:
                    v_part(0, 0)
                if l % NT == 5 and exists(i, l):
                    hh, par = 2 * i + l // NT, l // NT
                    part_lo(o2[par][1][:], o_raw[:], o2[par][0][:], o_lo, hh + 1, o_hi)
                if l % 4 == OUT_LAG % 4 and exists(i, l, OUT_LAG):
                    J, jp, _, _ = lagging(i, l, OUT_LAG)
                    part_lo(y2[jp][1][:], y[:], y2[jp][0][:], s_y_lo, J + 1, s_y_hi)

            steps(pool, step)

        @block.scalar
        def _(act):
            nc.scalar.preload_act_table(ACT.Exp)

            def k_split(h, hp):
                act.wait_ge(kn_done, h + 1)
                wait(act, s_scores, (h - 1) * NT)
                nc.scalar.activation(k2[hp][0][:], kn[:], ACT.Copy).then_inc(k_hi, 1)

            def v_part(h, hp):
                act.wait_ge(v_in, (h + 1) * 16)
                wait(act, s_pv, 2 * h - 2)
                nc.scalar.activation(v2[hp][0][:], v_raw[:], ACT.Copy).then_inc(v_hi, 1)

            k_split(0, 0)

            def step(i, l):
                p = BODY * i + l
                if exists(i, l, T_LAG):
                    q = p - T_LAG
                    J, jp, _, w = lagging(i, l, T_LAG)
                    for b in range(2):
                        act.wait_ge(s_T, 2 * q + b + 1)
                        if w == 0 and b == 0:
                            wait(act, s_pv, J - 1)
                        nc.scalar.activation(
                            pT2[jp][0][:, 4 * b:4 * b + 4, w * P:(w + 1) * P],
                            T_BANKS[:, b * HALF:(b + 1) * HALF].rearrange("p (k n) -> p k n", k=4),
                            ACT.Copy).then_inc(s_pT_hi, 1)
                if exists(i, l):
                    act.wait_ge(s_bias, p + 1)
                    wait(act, s_T, 2 * (p - 4) + 2)
                    nc.scalar.activation(probs[l % 4][:], scores(l)[:], ACT.Exp, bias=nbias[:, l % 4:l % 4 + 1],
                                         scale=rq[:, l % NT:l % NT + 1], accum_out=sums[:, l % 4:l % 4 + 1])\
                        .then_inc(s_exp, 1)
                if l % 4 == OUT_LAG % 4 and exists(i, l, OUT_LAG):
                    J, jp, _, _ = lagging(i, l, OUT_LAG)
                    act.wait_ge(s_y, J + 1)
                    wait(act, s_wo, 4 * (J - 1))
                    nc.scalar.activation(y2[jp][0][:], y[:], ACT.Copy).then_inc(s_y_hi, 1)
                h, hp, there = next_head(i, l)
                if l % NT == 1 and there:
                    k_split(h, hp)
                if l % NT == 7 and there:
                    v_part(h, hp)
                if l == 0 and isinstance(i, int) and i == 0:
                    v_part(0, 0)
                if l % NT == 5 and exists(i, l):
                    hh, par = 2 * i + l // NT, l // NT
                    act.wait_ge(o_in, (hh + 1) * 16)
                    wait(act, s_wo, (hh - 1) * NT)
                    nc.scalar.activation(o2[par][0][:], o_raw[:], ACT.Copy).then_inc(o_hi, 1)

            steps(act, step)

        @block.vector
        def _(v):
            def k_part(h):
                v.wait_ge(k_in, (h + 1) * 16)
                wait(v, k_lo, h)
                nc.vector.scalar_tensor_tensor(out=kn[:], in0=k_raw[:], scalar=gk[:, bass.ds(h, 1)], in1=rk,
                                               op0=ALU.mult, op1=ALU.mult).then_inc(kn_done, 1)

            def q_part(h, hp):
                v.wait_ge(q_in, (h + 1) * 16)
                wait(v, s_scores, (h - 1) * NT)
                nc.vector.tensor_scalar(q2[hp][0][:], q_raw[:], gq[:, bass.ds(h, 1)], None, ALU.mult)\
                    .then_inc(q_hi, 1)
                v.wait_ge(q_hi, h + 1)
                nc.vector.scalar_tensor_tensor(out=q2[hp][1][:], in0=q_raw[:], scalar=gq[:, bass.ds(h, 1)],
                                               in1=q2[hp][0][:], op0=ALU.mult, op1=ALU.subtract).then_inc(q_lo, 1)

            k_part(0)
            q_part(0, 0)

            def step(i, l):
                p = BODY * i + l
                if exists(i, l):
                    v.wait_ge(s_scores, p + 1)
                    nc.vector.reduce_max(maxes[:, l % 4:l % 4 + 1], scores(l)[:], AX.X).then_inc(s_max, 1)
                    v.wait_ge(s_max, p + 1)
                    nc.vector.tensor_scalar(nbias[:, l % 4:l % 4 + 1], maxes[:, l % 4:l % 4 + 1],
                                            rq[:, l % NT:l % NT + 1], -1.0, ALU.mult, ALU.mult).then_inc(s_bias, 1)
                if exists(i, l, T_LAG):
                    q = p - T_LAG
                    _, jp, _, w = lagging(i, l, T_LAG)
                    for b in range(2):
                        v.wait_ge(s_pT_hi, 2 * q + b + 1)
                        out = (slice(None), slice(4 * b, 4 * b + 4), slice(w * P, (w + 1) * P))
                        nc.vector.tensor_tensor(
                            pT2[jp][1][out], T_BANKS[:, b * HALF:(b + 1) * HALF].rearrange("p (k n) -> p k n", k=4),
                            pT2[jp][0][out], ALU.subtract).then_inc(s_pT_lo, 1)
                if exists(i, l):
                    v.wait_ge(s_exp, p + 1)
                    nc.vector.reciprocal(rsums[:, l % 4:l % 4 + 1], sums[:, l % 4:l % 4 + 1]).then_inc(s_rsum, 1)
                if l % 4 == OUT_LAG % 4 and exists(i, l, OUT_LAG):
                    J, _, _, _ = lagging(i, l, OUT_LAG)
                    head = 2 * i + (l - OUT_LAG) // NT
                    v.wait_ge(s_pv, J + 1)
                    wait(v, s_y_lo, J)
                    nc.vector.tensor_scalar(y[:], core.bank(PV_BANK), bv[:, bass.ds(head, 1)], None, ALU.add)\
                        .then_inc(s_y, 1)
                if exists(i, l, WO_LAG):
                    _, jp, _, w = lagging(i, l, WO_LAG)
                    tile = jp * 4 + w
                    v.wait_ge(s_wo, p - WO_LAG + 1)
                    if isinstance(i, int) and i == 0:
                        v.wait_ge(s_bo, NT)
                    wait(v, s_added, p - WO_LAG)
                    nc.vector.tensor_tensor(x[:, tile, :], core.bank(WO_BANK), x[:, tile, :], ALU.add)\
                        .then_inc(s_added, 1)
                h, hp, there = next_head(i, l)
                if l % NT == 0 and there:
                    k_part(h)
                if l % NT == 2 and there:
                    q_part(h, hp)

            steps(v, step)

        @block.tensor
        def _(pe):
            def step(i, l):
                p = BODY * i + l
                if exists(i, l):
                    qt, hp = l % NT, l // NT
                    if qt == 0:
                        for s in (k_hi, k_lo, q_hi, q_lo):
                            pe.wait_ge(s, 2 * i + hp + 1)
                    wait(pe, s_exp, p - 1)
                    s = slice(qt * P, (qt + 1) * P)
                    for n in range(NH):
                        m = slice(n * HALF, (n + 1) * HALF)
                        last = product(nc, scores(l)[:, m], [((q2[hp][0][:, s], q2[hp][1][:, s]),
                                                              (k2[hp][0][:, m], k2[hp][1][:, m]))])
                    last.then_inc(s_scores, 1)
                if exists(i, l, T_LAG):
                    q = p - T_LAG
                    pe.wait_ge(s_norm, q + 1)
                    for b in range(2):
                        wait(pe, s_pT_lo, 2 * (q - 1) + b + 1)
                        for k in range(4 * b, 4 * b + 4):
                            last = nc.tensor.transpose(T_BANKS[:, k * P:(k + 1) * P],
                                                       probs[(l - T_LAG) % 4][:, k * P:(k + 1) * P], core.ident[:])
                        last.then_inc(s_T, 1)
                if exists(i, l, WO_LAG):
                    J, jp, hp, w = lagging(i, l, WO_LAG)
                    if w == 0:
                        pe.wait_ge(s_y_lo, J + 1)
                        if jp == 0:
                            pe.wait_ge(o_lo, 2 * i + (l - WO_LAG) // NT + 1)
                    wait(pe, s_added, p - WO_LAG)
                    s = slice(w * P, (w + 1) * P)
                    product(nc, core.bank(WO_BANK), [((y2[jp][0][:, s], y2[jp][1][:, s]),
                                                      (o2[hp][0][:], o2[hp][1][:]))]).then_inc(s_wo, 1)
                if exists(i, l, PV_LAG):
                    J, jp, hp, c = lagging(i, l, PV_LAG)
                    if c == 0:
                        pe.wait_ge(s_pT_lo, 8 * J + 8)
                        wait(pe, s_y, J)
                        if jp == 0:
                            pe.wait_ge(v_lo, 2 * i + (l - PV_LAG) // NT + 1)
                    terms = []
                    for k in (2 * c, 2 * c + 1):
                        (vh, vl), (ph, pl) = v2[hp], pT2[jp]
                        terms += [(vh, ph, k), (vh, pl, k), (vl, ph, k)]
                    for n, (a, b, k) in enumerate(terms):
                        last = nc.tensor.matmul(core.bank(PV_BANK), a[:, k, :], b[:, k, :], start=(c == 0 and n == 0),
                                                stop=(c == 3 and n == len(terms) - 1))
                    if c == 3:
                        last.then_inc(s_pv, 1)

            steps(pe, step)


class Truncation:

    def __init__(self, core, ctx, tag):
        self.nc = nc = core.nc

        def sb(name):
            return ctx.enter_context(nc.sbuf_tensor(f"{tag}_{name}", [P, 2, HALF], F32))

        def sem(name):
            return core.semaphore(ctx, f"{tag}_{name}")

        self.clipped, self.mag, self.sign, self.near, self.over = (
            sb(n) for n in ("clipped", "magnitude", "sign", "nearest", "over"))
        self.s_clip, self.s_mag, self.s_near, self.s_over, self.s_floor, self.s_out = (
            sem(n) for n in ("clip_done", "magnitude_done", "nearest_done", "over_done", "floor_done", "trunc_done"))

    def clip(self, v, n):
        s = n % 2
        self.nc.vector.tensor_scalar(self.clipped[:, s, :], self.clipped[:, s, :], -QSCALE, QSCALE - 1,
                                     ALU.max, ALU.min).then_inc(self.s_clip, 1)

    def magnitude(self, act, n):
        s = n % 2
        act.wait_ge(self.s_clip, n + 1)
        wait(act, self.s_out, n - 1)
        self.nc.scalar.activation(self.mag[:, s, :], self.clipped[:, s, :], ACT.Abs)
        self.nc.scalar.activation(self.sign[:, s, :], self.clipped[:, s, :], ACT.Sign).then_inc(self.s_mag, 1)

    def floor(self, v, n):
        s = n % 2
        v.wait_ge(self.s_mag, n + 1)
        wait(v, self.s_out, n - 1)
        self.nc.vector.tensor_scalar(self.near[:, s, :], self.mag[:, s, :], ROUND, ROUND, ALU.add, ALU.subtract)\
            .then_inc(self.s_near, 1)
        v.wait_ge(self.s_near, n + 1)
        self.nc.vector.tensor_tensor(self.over[:, s, :], self.near[:, s, :], self.mag[:, s, :], ALU.is_gt)\
            .then_inc(self.s_over, 1)
        v.wait_ge(self.s_over, n + 1)
        self.nc.vector.tensor_tensor(self.near[:, s, :], self.near[:, s, :], self.over[:, s, :], ALU.subtract)\
            .then_inc(self.s_floor, 1)

    def signed(self, pool, n, out):
        s = n % 2
        pool.wait_ge(self.s_floor, n + 1)
        self.nc.gpsimd.tensor_tensor(out, self.near[:, s, :], self.sign[:, s, :], ALU.mult).then_inc(self.s_out, 1)


def ffn1_block(core, ins, tag, out=None):
    nc = core.nc
    x = core.x
    with ExitStack() as ctx:
        def sb(name, shape, dt=F32):
            return ctx.enter_context(nc.sbuf_tensor(f"{tag}_{name}", shape, dt))

        def sem(name):
            return core.semaphore(ctx, f"{tag}_{name}")

        ln = LayerNorm(core, ctx, tag)
        tr = Truncation(core, ctx, tag)
        w = [sb(f"w{i}", [P, 2, KB, P]) for i in range(2)]
        w_hi = [sb(f"w{i}_hi", [P, 2, KB, P], F32R) for i in range(2)]
        w_lo = [sb(f"w{i}_lo", [P, 2, KB, P], F32R) for i in range(2)]
        wd = [sb(f"wd{i}", [P, DM]) for i in range(2)]
        wd_hi, wd_lo = sb("wd_hi", [P, IB, DM], F32R), sb("wd_lo", [P, IB, DM], F32R)
        sig = sb("sig", [P, 2, HALF])
        silu = sb("silu", [P, 2, HALF])
        inter = sb("inter", [P, IB, TOK], F32R)
        q8 = sb("q8", [P, 2, HALF])
        w_in = [sem(f"w_in{i}") for i in range(2)]
        wd_in = [sem(f"wd_in{i}") for i in range(2)]
        w_hi_done, w_lo_done, wd_hi_done, wd_lo_done = (
            sem(n) for n in ("w_hi_done", "w_lo_done", "wd_hi_done", "wd_lo_done"))
        up_done, sig_done, silu_done, prod_done = (
            sem(n) for n in ("up_done", "sig_done", "silu_done", "prod_done"))
        down_done, scaled, added, stored = sem("down_done"), sem("scaled"), sem("added"), sem("stored")
        block = core.open_block(ctx)
        UP_UNITS = IB * NH

        @block.sync
        def _(sp):
            for b in range(IB):
                wait(sp, w_lo_done, b - 1)
                sp.dma_start(w[b % 2][:], ins["wgu"][b]).then_inc(w_in[b % 2], 16)
                wait(sp, wd_lo_done, b - 1)
                sp.dma_start(wd[b % 2][:], ins["wdT"][b]).then_inc(wd_in[b % 2], 16)
            if out is not None:
                for t in range(NT):
                    sp.wait_ge(added, t + 1)
                    sp.dma_start(out[t * P:(t + 1) * P, :], x[:, t, :]).then_inc(stored, 16)
                sp.wait_ge(stored, 16 * NT)

        @block.gpsimd
        def _(pool):
            for b in range(IB):
                pool.wait_ge(wd_hi_done, b + 1)
                nc.gpsimd.tensor_tensor(wd_lo[:, b, :], wd[b % 2][:], wd_hi[:, b, :], ALU.subtract)\
                    .then_inc(wd_lo_done, 1)
                for th in range(NH):
                    tr.signed(pool, NH * b + th, inter[:, b, th * HALF:(th + 1) * HALF])
            for t in range(NT):
                wait(pool, added, t - 1)
                tr.signed(pool, UP_UNITS + t, q8[:, t % 2, :])

        @block.scalar
        def _(act):
            def w_split(b):
                act.wait_ge(w_in[b % 2], 16 * (b // 2 + 1))
                wait(act, up_done, NH * (b - 1))
                nc.scalar.activation(w_hi[b % 2][:], w[b % 2][:], ACT.Copy).then_inc(w_hi_done, 1)

            ln.sqrt(act)
            w_split(0)
            ln.hi_parts(act)
            for n in range(UP_UNITS + 1):
                if n < UP_UNITS:
                    b, th = n // NH, n % NH
                    if th == 0:
                        if b + 1 < IB:
                            w_split(b + 1)
                        act.wait_ge(wd_in[b % 2], 16 * (b // 2 + 1))
                        nc.scalar.activation(wd_hi[:, b, :], wd[b % 2][:], ACT.Copy).then_inc(wd_hi_done, 1)
                    act.wait_ge(up_done, n + 1)
                    wait(act, silu_done, n - 1)
                    nc.scalar.activation(sig[:, n % 2, :], core.bank(2 * (n % 4)), ACT.Sigmoid, scale=1.0 / QSCALE)\
                        .then_inc(sig_done, 1)
                if n >= 1:
                    tr.magnitude(act, n - 1)
            for t in range(NT):
                tr.magnitude(act, UP_UNITS + t)

        @block.vector
        def _(v):
            def w_split(b):
                v.wait_ge(w_hi_done, b + 1)
                wait(v, up_done, NH * (b - 1))
                nc.vector.tensor_tensor(w_lo[b % 2][:], w[b % 2][:], w_hi[b % 2][:], ALU.subtract)\
                    .then_inc(w_lo_done, 1)

            ln.statistics(v)
            w_split(0)
            ln.normalise(v)
            for n in range(UP_UNITS + 1):
                if n < UP_UNITS:
                    b, th = n // NH, n % NH
                    if th == 0 and b + 1 < IB:
                        w_split(b + 1)
                    v.wait_ge(sig_done, n + 1)
                    nc.vector.scalar_tensor_tensor(out=silu[:, n % 2, :], in0=core.bank(2 * (n % 4)),
                                                   scalar=1.0 / QSCALE, in1=sig[:, n % 2, :],
                                                   op0=ALU.mult, op1=ALU.mult).then_inc(silu_done, 1)
                    v.wait_ge(silu_done, n + 1)
                    wait(v, tr.s_mag, n - 1)
                    nc.vector.tensor_tensor(tr.clipped[:, n % 2, :], core.bank(2 * (n % 4) + 1),
                                            silu[:, n % 2, :], ALU.mult).then_inc(prod_done, 1)
                    v.wait_ge(prod_done, n + 1)
                    tr.clip(v, n)
                if n >= 1:
                    tr.floor(v, n - 1)

            def add(t):
                v.wait_ge(tr.s_out, UP_UNITS + t + 1)
                nc.vector.scalar_tensor_tensor(out=x[:, t, :], in0=q8[:, t % 2, :], scalar=0.5, in1=x[:, t, :],
                                               op0=ALU.mult, op1=ALU.add).then_inc(added, 1)

            for t in range(NT):
                v.wait_ge(down_done, t + 1)
                wait(v, tr.s_mag, UP_UNITS + t - 1)
                nc.vector.tensor_scalar(tr.clipped[:, t % 2, :], core.bank(t % 2), QSCALE, None, ALU.mult)\
                    .then_inc(scaled, 1)
                v.wait_ge(scaled, t + 1)
                tr.clip(v, UP_UNITS + t)
                tr.floor(v, UP_UNITS + t)
                if t >= 1:
                    add(t - 1)
            add(NT - 1)

        @block.tensor
        def _(pe):
            ln.transposes(pe)
            for n in range(UP_UNITS):
                b, th = n // NH, n % NH
                s = slice(th * HALF, (th + 1) * HALF)
                pe.wait_ge(w_lo_done, b + 1)
                if b == 0:
                    ln.ready(pe, NH - 1)
                wait(pe, prod_done, n - 3)
                for part in range(2):
                    last = product(nc, core.bank(2 * (n % 4) + part), [
                        ((w_hi[b % 2][:, part, k, :], w_lo[b % 2][:, part, k, :]), (ln.hi[:, k, s], ln.lo[:, k, s]))
                        for k in range(KB)])
                last.then_inc(up_done, 1)
            pe.wait_ge(wd_lo_done, IB)
            pe.wait_ge(tr.s_out, UP_UNITS)
            for t in range(NT):
                wait(pe, scaled, t - 1)
                product(nc, core.bank(t % 2), [
                    ((inter[:, b, t * P:(t + 1) * P], None), (wd_hi[:, b, :], wd_lo[:, b, :])) for b in range(IB)])\
                    .then_inc(down_done, 1)


def retrieval_block(core, ins):
    nc = core.nc
    x = core.x
    with ExitStack() as ctx:
        def sb(name, shape, dt=F32):
            return ctx.enter_context(nc.sbuf_tensor(f"rt_{name}", shape, dt))

        def sem(name):
            return core.semaphore(ctx, f"rt_{name}")

        ln = LayerNorm(core, ctx, "rt")
        wq = [sb(f"wq{i}", [P, HALF]) for i in range(2)]
        wq_hi, wq_lo = sb("wq_hi", [P, KB, KVH * HD], F32R), sb("wq_lo", [P, KB, KVH * HD], F32R)
        bq = sb("bq", [P, KVH])
        mz = sb("mz", [P, KVH, MZ])
        mz_hi, mz_lo = sb("mz_hi", [P, KVH, MZ], F32R), sb("mz_lo", [P, KVH, MZ], F32R)
        wo = sb("wo", [P, REP, DM])
        wo_a = sb("wo_a", [P, DM])
        wo_hi, wo_lo = sb("wo_hi", [P, KVH, DM], F32R), sb("wo_lo", [P, KVH, DM], F32R)
        e = sb("e", [P, 2, HALF])
        r = sb("r", [P, 2, HALF])
        sig = sb("sig", [P, 2, HALF])
        sig_hi, sig_lo = sb("sig_hi", [P, KVH, HALF], F32R), sb("sig_lo", [P, KVH, HALF], F32R)
        den = sb("den", [P, 2, 2, 1])
        rden = sb("rden", [P, 2, 2, 1])
        ret = [sb(f"ret{i}", [P, 2, HD]) for i in range(2)]
        ret_hi = [sb(f"ret_hi{i}", [P, KVH, P], F32R) for i in range(2)]
        ret_lo = [sb(f"ret_lo{i}", [P, KVH, P], F32R) for i in range(2)]
        wq_in = [sem(f"wq_in{i}") for i in range(2)]
        bq_in, mz_in, wo_in = sem("bq_in"), sem("mz_in"), sem("wo_in")
        wq_hi_done, wq_lo_done, mz_hi_done, mz_lo_done = (
            sem(n) for n in ("wq_hi_done", "wq_lo_done", "mz_hi_done", "mz_lo_done"))
        wo_sum, wo_hi_done, wo_lo_done = sem("wo_sum"), sem("wo_hi_done"), sem("wo_lo_done")
        q_done, neg_done, er_done, sig_done, sig_hi_done, sig_lo_done = (
            sem(n) for n in ("q_done", "neg_done", "er_done", "sig_done", "sig_hi_done", "sig_lo_done"))
        num_done, den_done, rden_done, ret_done = (sem(n) for n in ("num_done", "den_done", "rden_done", "ret_done"))
        ret_T, ret_hi_done, ret_lo_done = sem("ret_transposed"), sem("ret_hi_done"), sem("ret_lo_done")
        y_done, added = sem("y_done"), sem("added")
        block = core.open_block(ctx)
        TH = NT // NH
        PAIRS = KVH // 2

        def half(n):
            return slice(n % 2 * HALF, (n % 2 + 1) * HALF)

        @block.sync
        def _(sp):
            for n in range(2 * KB):
                wait(sp, wq_lo_done, n - 1)
                sp.dma_start(wq[n % 2][:], ins["wq1T"][:, n // 2, half(n)]).then_inc(wq_in[n % 2], 16)
                if n == 1:
                    sp.dma_start(bq[:], ins["bq1T"]).then_inc(bq_in, 16)
                    sp.dma_start(mz[:], ins["mz"]).then_inc(mz_in, 16)
            for h in range(KVH):
                wait(sp, wo_sum, 3 * h)
                sp.dma_start(wo[:], ins["wo1T"][h].rearrange("g e n -> e g n")).then_inc(wo_in, 16)

        @block.gpsimd
        def _(pool):
            pool.wait_ge(mz_hi_done, 1)
            nc.gpsimd.tensor_tensor(mz_lo[:], mz[:], mz_hi[:], ALU.subtract).then_inc(mz_lo_done, 1)
            for n in range(NH * KVH):
                th, h = n // KVH, n % KVH
                pool.wait_ge(sig_hi_done, n + 1)
                nc.gpsimd.tensor_tensor(sig_lo[:, h, :], sig[:, n % 2, :], sig_hi[:, h, :], ALU.subtract)\
                    .then_inc(sig_lo_done, 1)

        @block.scalar
        def _(act):
            ln.sqrt(act)
            for n in range(2 * KB):
                act.wait_ge(wq_in[n % 2], 16 * (n // 2 + 1))
                nc.scalar.activation(wq_hi[:, n // 2, half(n)], wq[n % 2][:], ACT.Copy).then_inc(wq_hi_done, 1)
            ln.hi_parts(act)
            act.wait_ge(mz_in, 16)
            nc.scalar.activation(mz_hi[:], mz[:], ACT.Copy).then_inc(mz_hi_done, 1)
            act.wait_ge(bq_in, 16)

            def sig_split(n):
                th, h = n // KVH, n % KVH
                act.wait_ge(sig_done, n + 1)
                if th >= 1:
                    act.wait_ge(num_done, PAIRS * TH * th)
                nc.scalar.activation(sig_hi[:, h, :], sig[:, n % 2, :], ACT.Copy).then_inc(sig_hi_done, 1)

            for th in range(NH):
                for h in range(KVH):
                    n = th * KVH + h
                    act.wait_ge(neg_done, n + 1)
                    wait(act, sig_done, n - 1)
                    nc.scalar.activation(e[:, n % 2, :], e[:, n % 2, :], ACT.Exp)
                    nc.scalar.activation(r[:, n % 2, :], core.bank(n % 2), ACT.Relu, bias=bq[:, h:h + 1])\
                        .then_inc(er_done, 1)
                    if th == 0:
                        act.wait_ge(wo_sum, 3 * h + 3)
                        nc.scalar.activation(wo_hi[:, h, :], wo_a[:], ACT.Copy).then_inc(wo_hi_done, 1)
                    if h >= 1:
                        sig_split(n - 1)
                sig_split(th * KVH + KVH - 1)
                for m in range(th * TH * PAIRS, (th + 1) * TH * PAIRS):
                    t, pr = m // PAIRS, m % PAIRS
                    act.wait_ge(ret_T, m + 1)
                    wait(act, y_done, t - 1)
                    nc.scalar.activation(ret_hi[t % 2][:, 2 * pr:2 * pr + 2, :],
                                         core.bank(4 + m % 2)[:, 0:2 * P].rearrange("p (h n) -> p h n", h=2),
                                         ACT.Copy).then_inc(ret_hi_done, 1)

        @block.vector
        def _(v):
            ln.statistics(v)
            for n in range(2 * KB):
                v.wait_ge(wq_hi_done, n + 1)
                nc.vector.tensor_tensor(wq_lo[:, n // 2, half(n)], wq[n % 2][:], wq_hi[:, n // 2, half(n)],
                                        ALU.subtract).then_inc(wq_lo_done, 1)
            ln.normalise(v)

            def wo_parts(h):
                v.wait_ge(wo_in, 16 * (h + 1))
                wait(v, wo_lo_done, h)
                for g in range(1, REP):
                    wait(v, wo_sum, 3 * h + g - 1)
                    nc.vector.tensor_tensor(wo_a[:], wo[:, 0, :] if g == 1 else wo_a[:], wo[:, g, :], ALU.add)\
                        .then_inc(wo_sum, 1)

            def wo_low(h):
                v.wait_ge(wo_hi_done, h + 1)
                nc.vector.tensor_tensor(wo_lo[:, h, :], wo_a[:], wo_hi[:, h, :], ALU.subtract)\
                    .then_inc(wo_lo_done, 1)

            def retrieve(m):
                s = m % 2
                psum = core.bank(2 + s).rearrange("p (h n) -> p h n", h=2)
                v.wait_ge(num_done, m + 1)
                nc.vector.tensor_scalar_add(den[:, s], psum[:, :, HD:HD + 1], RET_EPS).then_inc(den_done, 1)
                v.wait_ge(den_done, m + 1)
                nc.vector.reciprocal(rden[:, s], den[:, s]).then_inc(rden_done, 1)
                v.wait_ge(rden_done, m + 1)
                wait(v, ret_T, m - 1)
                nc.vector.tensor_tensor(ret[s][:], psum[:, :, 0:HD], rden[:, s].broadcast_to([P, 2, HD]), ALU.mult)\
                    .then_inc(ret_done, 1)

            def ret_low(m):
                t, pr = m // PAIRS, m % PAIRS
                v.wait_ge(ret_hi_done, m + 1)
                nc.vector.tensor_tensor(ret_lo[t % 2][:, 2 * pr:2 * pr + 2, :],
                                        core.bank(4 + m % 2)[:, 0:2 * P].rearrange("p (h n) -> p h n", h=2),
                                        ret_hi[t % 2][:, 2 * pr:2 * pr + 2, :], ALU.subtract)\
                    .then_inc(ret_lo_done, 1)

            def add(t):
                v.wait_ge(y_done, t + 1)
                nc.vector.tensor_tensor(x[:, t, :], core.bank(6 + t % 2), x[:, t, :], ALU.add).then_inc(added, 1)

            def sig_sum(n):
                v.wait_ge(er_done, n + 1)
                wait(v, sig_lo_done, n - 1)
                nc.vector.tensor_tensor(sig[:, n % 2, :], e[:, n % 2, :], r[:, n % 2, :], ALU.add)\
                    .then_inc(sig_done, 1)

            v.wait_ge(bq_in, 16)
            for th in range(NH):
                for h in range(KVH):
                    n = th * KVH + h
                    if th == 0:
                        wo_parts(h)
                    v.wait_ge(q_done, n + 1)
                    wait(v, sig_done, n - 1)
                    nc.vector.tensor_scalar(e[:, n % 2, :], core.bank(n % 2), bq[:, h:h + 1], 0.0,
                                            ALU.add, ALU.min).then_inc(neg_done, 1)
                    if h >= 1:
                        sig_sum(n - 1)
                    if th == 0:
                        wo_low(h)
                sig_sum(th * KVH + KVH - 1)
                for m in range(th * TH * PAIRS, (th + 1) * TH * PAIRS):
                    retrieve(m)
                    if m % (TH * PAIRS) >= 1:
                        ret_low(m - 1)
                    t = m // PAIRS
                    if m % PAIRS == 2 and t % TH >= 1:
                        add(t - 1)
                ret_low((th + 1) * TH * PAIRS - 1)
                add((th + 1) * TH - 1)

        @block.tensor
        def _(pe):
            ln.transposes(pe)
            pe.wait_ge(wq_lo_done, 2 * KB)
            ln.ready(pe, NH - 1)

            def back(m):
                pe.wait_ge(ret_done, m + 1)
                wait(pe, ret_lo_done, m - 1)
                for j in range(2):
                    last = nc.tensor.transpose(core.bank(4 + m % 2)[:, j * P:(j + 1) * P], ret[m % 2][:, j, :],
                                               core.ident[:])
                last.then_inc(ret_T, 1)

            def project(t):
                pe.wait_ge(ret_lo_done, (t + 1) * PAIRS)
                wait(pe, added, t - 1)
                product(nc, core.bank(6 + t % 2), [
                    ((ret_hi[t % 2][:, h, :], ret_lo[t % 2][:, h, :]), (wo_hi[:, h, :], wo_lo[:, h, :]))
                    for h in range(KVH)]).then_inc(y_done, 1)

            for th in range(NH):
                s = slice(th * HALF, (th + 1) * HALF)
                for h in range(KVH):
                    n = th * KVH + h
                    wait(pe, er_done, n - 1)
                    c = slice(h * HD, (h + 1) * HD)
                    product(nc, core.bank(n % 2), [
                        ((wq_hi[:, k, c], wq_lo[:, k, c]), (ln.hi[:, k, s], ln.lo[:, k, s])) for k in range(KB)])\
                        .then_inc(q_done, 1)
                pe.wait_ge(sig_lo_done, (th + 1) * KVH)
                pe.wait_ge(mz_lo_done, 1)
                pe.wait_ge(wo_lo_done, KVH)
                first = th * TH * PAIRS
                for m in range(first, first + TH * PAIRS):
                    t, pr = m // PAIRS, m % PAIRS
                    wait(pe, ret_done, m - 1)
                    q = slice((t % TH) * P, (t % TH + 1) * P)
                    for j in range(2):
                        h = 2 * pr + j
                        last = product(nc, core.bank(2 + m % 2)[:, j * 256:j * 256 + MZ], [
                            ((sig_hi[:, h, q], sig_lo[:, h, q]), (mz_hi[:, h, :], mz_lo[:, h, :]))])
                    last.then_inc(num_done, 1)
                    if m > first:
                        back(m - 1)
                    if pr == 1 and t % TH >= 1:
                        project(t - 1)
                back(first + TH * PAIRS - 1)
                project((th + 1) * TH - 1)


def macaron(nc, ins, out):
    scratch = {n: nc.dram_tensor(f"scratch_{n}", [HEADS, P, TOK], F32).ap() for n in "qk"}
    v = nc.dram_tensor("scratch_v", [HEADS, P, NT, HD], F32).ap()
    scratch["v"] = v
    scratch["v_flat"] = v.rearrange("h p t d -> h p (t d)")
    with ExitStack() as ctx:
        core = Core(nc, ctx)
        setup_block(core, ins)
        ffn0_block(core, ins, "f0a")
        with ExitStack() as attention:
            core.open_attention(attention)
            qkv_block(core, ins, scratch)
            attention_block(core, ins, scratch)
        ffn0_block(core, ins, "f0b")
        ffn1_block(core, ins, "f1a")
        retrieval_block(core, ins)
        ffn1_block(core, ins, "f1b", out=out)


def kernel(**inputs):
    import numpy as np
    import concourse.bacc as bacc
    from concourse.bass_utils import run_bass_kernel_spmd

    a = {n: np.asarray(v) for n, v in inputs.items()}
    c = np.ascontiguousarray

    def blocks(w, n=P):
        return c(w.reshape(-1, n, w.shape[1]).transpose(1, 0, 2))

    def chunks(w):
        return c(w.reshape(KB, P, -1, HALF).transpose(2, 1, 0, 3))

    def cols(b):
        return c(b.reshape(-1, P).T)

    def padded(w):
        z = np.zeros((IB * P, w.shape[1]), w.dtype)
        z[:w.shape[0]] = w
        return z

    gate, up = (padded(a[f"L1_ffn_w_{n}"]).reshape(IB, P, KB, P) for n in ("gate", "up"))
    mz = np.zeros((P, KVH, MZ), a["L1_attn_M"].dtype)
    mz[:, :, :HD] = a["L1_attn_M"].transpose(1, 0, 2)
    mz[:, :, HD] = a["L1_attn_z"].T
    arrays = {
        "x": c(a["L0_attn_hidden_states"].reshape(TOK, DM)),
        "w12T": blocks(a["L0_ffn_w12"].T), "b12T": cols(a["L0_ffn_b12"]),
        "w3T": blocks(a["L0_ffn_w3"].T), "b3": c(a["L0_ffn_b3"]),
        "Wq": chunks(a["L0_attn_Wq"]), "Wk": chunks(a["L0_attn_Wk"]), "Wv": chunks(a["L0_attn_Wv"]),
        "Wo": c(a["L0_attn_Wo"].reshape(HEADS, HD, DM)), "bo": c(a["L0_attn_bo"]),
        "bq": cols(a["L0_attn_bq"]), "bk": cols(a["L0_attn_bk"]), "bv": cols(a["L0_attn_bv"]),
        "gq": cols(a["L0_attn_gq"]), "gk": cols(a["L0_attn_gk"]),
        "wgu": c(np.stack([gate, up], axis=1).transpose(0, 4, 1, 3, 2)),
        "wdT": padded(a["L1_ffn_w_down"].T).reshape(IB, P, DM),
        "wq1T": blocks(a["L1_attn_Wq"].reshape(KVH, REP, HD, DM)[:, 0].reshape(KVH * HD, DM).T),
        "bq1T": cols(a["L1_attn_bq"].reshape(KVH, REP, HD)[:, 0].reshape(-1)),
        "mz": mz,
        "wo1T": c(a["L1_attn_Wo"].T.reshape(KVH, REP, HD, DM)),
    }
    nc = bacc.Bacc("TRN2", target_bir_lowering=False, num_devices=1)
    ins = {n: nc.dram_tensor(f"in_{n}", v.shape, mybir.dt.from_np(v.dtype), kind="ExternalInput").ap()
           for n, v in arrays.items()}
    out = nc.dram_tensor("out_x", (TOK, DM), F32, kind="ExternalOutput").ap()
    macaron(nc, ins, out)
    r = run_bass_kernel_spmd(nc, [{f"in_{n}": v for n, v in arrays.items()}], core_ids=[0])
    return r.results[0]["out_x"].reshape(1, TOK, DM)
```

```python
from contextlib import ExitStack

import concourse.bass as bass
from concourse import mybir

F32 = mybir.dt.float32
F32R = mybir.dt.float32r
ALU = mybir.AluOpType
ACT = mybir.ActivationFunctionType
AX = mybir.AxisListType

P = 128
TOK = 1024
DM = 512
NT = TOK // P
KB = DM // P
HALF = 512
NH = TOK // HALF
CHUNK = 1024
LN_EPS = 1e-5
RMS_EPS = 1e-6

HEADS = 32
HD = 128
INNER = HEADS * HD
GROUP = HALF // HD
NGROUPS = HEADS // GROUP

M0 = 512
MB0 = M0 // P

INTER = 1376
IB = (INTER + P - 1) // P
QSCALE = 128.0
ROUND = float(2 ** 23)

KVH = 8
REP = HEADS // KVH
MZ = HD + 2
HEADW = KB * HD + MZ
RET_EPS = 1e-6


def wait(eng, sem, value):
    if isinstance(value, int) and value <= 0:
        return
    eng.wait_ge(sem, value)


class Core:

    def __init__(self, nc, ctx):
        self.nc = nc
        self.sems = []
        self.cols_in = ctx.enter_context(nc.semaphore("cols_in"))
        self.x = ctx.enter_context(nc.sbuf_tensor("x", [P, NT, DM], F32))
        self.ident = ctx.enter_context(nc.sbuf_tensor("ident", [P, P], F32))
        self.half = ctx.enter_context(nc.sbuf_tensor("half", [P, 1], F32))
        self.ln = LayerNormBuffers(nc, ctx)
        self.first = Chunk(nc, ctx, "first")
        self.ps = [ctx.enter_context(nc.psum_tensor(f"ps{i}", [P, 2 * HALF], F32)) for i in range(4)]

    def open_attention(self, ctx):
        nc = self.nc
        self.rms = ctx.enter_context(nc.sbuf_tensor("rms", [P, TOK + NT], F32))
        self.k_raw, self.q_raw, self.kn = (ctx.enter_context(nc.sbuf_tensor(n, [P, TOK], F32))
                                           for n in ("k_raw", "q_raw", "kn"))
        self.cols = {n: ctx.enter_context(nc.sbuf_tensor(f"col_{n}", [P, HEADS], F32))
                     for n in ("bq", "bk", "bv", "gq", "gk")}

    def semaphore(self, ctx, name):
        s = ctx.enter_context(self.nc.semaphore(name))
        self.sems.append(s)
        return s

    def open_block(self, ctx):
        nc, ctx_sems, self.sems = self.nc, self.sems, []

        def clear():
            nums = sorted(s.num for s in ctx_sems)
            starts = [n for n in nums if n - 1 not in nums]
            ends = [n + 1 for n in nums if n + 1 not in nums]
            with nc.Block() as block:
                @block.gpsimd
                def _(pool):
                    for a, b in zip(starts, ends):
                        nc.gpsimd.sem_clear(range(a, b))

        ctx.callback(clear)
        return ctx.enter_context(nc.Block())

    def bank(self, b):
        return self.ps[b // 2][:, (b % 2) * HALF:(b % 2 + 1) * HALF]


class Chunk:

    def __init__(self, nc, ctx, name, n=CHUNK, raw=True):
        if raw:
            self.raw = ctx.enter_context(nc.sbuf_tensor(f"{name}_raw", [P, n], F32))
        self.hi = ctx.enter_context(nc.sbuf_tensor(f"{name}_hi", [P, n], F32R))
        self.lo = ctx.enter_context(nc.sbuf_tensor(f"{name}_lo", [P, n], F32R))

    def parts(self, c, n=P):
        return self.hi[:, c:c + n], self.lo[:, c:c + n]


class Prefetch:

    def __init__(self, core, ctx, tag, src):
        self.nc, self.first, self.src, self.n = core.nc, core.first, src, src.shape[-1]
        self.s_in, self.s_hi, self.s_lo = (core.semaphore(ctx, f"{tag}_first_{n}") for n in ("in", "hi", "lo"))

    def load(self, sp):
        sp.dma_start(self.first.raw[:, :self.n], self.src).then_inc(self.s_in, 16)

    def high(self, act):
        act.wait_ge(self.s_in, 16)
        self.nc.scalar.activation(self.first.hi[:, :self.n], self.first.raw[:, :self.n], ACT.Copy)\
            .then_inc(self.s_hi, 1)

    def low(self, pool):
        pool.wait_ge(self.s_hi, 1)
        self.nc.gpsimd.tensor_tensor(self.first.lo[:, :self.n], self.first.raw[:, :self.n],
                                     self.first.hi[:, :self.n], ALU.subtract).then_inc(self.s_lo, 1)


class LayerNormBuffers:

    def __init__(self, nc, ctx):
        def sb(name, shape, dt=F32):
            return ctx.enter_context(nc.sbuf_tensor(f"ln_{name}", shape, dt))

        self.stats = sb("stats", [P, NT, 6])
        self.meanvar = sb("meanvar", [P, NT, 2])
        self.var, self.sd, self.r0, self.corr, self.rstd = (sb(n, [P, NT]) for n in ("var", "sd", "r0", "corr", "rstd"))
        self.xn = sb("xn", [P, 2, DM])
        self.hi = sb("xT_hi", [P, KB, TOK], F32R)
        self.lo = sb("xT_lo", [P, KB, TOK], F32R)


class LayerNorm:
    STEPS = NT + 4

    def __init__(self, core, ctx, tag, banks):
        self.core, self.nc, self.banks, b = core, core.nc, banks, core.ln
        self.stats, self.meanvar, self.var, self.sd, self.r0, self.corr, self.rstd, self.xn, self.hi, self.lo = (
            b.stats, b.meanvar, b.var, b.sd, b.r0, b.corr, b.rstd, b.xn, b.hi, b.lo)

        def sem(name):
            return core.semaphore(ctx, f"{tag}_ln_{name}")

        self.s_stats, self.s_aggr, self.s_var, self.s_r0, self.s_corr, self.s_rstd = (
            sem(n) for n in ("stats_done", "aggr_done", "var_done", "r0_done", "corr_done", "rstd_done"))
        self.s_sd, self.s_xn, self.s_T = sem("sd_done"), sem("xn_done"), sem("transposed")
        self.s_hi, self.s_lo = sem("hi_done"), sem("lo_done")

    def _psum(self, t):
        return self.core.bank(self.banks[t % 2]).rearrange("p (k n) -> p k n", k=KB)

    def invert(self, v, k):
        t = k - 1
        if 0 <= t < NT:
            v.wait_ge(self.s_sd, t + 1)
            self.nc.vector.reciprocal(self.r0[:, t:t + 1], self.sd[:, t:t + 1]).then_inc(self.s_r0, 1)

    def vector(self, v, k):
        nc = self.nc
        if k < NT:
            nc.vector.bn_stats(out=self.stats[:, k, :], in_=self.core.x[:, k, :]).then_inc(self.s_stats, 1)
            v.wait_ge(self.s_stats, k + 1)
            nc.vector.bn_aggr(out=self.meanvar[:, k, :], in_=self.stats[:, k, :]).then_inc(self.s_aggr, 1)
        t = k - 2
        if 0 <= t < NT:
            v.wait_ge(self.s_rstd, t + 1)
            wait(v, self.s_T, t - 1)
            nc.vector.tensor_scalar(self.xn[:, t % 2, :], self.core.x[:, t, :], self.meanvar[:, t, 0:1],
                                    self.rstd[:, t:t + 1], ALU.subtract, ALU.mult).then_inc(self.s_xn, 1)
        t = k - 4
        if t >= 0:
            v.wait_ge(self.s_hi, t + 1)
            nc.vector.tensor_tensor(self.lo[:, :, t * P:(t + 1) * P], self._psum(t),
                                    self.hi[:, :, t * P:(t + 1) * P], ALU.subtract).then_inc(self.s_lo, 1)

    def gpsimd(self, pool, k):
        nc = self.nc
        if k < NT:
            pool.wait_ge(self.s_aggr, k + 1)
            nc.gpsimd.tensor_scalar(self.var[:, k:k + 1], self.meanvar[:, k, 1:2], LN_EPS, None, ALU.add)\
                .then_inc(self.s_var, 1)
        t = k - 1
        if 0 <= t < NT:
            c = slice(t, t + 1)
            pool.wait_ge(self.s_r0, t + 1)
            nc.gpsimd.tensor_tensor(self.corr[:, c], self.var[:, c], self.r0[:, c], ALU.mult).then_inc(self.s_corr, 1)
            pool.wait_ge(self.s_corr, 3 * t + 1)
            nc.gpsimd.tensor_tensor(self.corr[:, c], self.corr[:, c], self.r0[:, c], ALU.mult)\
                .then_inc(self.s_corr, 1)
            pool.wait_ge(self.s_corr, 3 * t + 2)
            nc.gpsimd.tensor_scalar(self.corr[:, c], self.corr[:, c], -0.5, 1.5, ALU.mult, ALU.add)\
                .then_inc(self.s_corr, 1)
            pool.wait_ge(self.s_corr, 3 * t + 3)
            nc.gpsimd.tensor_tensor(self.rstd[:, c], self.r0[:, c], self.corr[:, c], ALU.mult)\
                .then_inc(self.s_rstd, 1)

    def scalar(self, act, k):
        if k < NT:
            act.wait_ge(self.s_var, k + 1)
            self.nc.scalar.activation(self.sd[:, k:k + 1], self.var[:, k:k + 1], ACT.Sqrt).then_inc(self.s_sd, 1)
        t = k - 3
        if 0 <= t < NT:
            act.wait_ge(self.s_T, t + 1)
            self.nc.scalar.activation(self.hi[:, :, t * P:(t + 1) * P], self._psum(t), ACT.Copy)\
                .then_inc(self.s_hi, 1)

    def tensor(self, pe, k):
        t = k - 3
        if 0 <= t < NT:
            pe.wait_ge(self.s_xn, t + 1)
            wait(pe, self.s_lo, t - 1)
            for b in range(KB):
                last = self.nc.tensor.transpose(self._psum(t)[:, b, :], self.xn[:, t % 2, b * P:(b + 1) * P],
                                                self.core.ident[:])
            last.then_inc(self.s_T, 1)


def product(nc, out, pairs, start=True, stop=True):
    terms = []
    for (sh, sl), (mh, ml) in pairs:
        terms.append((sh, mh))
        if ml is not None:
            terms.append((sh, ml))
        if sl is not None:
            terms.append((sl, mh))
    for n, (s, m) in enumerate(terms):
        last = nc.tensor.matmul(out, s, m, start=(start and n == 0), stop=(stop and n == len(terms) - 1))
    return last


def setup_block(core, ins, following):
    nc = core.nc
    with ExitStack() as ctx:
        loaded = [core.semaphore(ctx, f"setup_loaded{t}") for t in range(NT)]
        made = core.semaphore(ctx, "setup_made")
        ln = LayerNorm(core, ctx, "setup", (0, 1))
        prefetch = Prefetch(core, ctx, "setup", following)
        block = core.open_block(ctx)

        @block.sync
        def _(sp):
            for t in range(NT):
                sp.dma_start(core.x[:, t, :], ins["x"][t * P:(t + 1) * P, :]).then_inc(loaded[t], 16)
                if t == 3:
                    prefetch.load(sp)

        @block.gpsimd
        def _(pool):
            nc.gpsimd.memset(core.ident[:], 0.0).then_inc(made, 1)
            pool.wait_ge(made, 1)
            nc.gpsimd.affine_select(out=core.ident[:], in_=core.ident[:], compare_op=ALU.not_equal, fill=1.0,
                                    base=0, pattern=[[-1, P]], channel_multiplier=1).then_inc(made, 1)
            nc.gpsimd.memset(core.half[:], 0.5)
            for k in range(ln.STEPS):
                if k == 6:
                    prefetch.low(pool)
                ln.gpsimd(pool, k)

        @block.vector
        def _(v):
            for k in range(ln.STEPS):
                if k < NT:
                    v.wait_ge(loaded[k], 16)
                ln.invert(v, k)
                ln.vector(v, k)

        @block.scalar
        def _(act):
            for k in range(ln.STEPS):
                ln.scalar(act, k)
                if k == 3:
                    prefetch.high(act)

        @block.tensor
        def _(pe):
            pe.wait_ge(made, 2)
            for k in range(ln.STEPS):
                ln.tensor(pe, k)


def ffn0_block(core, ins, tag, following):
    nc = core.nc
    x, xT = core.x, core.ln
    with ExitStack() as ctx:
        def sb(name, shape, dt=F32):
            return ctx.enter_context(nc.sbuf_tensor(f"{tag}_{name}", shape, dt))

        def sem(name):
            return core.semaphore(ctx, f"{tag}_{name}")

        ln = LayerNorm(core, ctx, tag, (6, 7))
        prefetch = Prefetch(core, ctx, tag, following)
        w = [core.first, Chunk(nc, ctx, f"{tag}_w12")]
        w3 = sb("w3", [P, MB0, DM])
        w3_hi, w3_lo = sb("w3_hi", [P, MB0, DM], F32R), sb("w3_lo", [P, MB0, DM], F32R)
        b12 = sb("b12", [P, 2 * MB0])
        b3 = sb("b3", [P, DM])
        sig = sb("sig", [P, 2, HALF])
        gated = sb("gated", [P, 2, HALF])
        h = sb("h", [P, 2, HALF])
        h_hi, h_lo = sb("h_hi", [P, MB0, TOK], F32R), sb("h_lo", [P, MB0, TOK], F32R)
        w_in = [sem(f"w_in{i}") for i in range(2)]
        w3_in, bias_in, b3_in = sem("w3_in"), sem("bias_in"), sem("b3_in")
        w_hi_done, w_lo_done = sem("w_hi_done"), sem("w_lo_done")
        w3_hi_done, w3_lo_done = sem("w3_hi_done"), sem("w3_lo_done")
        up_done, sig_done, gated_done, h_done = sem("up_done"), sem("sig_done"), sem("gated_done"), sem("h_done")
        h_hi_done, h_lo_done = sem("h_hi_done"), sem("h_lo_done")
        biased, down_done, added = sem("biased"), sem("down_done"), sem("added")
        block = core.open_block(ctx)
        units = [(mb, th) for mb in range(MB0) for th in range(NH)]

        def tok(th):
            return slice(th * HALF, (th + 1) * HALF)

        @block.sync
        def _(sp):
            sp.dma_start(w[1].raw[:], ins["w12"][1]).then_inc(w_in[1], 16)
            sp.dma_start(b12[:], ins["b12T"]).then_inc(bias_in, 16)
            sp.dma_start(b3[:], ins["b3"].partition_broadcast(P)).then_inc(b3_in, 16)
            for b in range(2, MB0):
                wait(sp, w_lo_done, b - 2)
                sp.dma_start(w[b % 2].raw[:], ins["w12"][b]).then_inc(w_in[b % 2], 16)
                if b == 2:
                    sp.dma_start(w3[:], ins["w3T"]).then_inc(w3_in, 16)
            sp.wait_ge(up_done, NH * (MB0 - 1))
            prefetch.load(sp)

        @block.gpsimd
        def _(pool):
            pool.wait_ge(b3_in, 16)
            nc.gpsimd.tensor_tensor(b3[:], b3[:], core.half[:].broadcast_to([P, DM]), ALU.mult).then_inc(biased, 1)
            pool.wait_ge(biased, 1)
            for u, (mb, th) in enumerate(units):
                nc.gpsimd.tensor_tensor(x[:, u, :], x[:, u, :], b3[:], ALU.add).then_inc(biased, 1)
                if u % NH == 0:
                    pool.wait_ge(w3_hi_done, mb + 1)
                    nc.gpsimd.tensor_tensor(w3_lo[:, mb, :], w3[:, mb, :], w3_hi[:, mb, :], ALU.subtract)\
                        .then_inc(w3_lo_done, 1)
                pool.wait_ge(h_hi_done, u + 1)
                nc.gpsimd.tensor_tensor(h_lo[:, mb, tok(th)], h[:, u % 2, :], h_hi[:, mb, tok(th)], ALU.subtract)\
                    .then_inc(h_lo_done, 1)
            prefetch.low(pool)
            for k in range(ln.STEPS):
                ln.gpsimd(pool, k)

        @block.vector
        def _(v):
            v.wait_ge(bias_in, 16)
            for u, (mb, th) in enumerate(units):
                x1, x2 = core.bank(2 * (u % 2)), core.bank(2 * (u % 2) + 1)
                if th == 0 and mb + 1 < MB0:
                    v.wait_ge(w_hi_done, mb + 1)
                    nxt = w[(mb + 1) % 2]
                    nc.vector.tensor_tensor(nxt.lo[:], nxt.raw[:], nxt.hi[:], ALU.subtract).then_inc(w_lo_done, 1)
                v.wait_ge(sig_done, u + 1)
                nc.vector.scalar_tensor_tensor(out=gated[:, u % 2, :], in0=x1, scalar=b12[:, mb:mb + 1],
                                               in1=sig[:, u % 2, :], op0=ALU.add, op1=ALU.mult)\
                    .then_inc(gated_done, 1)
                v.wait_ge(gated_done, u + 1)
                wait(v, h_lo_done, u - 1)
                nc.vector.scalar_tensor_tensor(out=h[:, u % 2, :], in0=x2, scalar=b12[:, MB0 + mb:MB0 + mb + 1],
                                               in1=gated[:, u % 2, :], op0=ALU.add, op1=ALU.mult)\
                    .then_inc(h_done, 1)
            for k in range(ln.STEPS):
                ln.invert(v, k)
                if k < NT:
                    v.wait_ge(down_done, k + 1)
                    v.wait_ge(biased, k + 2)
                    nc.vector.scalar_tensor_tensor(out=x[:, k, :], in0=core.bank(4 + k % 2), scalar=0.5,
                                                   in1=x[:, k, :], op0=ALU.mult, op1=ALU.add).then_inc(added, 1)
                    v.wait_ge(added, k + 1)
                ln.vector(v, k)

        @block.scalar
        def _(act):
            def w_split(b):
                act.wait_ge(w_in[b % 2], 16 * ((b + 1) // 2))
                wait(act, up_done, NH * (b - 1))
                nc.scalar.activation(w[b % 2].hi[:], w[b % 2].raw[:], ACT.Copy).then_inc(w_hi_done, 1)

            def split(u):
                mb, th = units[u]
                act.wait_ge(h_done, u + 1)
                nc.scalar.activation(h_hi[:, mb, tok(th)], h[:, u % 2, :], ACT.Copy).then_inc(h_hi_done, 1)

            act.wait_ge(bias_in, 16)
            for u, (mb, th) in enumerate(units):
                if th == 0 and mb + 1 < MB0:
                    w_split(mb + 1)
                act.wait_ge(up_done, u + 1)
                wait(act, gated_done, u - 1)
                nc.scalar.activation(sig[:, u % 2, :], core.bank(2 * (u % 2)), ACT.Sigmoid,
                                     bias=b12[:, mb:mb + 1]).then_inc(sig_done, 1)
                if th == 0:
                    act.wait_ge(w3_in, 16)
                    nc.scalar.activation(w3_hi[:, mb, :], w3[:, mb, :], ACT.Copy).then_inc(w3_hi_done, 1)
                if u >= 1:
                    split(u - 1)
            split(len(units) - 1)
            prefetch.high(act)
            for k in range(ln.STEPS):
                ln.scalar(act, k)

        @block.tensor
        def _(pe):
            for u, (mb, th) in enumerate(units):
                wait(pe, w_lo_done, mb)
                wait(pe, h_done, u - 1)
                for part in range(2):
                    last = product(nc, core.bank(2 * (u % 2) + part), [
                        (w[mb % 2].parts((part * KB + k) * P), (xT.hi[:, k, tok(th)], xT.lo[:, k, tok(th)]))
                        for k in range(KB)])
                last.then_inc(up_done, 1)
            pe.wait_ge(w3_lo_done, MB0)
            for k in range(ln.STEPS):
                if k < NT:
                    s = slice(k * P, (k + 1) * P)
                    down = [((h_hi[:, m, s], h_lo[:, m, s]), (w3_hi[:, m, :], w3_lo[:, m, :])) for m in range(MB0)]
                    th = k * P // HALF
                    pe.wait_ge(h_lo_done, NH * (MB0 - 2) + th + 1)
                    wait(pe, added, k - 1)
                    product(nc, core.bank(4 + k % 2), down[:-1], stop=False)
                    pe.wait_ge(h_lo_done, NH * (MB0 - 1) + th + 1)
                    product(nc, core.bank(4 + k % 2), down[-1:], start=False).then_inc(down_done, 1)
                ln.tensor(pe, k)


def qkv_block(core, ins, scratch):
    nc = core.nc
    with ExitStack() as ctx:
        def sb(name, shape, dt=F32):
            return ctx.enter_context(nc.sbuf_tensor(f"qkv_{name}", shape, dt))

        def sem(name):
            return core.semaphore(ctx, f"qkv_{name}")

        Q, K, V = range(3)
        UNITS = 8
        FIRST = CHUNK // DM
        xT = core.ln
        w = [sb(f"w{t}", [P, KB, HALF]) for t in range(3)]
        w_hi = [sb(f"w{t}_hi", [P, KB, HALF], F32R) for t in range(3)]
        w_lo = [sb(f"w{t}_lo", [P, KB, HALF], F32R) for t in range(3)]
        res = [sb(f"res{i}", [P, HALF]) for i in range(4)]
        sq = sb("sq", [P, 2, HALF])
        acc = [sb(f"acc{t}", [P, TOK]) for t in (Q, K)]
        ones = sb("ones", [P, P])
        bo = sb("bo", [P, DM])
        ms, sd, r0, corr, rs = (sb(n, [P, 2, NT]) for n in ("ms", "sd", "r0", "corr", "rs"))
        diag = sb("diag", [P, NT, P])
        w_in = [sem(f"w_in{t}") for t in range(3)]
        w_hi_done, w_lo_done, proj_done, res_done = (sem(n) for n in
                                                     ("w_hi_done", "w_lo_done", "proj_done", "res_done"))
        stored = [sem(f"stored{i}") for i in range(4)]
        sq_done, acc_done, sums_done, ms_done, sd_done, rs_done, diag_done, spread_done, rms_done = (
            sem(n) for n in ("sq_done", "acc_done", "sums_done", "ms_done", "sd_done", "rs_done", "diag_done",
                             "spread_done", "rms_done"))
        k_in, q_in, bo_in = sem("k_in"), sem("q_in"), sem("bo_in")
        AT_SUMS, AT_SPREAD = 1, 5
        block = core.open_block(ctx)
        weights = [ins["Wq"], ins["Wk"], ins["Wv"]]
        bias = [core.cols["bq"], core.cols["bk"]]

        def groups(eng, body):
            body(0)
            with eng.Fori(1, NGROUPS - 1) as g:
                body(g)
            body(NGROUPS - 1)

        def is_last(g):
            return isinstance(g, int) and g == NGROUPS - 1

        @block.sync
        def _(sp):
            def load(g, t):
                wait(sp, w_hi_done, (g - 1) * 3 + t + 1)
                wait(sp, w_lo_done, (g - 1) * 3 + t + 1)
                sp.dma_start(w[t][:], weights[t][bass.ds(g, 1)].rearrange("a p k n -> p (a k) n"))\
                    .then_inc(w_in[t], 16)

            load(0, Q)
            sp.dma_start(bo[:], ins["bo"].partition_broadcast(P)).then_inc(bo_in, 16)
            for n in core.cols:
                sp.dma_start(core.cols[n][:], ins[n]).then_inc(core.cols_in, 16)
            load(0, K)

            def body(g):
                for t in (Q, K, V):
                    if t == Q:
                        load(g, V)
                    elif not is_last(g):
                        load(g + 1, t - 1)
                    elif t == V:
                        for i in range(4):
                            sp.wait_ge(stored[i], 6 * 16)
                        sp.dma_start(core.k_raw[:], scratch["k"][0]).then_inc(k_in, 16)
                        sp.dma_start(core.q_raw[:], scratch["q"][0]).then_inc(q_in, 16)
                    for u in range(UNITS):
                        sp.wait_ge(res_done, g * 24 + t * UNITS + u + 1)
                        if t == V:
                            dst = scratch["v"][bass.ds(g * GROUP, GROUP), :, u, :].rearrange("h p d -> p h d")
                            src = res[u % 4][:].rearrange("p (h d) -> p h d", h=GROUP)
                        else:
                            dst = scratch["qk"[t]][bass.ds(g * GROUP + u // 2, 1), :,
                                                   (u % 2) * HALF:(u % 2 + 1) * HALF]\
                                .rearrange("a p n -> p (a n)")
                            src = res[u % 4][:]
                        sp.dma_start(dst, src).then_inc(stored[u % 4], 16)

            groups(sp, body)
            for i in range(4):
                sp.wait_ge(stored[i], NGROUPS * 6 * 16)
            sp.wait_ge(q_in, 16)

        @block.scalar
        def _(act):
            def split(n, t, g):
                act.wait_ge(w_in[t], (g + 1) * 16)
                wait(act, proj_done, (n - 2) * UNITS)
                nc.scalar.activation(w_hi[t][:], w[t][:], ACT.Copy).then_inc(w_hi_done, 1)

            split(0, Q, 0)

            def body(g):
                for t in (Q, K, V):
                    n = g * 3 + t
                    if t < V:
                        split(n + 1, t + 1, g)
                    elif not is_last(g):
                        split(n + 1, Q, g + 1)
                    for u in range(UNITS):
                        if t == V:
                            continue
                        m = g * 16 + t * UNITS + u
                        act.wait_ge(res_done, n * UNITS + u + 1)
                        wait(act, acc_done, m + 2 - 1)
                        nc.scalar.activation(sq[:, u % 2, :], res[u % 4][:], ACT.Square).then_inc(sq_done, 1)

            groups(act, body)
            act.wait_ge(ms_done, 1)
            nc.scalar.activation(sd[:], ms[:], ACT.Sqrt).then_inc(sd_done, 1)

        @block.vector
        def _(v):
            def split(n, t):
                v.wait_ge(w_hi_done, n + 1)
                nc.vector.tensor_tensor(w_lo[t][:], w[t][:], w_hi[t][:], ALU.subtract).then_inc(w_lo_done, 1)

            def factors():
                v.wait_ge(sums_done, 1)
                nc.vector.tensor_scalar(ms[:], core.bank(6)[:, 0:2 * NT].rearrange("p (a t) -> p a t", a=2),
                                        1.0 / INNER, RMS_EPS, ALU.mult, ALU.add).then_inc(ms_done, 1)
                v.wait_ge(sd_done, 1)
                nc.vector.reciprocal(r0[:], sd[:]).then_inc(rs_done, 1)
                v.wait_ge(rs_done, 1)
                nc.vector.tensor_tensor(corr[:], ms[:], r0[:], ALU.mult).then_inc(rs_done, 1)
                v.wait_ge(rs_done, 2)
                nc.vector.tensor_tensor(corr[:], corr[:], r0[:], ALU.mult).then_inc(rs_done, 1)
                v.wait_ge(rs_done, 3)
                nc.vector.tensor_scalar(corr[:], corr[:], -0.5, 1.5, ALU.mult, ALU.add).then_inc(rs_done, 1)
                v.wait_ge(rs_done, 4)
                nc.vector.tensor_tensor(rs[:], r0[:], corr[:], ALU.mult).then_inc(rs_done, 1)
                v.wait_ge(rs_done, 5)
                nc.vector.tensor_scalar(core.rms[:, TOK:TOK + NT], rs[:, 0, :], float(HD) ** -0.5, None,
                                        ALU.mult).then_inc(rms_done, 1)
                nc.vector.tensor_tensor(diag[:], core.ident[:].unsqueeze(1).broadcast_to([P, NT, P]),
                                        rs[:, 1, :].unsqueeze(2).broadcast_to([P, NT, P]), ALU.mult)\
                    .then_inc(diag_done, 1)

            split(0, Q)
            v.wait_ge(core.cols_in, 16 * len(core.cols))

            def body(g):
                for t in (Q, K, V):
                    n = g * 3 + t
                    if t < V or not is_last(g):
                        split(n + 1, (t + 1) % 3)
                    for u in range(UNITS):
                        v.wait_ge(proj_done, n * UNITS + u + 1)
                        wait(v, stored[u % 4], (g * 6 + t * 2 + u // 4) * 16)
                        wait(v, sq_done, g * 16 + max(min(t * UNITS + u - 3, 16), 0))
                        if t == V:
                            nc.vector.tensor_copy(res[u % 4][:], core.bank(u % 4)).then_inc(res_done, 1)
                        else:
                            nc.vector.tensor_scalar(res[u % 4][:], core.bank(u % 4),
                                                    bias[t][:, bass.ds(g * GROUP + u // 2, 1)], None, ALU.add)\
                                .then_inc(res_done, 1)
                        if is_last(g) and t == V and u == AT_SUMS + 1:
                            factors()
                        if is_last(g) and t == V and u == AT_SPREAD + 1:
                            v.wait_ge(spread_done, 1)
                            nc.vector.tensor_copy(core.rms[:, 0:TOK], core.ps[2][:]).then_inc(rms_done, 1)

            groups(v, body)
            v.wait_ge(k_in, 16)
            v.wait_ge(rms_done, 2)
            nc.vector.scalar_tensor_tensor(out=core.kn[:], in0=core.k_raw[:], scalar=core.cols["gk"][:, 0:1],
                                           in1=core.rms[:, 0:TOK], op0=ALU.mult, op1=ALU.mult)

        @block.gpsimd
        def _(pool):
            nc.gpsimd.memset(ones[:], 1.0)
            for t in (Q, K):
                nc.gpsimd.memset(acc[t][:], 0.0).then_inc(acc_done, 1)
            pool.wait_ge(acc_done, 2)
            pool.wait_ge(bo_in, 16)
            for t in range(NT):
                nc.gpsimd.tensor_tensor(core.x[:, t, :], core.x[:, t, :], bo[:], ALU.add)

            def body(g):
                for t in (Q, K):
                    for u in range(UNITS):
                        m = g * 16 + t * UNITS + u
                        pool.wait_ge(sq_done, m + 1)
                        pool.wait_ge(acc_done, m + 2)
                        part = acc[t][:, (u % 2) * HALF:(u % 2 + 1) * HALF]
                        nc.gpsimd.tensor_tensor(part, part, sq[:, u % 2, :], ALU.add).then_inc(acc_done, 1)

            groups(pool, body)

        @block.tensor
        def _(pe):
            def sums():
                pe.wait_ge(acc_done, 2 + NGROUPS * 16)
                for a in (Q, K):
                    for t in range(NT):
                        last = nc.tensor.matmul(core.bank(6)[:, a * NT + t:a * NT + t + 1],
                                                acc[a][:, t * P:(t + 1) * P], ones[:, 0:1], start=True, stop=True)
                last.then_inc(sums_done, 1)

            def spread():
                pe.wait_ge(diag_done, 1)
                for th in range(NH):
                    last = nc.tensor.matmul(core.bank(4 + th), ones[:], diag[:, 4 * th:4 * th + 4, :],
                                            start=True, stop=True)
                last.then_inc(spread_done, 1)

            def body(g):
                for t in (Q, K, V):
                    n = g * 3 + t
                    start = isinstance(g, int) and g == 0 and t == Q
                    if not start:
                        pe.wait_ge(w_lo_done, n + 1)
                    for u in range(UNITS):
                        if start and u == FIRST * NH:
                            pe.wait_ge(w_lo_done, 1)
                        wait(pe, res_done, n * UNITS + u - 3)
                        if t == V:
                            s = slice(u * P, (u + 1) * P)
                            pairs = [((xT.hi[:, k, s], xT.lo[:, k, s]), (w_hi[t][:, k, :], w_lo[t][:, k, :]))
                                     for k in range(KB)]
                        else:
                            c = slice(u // 2 * HD, (u // 2 + 1) * HD)
                            s = slice((u % 2) * HALF, (u % 2 + 1) * HALF)
                            pairs = [((w_hi[t][:, k, c], w_lo[t][:, k, c]) if not start or u >= FIRST * NH
                                      else core.first.parts((k * FIRST + u // NH) * HD),
                                      (xT.hi[:, k, s], xT.lo[:, k, s])) for k in range(KB)]
                        product(nc, core.bank(u % 4), pairs).then_inc(proj_done, 1)
                        if is_last(g) and t == V and u == AT_SUMS:
                            sums()
                        if is_last(g) and t == V and u == AT_SPREAD:
                            spread()

            groups(pe, body)


def attention_block(core, ins, scratch, following):
    nc = core.nc
    x = core.x
    T_LAG, PV_LAG, OUT_LAG, WO_LAG = 2, 6, 10, 12
    BODY = 2 * NT
    STEPS = HEADS * NT
    with ExitStack() as ctx:
        def sb(name, shape, dt=F32):
            return ctx.enter_context(nc.sbuf_tensor(f"at_{name}", shape, dt))

        def sem(name):
            return core.semaphore(ctx, f"at_{name}")

        def pair(name, shape):
            return [(sb(f"{name}{i}_hi", shape, F32R), sb(f"{name}{i}_lo", shape, F32R)) for i in range(2)]

        k_raw, q_raw, v_raw = core.k_raw, core.q_raw, sb("v_raw", [P, NT, HD])
        o_raw = sb("o_raw", [P, DM])
        kn = core.kn
        k2, q2 = ([(xT[:, 2 * i, :], xT[:, 2 * i + 1, :]) for i in range(2)] for xT in (core.ln.hi, core.ln.lo))
        v2 = pair("v", [P, NT, HD])
        o2 = pair("o", [P, DM])
        pT2 = pair("pT", [P, NT, HALF])
        y2 = pair("y", [P, HALF])
        y = sb("y", [P, HALF])
        probs = [sb(f"probs{i}", [P, TOK]) for i in range(4)]
        maxes, nbias, sums, rsums = (sb(n, [P, 4]) for n in ("maxes", "nbias", "sums", "rsums"))
        k_in, q_in, v_in, o_in = (sem(f"{n}_in") for n in ("k", "q", "v", "o"))
        kn_done = sem("kn_done")
        k_hi, k_lo, q_hi, q_lo, v_hi, v_lo, o_hi, o_lo = (
            sem(f"{n}_done") for n in ("k_hi", "k_lo", "q_hi", "q_lo", "v_hi", "v_lo", "o_hi", "o_lo"))
        s_scores, s_max, s_bias, s_exp, s_rsum, s_norm = (
            sem(n) for n in ("scores_done", "max_done", "bias_done", "exp_done", "rsum_done", "norm_done"))
        s_T, s_pT_hi, s_pT_lo = sem("transposed"), sem("pT_hi_done"), sem("pT_lo_done")
        s_pv, s_y, s_y_hi, s_y_lo = sem("pv_done"), sem("y_done"), sem("y_hi_done"), sem("y_lo_done")
        s_wo, s_added = sem("wo_done"), sem("added")
        ln = LayerNorm(core, ctx, "at", (0, 1))
        prefetch = Prefetch(core, ctx, "at", following)
        block = core.open_block(ctx)
        rk, rq = core.rms[:, 0:TOK], core.rms[:, TOK:TOK + NT]
        gq, gk, bv = core.cols["gq"], core.cols["gk"], core.cols["bv"]
        T_BANKS, PV_BANK, WO_BANK = core.ps[2], 6, 7

        def scores(l):
            return core.ps[l % 2]

        def steps(eng, step, before_loop=None):
            for l in range(BODY):
                step(0, l)
            with eng.Fori(1, STEPS // BODY - 1) as i:
                for l in range(BODY):
                    step(i, l)
            for l in range(BODY):
                step(STEPS // BODY - 1, l)
            for l in range(WO_LAG):
                step(STEPS // BODY, l)

        def exists(i, l, lag=0):
            return not isinstance(i, int) or 0 <= BODY * i + l - lag < STEPS

        def final(i, l):
            k = BODY * i + l - WO_LAG - (HEADS - 1) * NT if isinstance(i, int) else -1
            return k if k >= 0 else None

        def lagging(i, l, lag):
            m = (l - lag) % BODY
            return (BODY // 4 * i + (l - lag) // 4), (m // 4) % 2, m // NT, m % 4

        def next_head(i, l):
            h = 2 * i + l // NT + 1
            return h, (l // NT + 1) % 2, not isinstance(h, int) or h < HEADS

        @block.sync
        def _(sp):
            def load(dst, src, h, arrived):
                sp.dma_start(dst, src[bass.ds(h, 1)].rearrange("a p n -> p (a n)")).then_inc(arrived, 16)

            def head(h):
                if not isinstance(h, int) or h >= 1:
                    wait(sp, kn_done, h - 1)
                    load(k_raw[:], scratch["k"], h, k_in)
                    wait(sp, q_lo, h)
                    load(q_raw[:], scratch["q"], h, q_in)
                wait(sp, v_lo, h)
                wait(sp, v_hi, h)
                load(v_raw[:].rearrange("p t d -> p (t d)"), scratch["v_flat"], h, v_in)
                wait(sp, o_lo, h)
                wait(sp, o_hi, h)
                load(o_raw[:], ins["Wo"], h, o_in)

            head(0)
            head(1)
            with sp.Fori(2, HEADS) as h:
                head(h)
            prefetch.load(sp)

        @block.gpsimd
        def _(pool):
            def part_lo(dst, a, b, done, count, arrived):
                pool.wait_ge(arrived, count)
                nc.gpsimd.tensor_tensor(dst, a, b, ALU.subtract).then_inc(done, 1)

            def k_part(h, hp):
                part_lo(k2[hp][1], kn[:], k2[hp][0], k_lo, h + 1, k_hi)

            def v_part(h, hp):
                part_lo(v2[hp][1][:], v_raw[:], v2[hp][0][:], v_lo, h + 1, v_hi)

            k_part(0, 0)

            def step(i, l):
                p = BODY * i + l
                if exists(i, l):
                    pool.wait_ge(s_rsum, p + 1)
                    nc.gpsimd.tensor_tensor(probs[l % 4][:], probs[l % 4][:],
                                            rsums[:, l % 4:l % 4 + 1].broadcast_to([P, TOK]), ALU.mult)\
                        .then_inc(s_norm, 1)
                h, hp, there = next_head(i, l)
                if l % NT == 1 and there:
                    k_part(h, hp)
                if l % NT == 7 and there:
                    v_part(h, hp)
                if l == 0 and isinstance(i, int) and i == 0:
                    v_part(0, 0)
                if l % NT == 5 and exists(i, l):
                    hh, par = 2 * i + l // NT, l // NT
                    part_lo(o2[par][1][:], o_raw[:], o2[par][0][:], o_lo, hh + 1, o_hi)
                if l % 4 == OUT_LAG % 4 and exists(i, l, OUT_LAG):
                    J, jp, _, _ = lagging(i, l, OUT_LAG)
                    part_lo(y2[jp][1][:], y[:], y2[jp][0][:], s_y_lo, J + 1, s_y_hi)
                if final(i, l) is not None:
                    ln.gpsimd(pool, final(i, l))

            steps(pool, step)
            for k in range(NT, ln.STEPS):
                ln.gpsimd(pool, k)
            prefetch.low(pool)

        @block.scalar
        def _(act):
            def k_split(h, hp):
                wait(act, kn_done, h)
                wait(act, s_scores, (h - 1) * NT)
                nc.scalar.activation(k2[hp][0], kn[:], ACT.Copy).then_inc(k_hi, 1)

            def v_part(h, hp):
                act.wait_ge(v_in, (h + 1) * 16)
                wait(act, s_pv, 2 * h - 2)
                nc.scalar.activation(v2[hp][0][:], v_raw[:], ACT.Copy).then_inc(v_hi, 1)

            k_split(0, 0)
            nc.scalar.preload_act_table(ACT.Exp)

            def step(i, l):
                p = BODY * i + l
                if exists(i, l, T_LAG):
                    q = p - T_LAG
                    J, jp, _, w = lagging(i, l, T_LAG)
                    for b in range(2):
                        act.wait_ge(s_T, 2 * q + b + 1)
                        if w == 0 and b == 0:
                            wait(act, s_pv, J - 1)
                        nc.scalar.activation(
                            pT2[jp][0][:, 4 * b:4 * b + 4, w * P:(w + 1) * P],
                            T_BANKS[:, b * HALF:(b + 1) * HALF].rearrange("p (k n) -> p k n", k=4),
                            ACT.Copy).then_inc(s_pT_hi, 1)
                if exists(i, l):
                    act.wait_ge(s_bias, p + 1)
                    wait(act, s_T, 2 * (p - 4) + 2)
                    nc.scalar.activation(probs[l % 4][:], scores(l)[:], ACT.Exp, bias=nbias[:, l % 4:l % 4 + 1],
                                         scale=rq[:, l % NT:l % NT + 1], accum_out=sums[:, l % 4:l % 4 + 1])\
                        .then_inc(s_exp, 1)
                if l % 4 == OUT_LAG % 4 and exists(i, l, OUT_LAG):
                    J, jp, _, _ = lagging(i, l, OUT_LAG)
                    act.wait_ge(s_y, J + 1)
                    wait(act, s_wo, 4 * (J - 1))
                    nc.scalar.activation(y2[jp][0][:], y[:], ACT.Copy).then_inc(s_y_hi, 1)
                h, hp, there = next_head(i, l)
                if l % NT == 1 and there:
                    k_split(h, hp)
                if l % NT == 7 and there:
                    v_part(h, hp)
                if l == 0 and isinstance(i, int) and i == 0:
                    v_part(0, 0)
                if l % NT == 5 and exists(i, l):
                    hh, par = 2 * i + l // NT, l // NT
                    act.wait_ge(o_in, (hh + 1) * 16)
                    wait(act, s_wo, (hh - 1) * NT)
                    nc.scalar.activation(o2[par][0][:], o_raw[:], ACT.Copy).then_inc(o_hi, 1)
                if final(i, l) is not None:
                    ln.scalar(act, final(i, l))

            steps(act, step)
            prefetch.high(act)
            for k in range(NT, ln.STEPS):
                ln.scalar(act, k)

        @block.vector
        def _(v):
            def k_part(h):
                v.wait_ge(k_in, h * 16)
                wait(v, k_lo, h)
                nc.vector.scalar_tensor_tensor(out=kn[:], in0=k_raw[:], scalar=gk[:, bass.ds(h, 1)], in1=rk,
                                               op0=ALU.mult, op1=ALU.mult).then_inc(kn_done, 1)

            def q_high(h, hp):
                wait(v, q_in, h * 16)
                wait(v, s_scores, (h - 1) * NT)
                nc.vector.tensor_scalar(q2[hp][0], q_raw[:], gq[:, bass.ds(h, 1)], None, ALU.mult)\
                    .then_inc(q_hi, 1)

            def q_low(h, hp):
                v.wait_ge(q_hi, h + 1)
                nc.vector.scalar_tensor_tensor(out=q2[hp][1], in0=q_raw[:], scalar=gq[:, bass.ds(h, 1)],
                                               in1=q2[hp][0], op0=ALU.mult, op1=ALU.subtract).then_inc(q_lo, 1)

            q_high(0, 0)
            q_low(0, 0)

            def step(i, l):
                p = BODY * i + l
                if l % 4 == OUT_LAG % 4 and exists(i, l, OUT_LAG):
                    J, _, _, _ = lagging(i, l, OUT_LAG)
                    head = 2 * i + (l - OUT_LAG) // NT
                    v.wait_ge(s_pv, J + 1)
                    wait(v, s_y_lo, J)
                    nc.vector.tensor_scalar(y[:], core.bank(PV_BANK), bv[:, bass.ds(head, 1)], None, ALU.add)\
                        .then_inc(s_y, 1)
                if exists(i, l):
                    v.wait_ge(s_scores, p + 1)
                    nc.vector.reduce_max(maxes[:, l % 4:l % 4 + 1], scores(l)[:], AX.X).then_inc(s_max, 1)
                    v.wait_ge(s_max, p + 1)
                    nc.vector.tensor_scalar(nbias[:, l % 4:l % 4 + 1], maxes[:, l % 4:l % 4 + 1],
                                            rq[:, l % NT:l % NT + 1], -1.0, ALU.mult, ALU.mult).then_inc(s_bias, 1)
                if exists(i, l, T_LAG):
                    q = p - T_LAG
                    _, jp, _, w = lagging(i, l, T_LAG)
                    for b in range(2):
                        v.wait_ge(s_pT_hi, 2 * q + b + 1)
                        out = (slice(None), slice(4 * b, 4 * b + 4), slice(w * P, (w + 1) * P))
                        nc.vector.tensor_tensor(
                            pT2[jp][1][out], T_BANKS[:, b * HALF:(b + 1) * HALF].rearrange("p (k n) -> p k n", k=4),
                            pT2[jp][0][out], ALU.subtract).then_inc(s_pT_lo, 1)
                if exists(i, l):
                    v.wait_ge(s_exp, p + 1)
                    nc.vector.reciprocal(rsums[:, l % 4:l % 4 + 1], sums[:, l % 4:l % 4 + 1]).then_inc(s_rsum, 1)
                if exists(i, l, WO_LAG):
                    _, jp, _, w = lagging(i, l, WO_LAG)
                    tile = jp * 4 + w
                    if final(i, l) is not None:
                        ln.invert(v, final(i, l))
                    v.wait_ge(s_wo, p - WO_LAG + 1)
                    wait(v, s_added, p - WO_LAG)
                    nc.vector.tensor_tensor(x[:, tile, :], core.bank(WO_BANK), x[:, tile, :], ALU.add)\
                        .then_inc(s_added, 1)
                    if final(i, l) is not None:
                        v.wait_ge(s_added, STEPS - NT + final(i, l) + 1)
                        ln.vector(v, final(i, l))
                h, hp, there = next_head(i, l)
                if l % NT == 0 and there:
                    k_part(h)
                if l % NT == 3 and there:
                    q_high(h, hp)
                if l % NT == 4 and there:
                    q_low(h, hp)

            steps(v, step)
            for k in range(NT, ln.STEPS):
                ln.invert(v, k)
                ln.vector(v, k)

        @block.tensor
        def _(pe):
            def step(i, l):
                p = BODY * i + l
                if exists(i, l):
                    qt, hp = l % NT, l // NT
                    if qt == 0:
                        for s in (k_hi, k_lo, q_hi, q_lo):
                            pe.wait_ge(s, 2 * i + hp + 1)
                    wait(pe, s_exp, p - 1)
                    s = slice(qt * P, (qt + 1) * P)
                    for n in range(NH):
                        m = slice(n * HALF, (n + 1) * HALF)
                        last = product(nc, scores(l)[:, m], [((q2[hp][0][:, s], q2[hp][1][:, s]),
                                                              (k2[hp][0][:, m], k2[hp][1][:, m]))])
                    last.then_inc(s_scores, 1)
                if exists(i, l, T_LAG):
                    q = p - T_LAG
                    pe.wait_ge(s_norm, q + 1)
                    for b in range(2):
                        wait(pe, s_pT_lo, 2 * (q - 1) + b + 1)
                        for k in range(4 * b, 4 * b + 4):
                            last = nc.tensor.transpose(T_BANKS[:, k * P:(k + 1) * P],
                                                       probs[(l - T_LAG) % 4][:, k * P:(k + 1) * P], core.ident[:])
                        last.then_inc(s_T, 1)
                if exists(i, l, WO_LAG):
                    J, jp, hp, w = lagging(i, l, WO_LAG)
                    if w == 0:
                        pe.wait_ge(s_y_lo, J + 1)
                        if jp == 0:
                            pe.wait_ge(o_lo, 2 * i + (l - WO_LAG) // NT + 1)
                    wait(pe, s_added, p - WO_LAG)
                    s = slice(w * P, (w + 1) * P)
                    product(nc, core.bank(WO_BANK), [((y2[jp][0][:, s], y2[jp][1][:, s]),
                                                      (o2[hp][0][:], o2[hp][1][:]))]).then_inc(s_wo, 1)
                if exists(i, l, PV_LAG):
                    J, jp, hp, c = lagging(i, l, PV_LAG)
                    if c == 0:
                        pe.wait_ge(s_pT_lo, 8 * J + 8)
                        wait(pe, s_y, J)
                        if jp == 0:
                            pe.wait_ge(v_lo, 2 * i + (l - PV_LAG) // NT + 1)
                    terms = []
                    for k in (2 * c, 2 * c + 1):
                        (vh, vl), (ph, pl) = v2[hp], pT2[jp]
                        terms += [(vh, ph, k), (vh, pl, k), (vl, ph, k)]
                    for n, (a, b, k) in enumerate(terms):
                        last = nc.tensor.matmul(core.bank(PV_BANK), a[:, k, :], b[:, k, :], start=(c == 0 and n == 0),
                                                stop=(c == 3 and n == len(terms) - 1))
                    if c == 3:
                        last.then_inc(s_pv, 1)
                if final(i, l) is not None:
                    pe.wait_ge(s_exp, STEPS)
                    ln.tensor(pe, final(i, l))

            steps(pe, step)
            for k in range(NT, ln.STEPS):
                ln.tensor(pe, k)


class Truncation:

    def __init__(self, core, ctx, tag):
        self.nc = nc = core.nc

        def sb(name):
            return ctx.enter_context(nc.sbuf_tensor(f"{tag}_{name}", [P, 2, HALF], F32))

        def sem(name):
            return core.semaphore(ctx, f"{tag}_{name}")

        self.clipped, self.mag, self.sign, self.near, self.over = (
            sb(n) for n in ("clipped", "magnitude", "sign", "nearest", "over"))
        self.s_clip, self.s_mag, self.s_near, self.s_over, self.s_floor, self.s_out = (
            sem(n) for n in ("clip_done", "magnitude_done", "nearest_done", "over_done", "floor_done", "trunc_done"))

    def clip(self, v, n):
        s = n % 2
        self.nc.vector.tensor_scalar(self.clipped[:, s, :], self.clipped[:, s, :], -QSCALE, QSCALE - 1,
                                     ALU.max, ALU.min).then_inc(self.s_clip, 1)

    def magnitude(self, act, n, scale=1.0):
        s = n % 2
        act.wait_ge(self.s_clip, n + 1)
        wait(act, self.s_out, n - 1)
        self.nc.scalar.activation(self.mag[:, s, :], self.clipped[:, s, :], ACT.Abs, scale=scale)
        self.nc.scalar.activation(self.sign[:, s, :], self.clipped[:, s, :], ACT.Sign).then_inc(self.s_mag, 1)

    def nearest(self, v, n):
        s = n % 2
        v.wait_ge(self.s_mag, n + 1)
        wait(v, self.s_out, n - 1)
        self.nc.vector.tensor_scalar(self.near[:, s, :], self.mag[:, s, :], ROUND, ROUND, ALU.add, ALU.subtract)\
            .then_inc(self.s_near, 1)
        v.wait_ge(self.s_near, n + 1)
        self.nc.vector.tensor_tensor(self.over[:, s, :], self.near[:, s, :], self.mag[:, s, :], ALU.is_gt)\
            .then_inc(self.s_over, 1)

    def signed(self, pool, n, out):
        s = n % 2
        pool.wait_ge(self.s_over, n + 1)
        self.nc.gpsimd.tensor_tensor(self.near[:, s, :], self.near[:, s, :], self.over[:, s, :], ALU.subtract)\
            .then_inc(self.s_floor, 1)
        pool.wait_ge(self.s_floor, n + 1)
        self.nc.gpsimd.tensor_tensor(out, self.near[:, s, :], self.sign[:, s, :], ALU.mult).then_inc(self.s_out, 1)


def ffn1_block(core, ins, tag, following=None, out=None):
    nc = core.nc
    x, xT = core.x, core.ln
    with ExitStack() as ctx:
        def sb(name, shape, dt=F32):
            return ctx.enter_context(nc.sbuf_tensor(f"{tag}_{name}", shape, dt))

        def sem(name):
            return core.semaphore(ctx, f"{tag}_{name}")

        ln = LayerNorm(core, ctx, tag, (0, 1)) if out is None else None
        prefetch = Prefetch(core, ctx, tag, following) if out is None else None
        tr = Truncation(core, ctx, tag)
        w = [core.first, Chunk(nc, ctx, f"{tag}_w")]
        wd = [sb(f"wd{i}", [P, DM]) for i in range(2)]
        wd_hi, wd_lo = sb("wd_hi", [P, IB, DM], F32R), sb("wd_lo", [P, IB, DM], F32R)
        sig = sb("sig", [P, 2, HALF])
        silu = sb("silu", [P, 2, HALF])
        inter = sb("inter", [P, IB, TOK], F32R)
        q8 = sb("q8", [P, 2, HALF])
        w_in = [sem(f"w_in{i}") for i in range(2)]
        wd_in = [sem(f"wd_in{i}") for i in range(2)]
        w_hi_done, w_lo_done, wd_hi_done, wd_lo_done = (
            sem(n) for n in ("w_hi_done", "w_lo_done", "wd_hi_done", "wd_lo_done"))
        up_done, sig_done, silu_done, prod_done = (
            sem(n) for n in ("up_done", "sig_done", "silu_done", "prod_done"))
        down_done, added, stored = sem("down_done"), sem("added"), sem("stored")
        block = core.open_block(ctx)
        UP_UNITS = IB * NH
        LN_LAG = 2
        AFTER = LN_LAG + (ln.STEPS - NT if ln else 0)

        @block.sync
        def _(sp):
            for b in range(IB):
                if b >= 1:
                    wait(sp, w_lo_done, b - 2)
                    sp.dma_start(w[b % 2].raw[:], ins["wgu"][b]).then_inc(w_in[b % 2], 16)
                wait(sp, wd_lo_done, b - 1)
                sp.dma_start(wd[b % 2][:], ins["wdT"][b]).then_inc(wd_in[b % 2], 16)
            if out is None:
                sp.wait_ge(up_done, UP_UNITS)
                prefetch.load(sp)
            else:
                for t in range(NT):
                    sp.wait_ge(added, t + 1)
                    sp.dma_start(out[t * P:(t + 1) * P, :], x[:, t, :]).then_inc(stored, 16)
                sp.wait_ge(stored, 16 * NT)

        @block.gpsimd
        def _(pool):
            for b in range(IB):
                pool.wait_ge(wd_hi_done, b + 1)
                nc.gpsimd.tensor_tensor(wd_lo[:, b, :], wd[b % 2][:], wd_hi[:, b, :], ALU.subtract)\
                    .then_inc(wd_lo_done, 1)
                for th in range(NH):
                    tr.signed(pool, NH * b + th, inter[:, b, th * HALF:(th + 1) * HALF])
            for k in range(NT + AFTER):
                if k - 1 in range(NT):
                    wait(pool, added, k - 2)
                    tr.signed(pool, UP_UNITS + k - 1, q8[:, (k - 1) % 2, :])
                if k == 2 and ln:
                    prefetch.low(pool)
                if ln and k >= LN_LAG:
                    ln.gpsimd(pool, k - LN_LAG)

        @block.scalar
        def _(act):
            def w_split(b):
                act.wait_ge(w_in[b % 2], 16 * ((b + 1) // 2))
                wait(act, up_done, NH * (b - 1))
                nc.scalar.activation(w[b % 2].hi[:], w[b % 2].raw[:], ACT.Copy).then_inc(w_hi_done, 1)

            for n in range(UP_UNITS + 1):
                if n < UP_UNITS:
                    b, th = n // NH, n % NH
                    if th == 0:
                        if b + 1 < IB:
                            w_split(b + 1)
                        act.wait_ge(wd_in[b % 2], 16 * (b // 2 + 1))
                        nc.scalar.activation(wd_hi[:, b, :], wd[b % 2][:], ACT.Copy).then_inc(wd_hi_done, 1)
                    act.wait_ge(up_done, n + 1)
                    wait(act, silu_done, n - 1)
                    nc.scalar.activation(sig[:, n % 2, :], core.bank(2 * (n % 3)), ACT.Sigmoid, scale=1.0 / QSCALE)\
                        .then_inc(sig_done, 1)
                if n >= 1:
                    tr.magnitude(act, n - 1)
            if out is None:
                prefetch.high(act)
            for k in range(NT + AFTER):
                if k < NT:
                    tr.magnitude(act, UP_UNITS + k, scale=QSCALE)
                if ln and k >= LN_LAG:
                    ln.scalar(act, k - LN_LAG)

        @block.vector
        def _(v):
            def w_split(b):
                v.wait_ge(w_hi_done, b)
                nc.vector.tensor_tensor(w[b % 2].lo[:], w[b % 2].raw[:], w[b % 2].hi[:], ALU.subtract)\
                    .then_inc(w_lo_done, 1)

            for n in range(UP_UNITS + 1):
                if n < UP_UNITS:
                    b, th = n // NH, n % NH
                    if th == 0 and b + 1 < IB:
                        w_split(b + 1)
                    v.wait_ge(sig_done, n + 1)
                    nc.vector.scalar_tensor_tensor(out=silu[:, n % 2, :], in0=core.bank(2 * (n % 3)),
                                                   scalar=1.0 / QSCALE, in1=sig[:, n % 2, :],
                                                   op0=ALU.mult, op1=ALU.mult).then_inc(silu_done, 1)
                    v.wait_ge(silu_done, n + 1)
                    wait(v, tr.s_mag, n - 1)
                    nc.vector.tensor_tensor(tr.clipped[:, n % 2, :], core.bank(2 * (n % 3) + 1),
                                            silu[:, n % 2, :], ALU.mult).then_inc(prod_done, 1)
                    v.wait_ge(prod_done, n + 1)
                    tr.clip(v, n)
                if n >= 1:
                    tr.nearest(v, n - 1)

            def add(t):
                v.wait_ge(tr.s_out, UP_UNITS + t + 1)
                nc.vector.scalar_tensor_tensor(out=x[:, t, :], in0=q8[:, t % 2, :], scalar=0.5, in1=x[:, t, :],
                                               op0=ALU.mult, op1=ALU.add).then_inc(added, 1)

            for k in range(NT + AFTER):
                if k < NT:
                    v.wait_ge(down_done, k + 1)
                    wait(v, tr.s_mag, UP_UNITS + k - 1)
                    nc.vector.tensor_scalar(tr.clipped[:, k % 2, :], core.bank(6 + k % 2), -1.0,
                                            (QSCALE - 1) / QSCALE, ALU.max, ALU.min).then_inc(tr.s_clip, 1)
                if ln and k >= LN_LAG:
                    ln.invert(v, k - LN_LAG)
                if k - 1 in range(NT):
                    tr.nearest(v, UP_UNITS + k - 1)
                if k - LN_LAG in range(NT):
                    add(k - LN_LAG)
                    v.wait_ge(added, k - LN_LAG + 1)
                if ln and k >= LN_LAG:
                    ln.vector(v, k - LN_LAG)

        @block.tensor
        def _(pe):
            for n in range(UP_UNITS):
                b, th = n // NH, n % NH
                s = slice(th * HALF, (th + 1) * HALF)
                wait(pe, w_lo_done, b)
                wait(pe, prod_done, n - 2)
                for part in range(2):
                    last = product(nc, core.bank(2 * (n % 3) + part), [
                        (w[b % 2].parts((part * KB + k) * P), (xT.hi[:, k, s], xT.lo[:, k, s]))
                        for k in range(KB)])
                last.then_inc(up_done, 1)
            pe.wait_ge(wd_lo_done, IB)
            for k in range(NT + AFTER):
                if k < NT:
                    down = [((inter[:, b, k * P:(k + 1) * P], None), (wd_hi[:, b, :], wd_lo[:, b, :]))
                            for b in range(IB)]
                    th = k * P // HALF
                    wait(pe, tr.s_clip, UP_UNITS + k - 1)
                    pe.wait_ge(tr.s_out, NH * (IB - 2) + th + 1)
                    product(nc, core.bank(6 + k % 2), down[:-1], stop=False)
                    pe.wait_ge(tr.s_out, NH * (IB - 1) + th + 1)
                    product(nc, core.bank(6 + k % 2), down[-1:], start=False).then_inc(down_done, 1)
                if ln and k >= LN_LAG:
                    ln.tensor(pe, k - LN_LAG)


def retrieval_block(core, ins, following):
    nc = core.nc
    x, xT = core.x, core.ln
    with ExitStack() as ctx:
        def sb(name, shape, dt=F32):
            return ctx.enter_context(nc.sbuf_tensor(f"rt_{name}", shape, dt))

        def sem(name):
            return core.semaphore(ctx, f"rt_{name}")

        ln = LayerNorm(core, ctx, "rt", (6, 7))
        prefetch = Prefetch(core, ctx, "rt", following)
        RING = 3
        TH = NT // NH
        w = [core.first] + [Chunk(nc, ctx, f"rt_w{i}", HEADW, raw=i == 1) for i in range(1, RING)]
        raws = [w[0].raw, w[1].raw]
        bq = sb("bq", [P, KVH])
        WO_RING = 3
        wo = [sb(f"wo{i}", [P, 2, DM]) for i in range(WO_RING)]
        wo_sum = sb("wo_sum", [P, DM])
        wo_hi, wo_lo = sb("wo_hi", [P, KVH, DM], F32R), sb("wo_lo", [P, KVH, DM], F32R)
        sig, r = sb("sig", [P, 2, HALF]), sb("r", [P, 2, HALF])
        ret = sb("ret", [P, 2, TH, HD])
        den, rden = sb("den", [P, 2, TH]), sb("rden", [P, 2, TH])
        sig_hi, sig_lo = sb("sig_hi", [P, 2, HALF], F32R), sb("sig_lo", [P, 2, HALF], F32R)
        ret_hi, ret_lo = sb("ret_hi", [P, KVH, TOK], F32R), sb("ret_lo", [P, KVH, TOK], F32R)
        w_in = [sem(f"w_in{i}") for i in range(2)]
        bq_in, wo_in = sem("bq_in"), [sem(f"wo_in{i}") for i in range(WO_RING)]
        w_hi_done, w_lo_done = sem("w_hi_done"), sem("w_lo_done")
        wo_pairs, wo_summed, wo_hi_done, wo_lo_done = (
            sem(n) for n in ("wo_pairs", "wo_summed", "wo_hi_done", "wo_lo_done"))
        q_done, neg_done, er_done, sig_done, sig_hi_done, sig_lo_done = (
            sem(n) for n in ("q_done", "neg_done", "er_done", "sig_done", "sig_hi_done", "sig_lo_done"))
        nd_done, den_done, rden_done, ret_done, ret_T, ret_hi_done, ret_lo_done = (
            sem(n) for n in ("nd_done", "den_done", "rden_done", "ret_done", "ret_transposed", "ret_hi_done",
                             "ret_lo_done"))
        y_done, added = sem("y_done"), sem("added")
        block = core.open_block(ctx)
        UNITS = KVH * NH
        LAG = 2
        def tok(n):
            return slice(n % NH * HALF, (n % NH + 1) * HALF)

        def nd_bank(m, pair):
            return core.bank(2 + 2 * (m % 2) + pair).rearrange("p (t n) -> p t n", t=2)

        @block.sync
        def _(sp):
            sp.dma_start(w[1].raw[:], ins["heads"][1]).then_inc(w_in[1], 16)
            sp.dma_start(bq[:], ins["bq1T"]).then_inc(bq_in, 16)
            for h in range(KVH):
                for p in (2 * h, 2 * h + 1):
                    wait(sp, wo_summed, (p - WO_RING) // 2 + 1)
                    sp.dma_start(wo[p % WO_RING][:], ins["wo1T"][h, p % 2 * 2:p % 2 * 2 + 2]
                                 .rearrange("g e n -> e g n")).then_inc(wo_in[p % WO_RING], 16)
                if h + 2 < KVH:
                    wait(sp, w_lo_done, h)
                    sp.dma_start(raws[h % 2][:, :HEADW], ins["heads"][h + 2]).then_inc(w_in[h % 2], 16)
            sp.wait_ge(nd_done, NH * (KVH - 1))
            prefetch.load(sp)

        @block.gpsimd
        def _(pool):
            def w_low(h):
                i, raw = h % RING, raws[h % 2]
                pool.wait_ge(w_hi_done, h)
                nc.gpsimd.tensor_tensor(w[i].lo[:, :HEADW], raw[:, :HEADW], w[i].hi[:, :HEADW], ALU.subtract)\
                    .then_inc(w_lo_done, 1)

            w_low(1)
            for n in range(UNITS):
                h, th = n // NH, n % NH
                pool.wait_ge(sig_hi_done, n + 1)
                nc.gpsimd.tensor_tensor(sig_lo[:, n % 2, :], sig[:, n % 2, :], sig_hi[:, n % 2, :], ALU.subtract)\
                    .then_inc(sig_lo_done, 1)
                two = wo[n % WO_RING]
                pool.wait_ge(wo_in[n % WO_RING], 16 * (n // WO_RING + 1))
                nc.gpsimd.tensor_tensor(two[:, 0, :], two[:, 0, :], two[:, 1, :], ALU.add).then_inc(wo_pairs, 1)
                if th == 1 and h + 2 < KVH:
                    w_low(h + 2)
            prefetch.low(pool)
            for k in range(ln.STEPS):
                ln.gpsimd(pool, k)

        @block.scalar
        def _(act):
            def w_split(h):
                act.wait_ge(w_in[h % 2], 16 * ((h + 1) // 2))
                wait(act, nd_done, NH * (h + 1 - RING))
                nc.scalar.activation(w[h % RING].hi[:, :HEADW], raws[h % 2][:, :HEADW], ACT.Copy)\
                    .then_inc(w_hi_done, 1)

            w_split(1)
            act.wait_ge(bq_in, 16)
            for n in range(UNITS + LAG + 1):
                if n < UNITS:
                    h, th = n // NH, n % NH
                    act.wait_ge(neg_done, n + 1)
                    nc.scalar.activation(sig[:, n % 2, :], sig[:, n % 2, :], ACT.Exp)
                    wait(act, sig_done, n - 1)
                    nc.scalar.activation(r[:, n % 2, :], core.bank(n % 2), ACT.Relu, bias=bq[:, h:h + 1])\
                        .then_inc(er_done, 1)
                m = n - LAG - 1
                if m >= 0:
                    act.wait_ge(ret_T, m + 1)
                    nc.scalar.activation(ret_hi[:, m // NH, tok(m)], core.bank(6 + m % 2), ACT.Copy)\
                        .then_inc(ret_hi_done, 1)
                if n < UNITS:
                    act.wait_ge(sig_done, n + 1)
                    wait(act, nd_done, n - 1)
                    nc.scalar.activation(sig_hi[:, n % 2, :], sig[:, n % 2, :], ACT.Copy).then_inc(sig_hi_done, 1)
                if n % NH == 1 and n > 1:
                    act.wait_ge(wo_summed, n // NH)
                    nc.scalar.activation(wo_hi[:, n // NH - 1, :], wo_sum[:], ACT.Copy).then_inc(wo_hi_done, 1)
                if n % NH == 1 and n // NH + 2 < KVH:
                    w_split(n // NH + 2)
            prefetch.high(act)
            for k in range(ln.STEPS):
                ln.scalar(act, k)

        @block.vector
        def _(v):
            v.wait_ge(bq_in, 16)
            for n in range(UNITS + LAG + 1):
                h, th = n // NH, n % NH
                if n < UNITS:
                    v.wait_ge(q_done, n + 1)
                    wait(v, sig_lo_done, n - 1)
                    nc.vector.tensor_scalar(sig[:, n % 2, :], core.bank(n % 2), bq[:, h:h + 1], 0.0,
                                            ALU.add, ALU.min).then_inc(neg_done, 1)
                m = n - LAG
                if 0 <= m < UNITS:
                    v.wait_ge(nd_done, m + 1)
                    for pair in range(2):
                        nc.vector.tensor_scalar_add(den[:, m % 2, 2 * pair:2 * pair + 2], nd_bank(m, pair)[:, :, HD],
                                                    RET_EPS).then_inc(den_done, 1)
                    v.wait_ge(den_done, 2 * m + 2)
                    nc.vector.reciprocal(rden[:, m % 2, :], den[:, m % 2, :]).then_inc(rden_done, 1)
                    v.wait_ge(rden_done, m + 1)
                    wait(v, ret_T, m - 1)
                    for pair in range(2):
                        two = slice(2 * pair, 2 * pair + 2)
                        nc.vector.tensor_tensor(ret[:, m % 2, two, :], nd_bank(m, pair)[:, :, 0:HD],
                                                rden[:, m % 2, two].unsqueeze(2).broadcast_to([P, 2, HD]), ALU.mult)\
                            .then_inc(ret_done, 1)
                if n < UNITS:
                    v.wait_ge(er_done, n + 1)
                    nc.vector.tensor_tensor(sig[:, n % 2, :], sig[:, n % 2, :], r[:, n % 2, :], ALU.add)\
                        .then_inc(sig_done, 1)
                m = n - LAG - 1
                if m >= 0:
                    v.wait_ge(ret_hi_done, m + 1)
                    nc.vector.tensor_tensor(ret_lo[:, m // NH, tok(m)], core.bank(6 + m % 2),
                                            ret_hi[:, m // NH, tok(m)], ALU.subtract).then_inc(ret_lo_done, 1)
                if th == 1 and 1 <= h <= KVH:
                    v.wait_ge(wo_hi_done, h)
                    nc.vector.tensor_tensor(wo_lo[:, h - 1, :], wo_sum[:], wo_hi[:, h - 1, :], ALU.subtract)\
                        .then_inc(wo_lo_done, 1)
                if th == 0 and 1 <= h <= KVH:
                    v.wait_ge(wo_pairs, NH * h)
                    wait(v, wo_lo_done, h - 1)
                    a, b = (wo[(n - NH + i) % WO_RING][:, 0, :] for i in range(2))
                    nc.vector.tensor_tensor(wo_sum[:], a, b, ALU.add).then_inc(wo_summed, 1)
            for k in range(ln.STEPS):
                ln.invert(v, k)
                if k < NT:
                    v.wait_ge(y_done, k + 1)
                    nc.vector.tensor_tensor(x[:, k, :], core.bank(k % 2), x[:, k, :], ALU.add)\
                        .then_inc(added, 1)
                    v.wait_ge(added, k + 1)
                ln.vector(v, k)

        @block.tensor
        def _(pe):
            def project(t, heads):
                s = slice(t * P, (t + 1) * P)
                return product(nc, core.bank(t % 2), [
                    ((ret_hi[:, h, s], ret_lo[:, h, s]), (wo_hi[:, h, :], wo_lo[:, h, :])) for h in heads],
                    start=heads[0] == 0, stop=heads[-1] == KVH - 1)

            def num_den(m):
                pe.wait_ge(sig_lo_done, m + 1)
                wait(pe, ret_done, 2 * (m - 1))
                for t in range(TH):
                    s = slice(t * P, (t + 1) * P)
                    last = product(nc, nd_bank(m, t // 2)[:, t % 2, 0:MZ], [
                        ((sig_hi[:, m % 2, s], sig_lo[:, m % 2, s]), w[m // NH % RING].parts(KB * HD, MZ))])
                last.then_inc(nd_done, 1)

            def back(m):
                pe.wait_ge(ret_done, 2 * m + 2)
                wait(pe, ret_lo_done, m - 1)
                for t in range(TH):
                    last = nc.tensor.transpose(core.bank(6 + m % 2)[:, t * P:(t + 1) * P], ret[:, m % 2, t, :],
                                               core.ident[:])
                last.then_inc(ret_T, 1)

            for n in range(UNITS):
                wait(pe, w_lo_done, n // NH)
                wait(pe, er_done, n - 1)
                product(nc, core.bank(n % 2), [
                    (w[n // NH % RING].parts(k * HD), (xT.hi[:, k, tok(n)], xT.lo[:, k, tok(n)]))
                    for k in range(KB)]).then_inc(q_done, 1)
                if n >= LAG:
                    num_den(n - LAG)
                if n >= LAG + 1:
                    back(n - LAG - 1)
            ready, rest = list(range(KVH - 2)), [KVH - 2, KVH - 1]
            pe.wait_ge(wo_lo_done, KVH - 2)
            pe.wait_ge(ret_lo_done, NH * (KVH - 2))
            pe.wait_ge(er_done, UNITS)
            project(0, ready)
            num_den(UNITS - 2)
            back(UNITS - 3)
            project(1, ready)
            num_den(UNITS - 1)
            back(UNITS - 2)
            pe.wait_ge(wo_lo_done, KVH)
            for k in range(ln.STEPS):
                if k < NT:
                    pe.wait_ge(ret_lo_done, UNITS - NH + k * P // HALF + 1)
                    wait(pe, added, k - 1)
                    project(k, rest if k < 2 else ready + rest).then_inc(y_done, 1)
                if k == 0:
                    back(UNITS - 1)
                ln.tensor(pe, k)


def macaron(nc, ins, out):
    scratch = {n: nc.dram_tensor(f"scratch_{n}", [HEADS, P, TOK], F32).ap() for n in "qk"}
    v = nc.dram_tensor("scratch_v", [HEADS, P, NT, HD], F32).ap()
    scratch["v"] = v
    scratch["v_flat"] = v.rearrange("h p t d -> h p (t d)")
    with ExitStack() as ctx:
        core = Core(nc, ctx)
        wq_first = ins["Wq_first"].rearrange("p k n -> p (k n)")
        setup_block(core, ins, following=ins["w12"][0])
        ffn0_block(core, ins, "f0a", following=wq_first)
        with ExitStack() as attention:
            core.open_attention(attention)
            qkv_block(core, ins, scratch)
            attention_block(core, ins, scratch, following=ins["w12"][0])
        ffn0_block(core, ins, "f0b", following=ins["wgu"][0])
        ffn1_block(core, ins, "f1a", following=ins["heads"][0])
        retrieval_block(core, ins, following=ins["wgu"][0])
        ffn1_block(core, ins, "f1b", out=out)


def kernel(**inputs):
    import numpy as np
    import concourse.bacc as bacc
    from concourse.bass_utils import run_bass_kernel_spmd

    a = {n: np.asarray(v) for n, v in inputs.items()}
    c = np.ascontiguousarray

    def blocks(w, n=P):
        return c(w.reshape(-1, n, w.shape[1]).transpose(1, 0, 2))

    def chunks(w):
        return c(w.reshape(KB, P, -1, HALF).transpose(2, 1, 0, 3))

    def cols(b):
        return c(b.reshape(-1, P).T)

    def padded(w):
        z = np.zeros((IB * P, w.shape[1]), w.dtype)
        z[:w.shape[0]] = w
        return z

    def paired(u, w):
        u, w = (m.reshape(-1, P, KB, P) for m in (u, w))
        return c(np.stack([u, w], axis=1).transpose(0, 4, 1, 3, 2).reshape(-1, P, 2 * KB * P))

    wq1 = a["L1_attn_Wq"].reshape(KVH, REP, HD, KB, P)[:, 0].transpose(0, 3, 2, 1)
    arrays = {
        "x": c(a["L0_attn_hidden_states"].reshape(TOK, DM)),
        "w12": paired(a["L0_ffn_w12"][:M0], a["L0_ffn_w12"][M0:]), "b12T": cols(a["L0_ffn_b12"]),
        "w3T": blocks(a["L0_ffn_w3"].T), "b3": c(a["L0_ffn_b3"]),
        "Wq": chunks(a["L0_attn_Wq"]), "Wk": chunks(a["L0_attn_Wk"]), "Wv": chunks(a["L0_attn_Wv"]),
        "Wq_first": c(blocks(a["L0_attn_Wq"])[:, :, :CHUNK // KB]),
        "Wo": c(a["L0_attn_Wo"].reshape(HEADS, HD, DM)), "bo": c(a["L0_attn_bo"]),
        "bq": cols(a["L0_attn_bq"]), "bk": cols(a["L0_attn_bk"]), "bv": cols(a["L0_attn_bv"]),
        "gq": cols(a["L0_attn_gq"]), "gk": cols(a["L0_attn_gk"]),
        "wgu": paired(padded(a["L1_ffn_w_gate"]), padded(a["L1_ffn_w_up"])),
        "wdT": padded(a["L1_ffn_w_down"].T).reshape(IB, P, DM),
        "heads": c(np.concatenate([wq1.reshape(KVH, P, KB * HD), a["L1_attn_M"],
                                   a["L1_attn_z"][:, :, None], np.zeros((KVH, P, 1), np.float32)], axis=2)),
        "bq1T": cols(a["L1_attn_bq"].reshape(KVH, REP, HD)[:, 0].reshape(-1)),
        "wo1T": c(a["L1_attn_Wo"].T.reshape(KVH, REP, HD, DM)),
    }
    nc = bacc.Bacc("TRN2", target_bir_lowering=False, num_devices=1)
    ins = {n: nc.dram_tensor(f"in_{n}", v.shape, mybir.dt.from_np(v.dtype), kind="ExternalInput").ap()
           for n, v in arrays.items()}
    out = nc.dram_tensor("out_x", (TOK, DM), F32, kind="ExternalOutput").ap()
    macaron(nc, ins, out)
    r = run_bass_kernel_spmd(nc, [{f"in_{n}": v for n, v in arrays.items()}], core_ids=[0])
    return r.results[0]["out_x"].reshape(1, TOK, DM)
```

```python
from contextlib import ExitStack

import concourse.bass as bass
from concourse import mybir

F32 = mybir.dt.float32
F32R = mybir.dt.float32r
ALU = mybir.AluOpType
ACT = mybir.ActivationFunctionType
AX = mybir.AxisListType

P = 128
TOK = 1024
DM = 512
NT = TOK // P
KB = DM // P
HALF = 512
NH = TOK // HALF
CHUNK = 1024
FIRST = CHUNK // DM
FFN1_BANK = 2
LN_EPS = 1e-5
RMS_EPS = 1e-6

HEADS = 32
HD = 128
INNER = HEADS * HD
GROUP = HALF // HD
NGROUPS = HEADS // GROUP

M0 = 512
MB0 = M0 // P

INTER = 1376
IB = (INTER + P - 1) // P
QSCALE = 128.0
ROUND = float(2 ** 23)

KVH = 8
REP = HEADS // KVH
MZ = HD + 2
HEADW = KB * HD + MZ
RET_EPS = 1e-6


def wait(eng, sem, value):
    if isinstance(value, int) and value <= 0:
        return
    eng.wait_ge(sem, value)


class Core:

    def __init__(self, nc, ctx):
        self.nc = nc
        self.sems, self.sem_ctx = [], ExitStack()
        self.past, self.past_ctx = [], ExitStack()
        self.cols_in = ctx.enter_context(nc.semaphore("cols_in"))
        self.x = ctx.enter_context(nc.sbuf_tensor("x", [P, NT, DM], F32))
        self.ident = ctx.enter_context(nc.sbuf_tensor("ident", [P, P], F32))
        self.half = ctx.enter_context(nc.sbuf_tensor("half", [P, 1], F32))
        self.ln = LayerNormBuffers(nc, ctx)
        self.first = Chunk(nc, ctx, "first")
        self.second_raw = ctx.enter_context(nc.sbuf_tensor("second_raw", [P, CHUNK], F32))
        self.ps = [ctx.enter_context(nc.psum_tensor(f"ps{i}", [P, 2 * HALF], F32)) for i in range(4)]

    def open_attention(self, ctx):
        nc = self.nc
        self.rms = ctx.enter_context(nc.sbuf_tensor("rms", [P, TOK + NT], F32))
        self.k_raw, self.q_raw, self.kn = (ctx.enter_context(nc.sbuf_tensor(n, [P, TOK], F32))
                                           for n in ("k_raw", "q_raw", "kn"))
        self.cols = {n: ctx.enter_context(nc.sbuf_tensor(f"col_{n}", [P, HEADS], F32))
                     for n in ("bq", "bk", "bv", "gq", "gk")}

    def semaphore(self, name):
        s = self.sem_ctx.enter_context(self.nc.semaphore(name))
        self.sems.append(s)
        return s

    def open_block(self, ctx):
        nc = self.nc
        nums = sorted(s.num for s in self.past)
        starts = [n for n in nums if n - 1 not in nums]
        ends = [n + 1 for n in nums if n + 1 not in nums]

        def close():
            self.past_ctx.close()
            self.past, self.past_ctx = self.sems, self.sem_ctx
            self.sems, self.sem_ctx = [], ExitStack()

        ctx.callback(close)
        block = ctx.enter_context(nc.Block())

        @block.gpsimd
        def _(pool):
            for a, b in zip(starts, ends):
                nc.gpsimd.sem_clear(range(a, b))

        return block

    def bank(self, b):
        return self.ps[b // 2][:, (b % 2) * HALF:(b % 2 + 1) * HALF]


class Chunk:

    def __init__(self, nc, ctx, name, n=CHUNK, raw=None):
        self.raw = raw or ctx.enter_context(nc.sbuf_tensor(f"{name}_raw", [P, n], F32))
        self.hi = ctx.enter_context(nc.sbuf_tensor(f"{name}_hi", [P, n], F32R))
        self.lo = ctx.enter_context(nc.sbuf_tensor(f"{name}_lo", [P, n], F32R))

    def parts(self, c, n=P):
        return self.hi[:, c:c + n], self.lo[:, c:c + n]


class Prefetch:

    def __init__(self, core, ctx, tag, following):
        self.nc, self.first, self.second_raw = core.nc, core.first, core.second_raw
        self.src, self.second = following[0], following[1] if len(following) > 1 else None
        self.n = self.src.shape[-1]
        self.s_second = core.semaphore(f"{tag}_second_in")
        self.s_in, self.s_hi, self.s_lo = (core.semaphore(f"{tag}_first_{n}") for n in ("in", "hi", "lo"))

    def load(self, sp):
        sp.dma_start(self.first.raw[:, :self.n], self.src).then_inc(self.s_in, 16)
        if self.second is not None:
            sp.dma_start(self.second_raw[:, :self.n], self.second).then_inc(self.s_second, 16)
            sp.wait_ge(self.s_second, 16)

    def high(self, act):
        act.wait_ge(self.s_in, 16)
        self.nc.scalar.activation(self.first.hi[:, :self.n], self.first.raw[:, :self.n], ACT.Copy)\
            .then_inc(self.s_hi, 1)

    def low(self, eng, engine):
        eng.wait_ge(self.s_hi, 1)
        engine.tensor_tensor(self.first.lo[:, :self.n], self.first.raw[:, :self.n],
                                     self.first.hi[:, :self.n], ALU.subtract).then_inc(self.s_lo, 1)


class LayerNormBuffers:

    def __init__(self, nc, ctx):
        def sb(name, shape, dt=F32):
            return ctx.enter_context(nc.sbuf_tensor(f"ln_{name}", shape, dt))

        self.stats = sb("stats", [P, NT, 6])
        self.meanvar = sb("meanvar", [P, NT, 2])
        self.var, self.sd, self.r0, self.corr, self.rstd = (sb(n, [P, NT]) for n in ("var", "sd", "r0", "corr", "rstd"))
        self.xn = sb("xn", [P, 2, DM])
        self.hi = sb("xT_hi", [P, KB, TOK], F32R)
        self.lo = sb("xT_lo", [P, KB, TOK], F32R)


class LayerNorm:
    STEPS = NT + 3

    def __init__(self, core, ctx, tag, banks, prefetch, ahead, ahead_at=NT):
        self.ahead_at = ahead_at
        self.prefetch, self.first_products = prefetch, ahead(core)
        self.core, self.nc, self.banks, b = core, core.nc, banks, core.ln
        self.stats, self.meanvar, self.var, self.sd, self.r0, self.corr, self.rstd, self.xn, self.hi, self.lo = (
            b.stats, b.meanvar, b.var, b.sd, b.r0, b.corr, b.rstd, b.xn, b.hi, b.lo)

        def sem(name):
            return core.semaphore(f"{tag}_ln_{name}")

        self.s_stats, self.s_aggr, self.s_var, self.s_r0, self.s_corr, self.s_rstd = (
            sem(n) for n in ("stats_done", "aggr_done", "var_done", "r0_done", "corr_done", "rstd_done"))
        self.s_sd, self.s_xn, self.s_T = sem("sd_done"), sem("xn_done"), sem("transposed")
        self.s_hi, self.s_lo = sem("hi_done"), sem("lo_done")

    def _psum(self, t):
        return self.core.bank(self.banks[t % 2]).rearrange("p (k n) -> p k n", k=KB)

    def vector_first(self, v, k):
        t = k - 1
        if 0 <= t < NT:
            v.wait_ge(self.s_sd, t + 1)
            self.nc.vector.reciprocal(self.r0[:, t:t + 1], self.sd[:, t:t + 1]).then_inc(self.s_r0, 1)

    def vector(self, v, k):
        self.moments(v, k)
        self.normalise(v, k)

    def moments(self, v, k):
        nc = self.nc
        if k < NT:
            nc.vector.bn_stats(out=self.stats[:, k, :], in_=self.core.x[:, k, :]).then_inc(self.s_stats, 1)
            v.wait_ge(self.s_stats, k + 1)
            nc.vector.bn_aggr(out=self.meanvar[:, k, :], in_=self.stats[:, k, :]).then_inc(self.s_aggr, 1)

    def normalise(self, v, k):
        nc = self.nc
        t = k - 2
        if 0 <= t < NT:
            v.wait_ge(self.s_rstd, t + 1)
            wait(v, self.s_T, t - 1)
            nc.vector.tensor_scalar(self.xn[:, t % 2, :], self.core.x[:, t, :], self.meanvar[:, t, 0:1],
                                    self.rstd[:, t:t + 1], ALU.subtract, ALU.mult).then_inc(self.s_xn, 1)
        for t in [k - 3] if k < NT else {NT + 1: [NT - 3], NT + 2: [NT - 2, NT - 1]}.get(k, []):
            if t >= 0:
                v.wait_ge(self.s_hi, t + 1)
                nc.vector.tensor_tensor(self.lo[:, :, t * P:(t + 1) * P], self._psum(t),
                                        self.hi[:, :, t * P:(t + 1) * P], ALU.subtract).then_inc(self.s_lo, 1)

    def gpsimd(self, pool, k):
        self.variance(pool, k)
        self.newton(pool, k)

    def variance(self, pool, k):
        nc = self.nc
        if k < NT:
            pool.wait_ge(self.s_aggr, k + 1)
            nc.gpsimd.tensor_scalar(self.var[:, k:k + 1], self.meanvar[:, k, 1:2], LN_EPS, None, ALU.add)\
                .then_inc(self.s_var, 1)

    def newton(self, pool, k):
        nc = self.nc
        t = k - 1
        if 0 <= t < NT:
            c = slice(t, t + 1)
            pool.wait_ge(self.s_r0, t + 1)
            nc.gpsimd.tensor_tensor(self.corr[:, c], self.var[:, c], self.r0[:, c], ALU.mult).then_inc(self.s_corr, 1)
            pool.wait_ge(self.s_corr, 3 * t + 1)
            nc.gpsimd.tensor_tensor(self.corr[:, c], self.corr[:, c], self.r0[:, c], ALU.mult)\
                .then_inc(self.s_corr, 1)
            pool.wait_ge(self.s_corr, 3 * t + 2)
            nc.gpsimd.tensor_scalar(self.corr[:, c], self.corr[:, c], -0.5, 1.5, ALU.mult, ALU.add)\
                .then_inc(self.s_corr, 1)
            pool.wait_ge(self.s_corr, 3 * t + 3)
            nc.gpsimd.tensor_tensor(self.rstd[:, c], self.r0[:, c], self.corr[:, c], ALU.mult)\
                .then_inc(self.s_rstd, 1)

    def scalar(self, act, k):
        self.high(act, k)
        self.root(act, k)

    def high(self, act, k):
        t = k - 3
        if 0 <= t < NT:
            act.wait_ge(self.s_T, t + 1)
            self.nc.scalar.activation(self.hi[:, :, t * P:(t + 1) * P], self._psum(t), ACT.Copy)\
                .then_inc(self.s_hi, 1)

    def root(self, act, k):
        if k < NT:
            act.wait_ge(self.s_var, k + 1)
            self.nc.scalar.activation(self.sd[:, k:k + 1], self.var[:, k:k + 1], ACT.Sqrt).then_inc(self.s_sd, 1)

    def tensor(self, pe, k):
        if k == self.ahead_at:
            self._ahead(pe, 0, 0, KB)
        t = k - 3
        if 0 <= t < NT:
            pe.wait_ge(self.s_xn, t + 1)
            wait(pe, self.s_lo, t - 1)
            for b in range(KB):
                last = self.nc.tensor.transpose(self._psum(t)[:, b, :], self.xn[:, t % 2, b * P:(b + 1) * P],
                                                self.core.ident[:])
            last.then_inc(self.s_T, 1)
        if k == NT + 1:
            self._ahead(pe, 1, 0, KB // 2)
        if k == NT + 2:
            self._ahead(pe, 1, KB // 2, KB)

    def _ahead(self, pe, j, k0, k1):
        if j < len(self.first_products):
            out, pairs = self.first_products[j]
            pe.wait_ge(self.s_lo, NT // NH)
            pe.wait_ge(self.prefetch.s_lo, 1)
            product(self.nc, out, pairs[k0:k1], start=k0 == 0, stop=k1 == KB)


def first_products(core, columns):
    return [(core.bank(b), [(core.first.parts(c), (core.ln.hi[:, k, 0:HALF], core.ln.lo[:, k, 0:HALF]))
                            for k, c in enumerate(blocks)]) for b, blocks in columns]


def ffn0_first(core):
    return first_products(core, [(part, [(part * KB + k) * P for k in range(KB)]) for part in range(2)])


def qkv_first(core):
    return first_products(core, [(NH * h, [(k * FIRST + h) * HD for k in range(KB)]) for h in range(FIRST)])


def ffn1_first(core):
    return first_products(core, [(FFN1_BANK + part, [(part * KB + k) * P for k in range(KB)])
                                 for part in range(2)])


def retrieval_first(core):
    return first_products(core, [(0, [k * HD for k in range(KB)])])


def product(nc, out, pairs, start=True, stop=True):
    terms = []
    for (sh, sl), (mh, ml) in pairs:
        terms.append((sh, mh))
        if ml is not None:
            terms.append((sh, ml))
        if sl is not None:
            terms.append((sl, mh))
    for n, (s, m) in enumerate(terms):
        last = nc.tensor.matmul(out, s, m, start=(start and n == 0), stop=(stop and n == len(terms) - 1))
    return last


def setup_block(core, ins, following, ahead):
    nc = core.nc
    with ExitStack() as ctx:
        loaded = [core.semaphore(f"setup_loaded{t}") for t in range(NT)]
        made = core.semaphore("setup_made")
        prefetch = Prefetch(core, ctx, "setup", following)
        ln = LayerNorm(core, ctx, "setup", (6, 7), prefetch, ahead)
        block = core.open_block(ctx)

        @block.sync
        def _(sp):
            for t in range(NT):
                sp.dma_start(core.x[:, t, :], ins["x"][t * P:(t + 1) * P, :]).then_inc(loaded[t], 16)
                if t == 3:
                    prefetch.load(sp)

        @block.gpsimd
        def _(pool):
            nc.gpsimd.memset(core.ident[:], 0.0).then_inc(made, 1)
            pool.wait_ge(made, 1)
            nc.gpsimd.affine_select(out=core.ident[:], in_=core.ident[:], compare_op=ALU.not_equal, fill=1.0,
                                    base=0, pattern=[[-1, P]], channel_multiplier=1).then_inc(made, 1)
            nc.gpsimd.memset(core.half[:], 0.5)
            for k in range(ln.STEPS):
                if k == 5:
                    prefetch.low(pool, nc.gpsimd)
                ln.gpsimd(pool, k)

        @block.vector
        def _(v):
            for k in range(ln.STEPS):
                if k < NT:
                    v.wait_ge(loaded[k], 16)
                ln.vector_first(v, k)
                ln.vector(v, k)

        @block.scalar
        def _(act):
            for k in range(ln.STEPS):
                ln.scalar(act, k)
                if k == 3:
                    prefetch.high(act)

        @block.tensor
        def _(pe):
            pe.wait_ge(made, 2)
            for k in range(ln.STEPS):
                ln.tensor(pe, k)


def ffn0_block(core, ins, tag, following, ahead):
    nc = core.nc
    x, xT = core.x, core.ln
    with ExitStack() as ctx:
        def sb(name, shape, dt=F32):
            return ctx.enter_context(nc.sbuf_tensor(f"{tag}_{name}", shape, dt))

        def sem(name):
            return core.semaphore(f"{tag}_{name}")

        prefetch = Prefetch(core, ctx, tag, following)
        ln = LayerNorm(core, ctx, tag, (6, 7), prefetch, ahead)
        w = [core.first, Chunk(nc, ctx, f"{tag}_w12", raw=core.second_raw)]
        w3 = sb("w3", [P, MB0, DM])
        w3_hi, w3_lo = sb("w3_hi", [P, MB0, DM], F32R), sb("w3_lo", [P, MB0, DM], F32R)
        b12 = sb("b12", [P, 2 * MB0])
        b3 = sb("b3", [P, DM])
        sig = sb("sig", [P, 2, HALF])
        gated = sb("gated", [P, 2, HALF])
        h = sb("h", [P, 2, HALF])
        h_hi, h_lo = sb("h_hi", [P, MB0, TOK], F32R), sb("h_lo", [P, MB0, TOK], F32R)
        w_in = [sem(f"w_in{i}") for i in range(2)]
        w3_in, bias_in, b3_in = sem("w3_in"), sem("bias_in"), sem("b3_in")
        w_hi_done, w_lo_done = sem("w_hi_done"), sem("w_lo_done")
        w3_hi_done, w3_lo_done = sem("w3_hi_done"), sem("w3_lo_done")
        up_done, sig_done, gated_done, h_done = sem("up_done"), sem("sig_done"), sem("gated_done"), sem("h_done")
        h_hi_done, h_lo_done = sem("h_hi_done"), sem("h_lo_done")
        biased, down_done, added = sem("biased"), sem("down_done"), sem("added")
        block = core.open_block(ctx)
        units = [(mb, th) for mb in range(MB0) for th in range(NH)]

        def tok(th):
            return slice(th * HALF, (th + 1) * HALF)

        @block.sync
        def _(sp):
            sp.dma_start(b12[:], ins["b12T"]).then_inc(bias_in, 16)
            sp.dma_start(b3[:], ins["b3"].partition_broadcast(P)).then_inc(b3_in, 16)
            for b in range(2, MB0):
                wait(sp, w_lo_done, b - 2)
                sp.dma_start(w[b % 2].raw[:], ins["w12"][b]).then_inc(w_in[b % 2], 16)
                if b == 2:
                    sp.dma_start(w3[:], ins["w3T"]).then_inc(w3_in, 16)
            sp.wait_ge(up_done, NH * (MB0 - 1) - 1)
            sp.wait_ge(w_lo_done, MB0 - 1)
            prefetch.load(sp)

        @block.gpsimd
        def _(pool):
            pool.wait_ge(b3_in, 16)
            nc.gpsimd.tensor_tensor(b3[:], b3[:], core.half[:].broadcast_to([P, DM]), ALU.mult).then_inc(biased, 1)
            pool.wait_ge(biased, 1)
            for u, (mb, th) in enumerate(units):
                nc.gpsimd.tensor_tensor(x[:, u, :], x[:, u, :], b3[:], ALU.add).then_inc(biased, 1)
                pool.wait_ge(h_hi_done, u + 1)
                nc.gpsimd.tensor_tensor(h_lo[:, mb, tok(th)], h[:, u % 2, :], h_hi[:, mb, tok(th)], ALU.subtract)\
                    .then_inc(h_lo_done, 1)
                if th == 0:
                    pool.wait_ge(w3_hi_done, mb + 1)
                    nc.gpsimd.tensor_tensor(w3_lo[:, mb, :], w3[:, mb, :], w3_hi[:, mb, :], ALU.subtract)\
                        .then_inc(w3_lo_done, 1)
            for k in range(ln.STEPS):
                ln.gpsimd(pool, k)

        @block.vector
        def _(v):
            for u, (mb, th) in enumerate(units):
                x1, x2 = core.bank(2 * (u % 2)), core.bank(2 * (u % 2) + 1)
                if th == 0 and mb + 1 < MB0:
                    v.wait_ge(w_hi_done, mb + 1)
                    nxt = w[(mb + 1) % 2]
                    nc.vector.tensor_tensor(nxt.lo[:], nxt.raw[:], nxt.hi[:], ALU.subtract).then_inc(w_lo_done, 1)
                if u == 0:
                    v.wait_ge(bias_in, 16)
                if u == len(units) - 1:
                    prefetch.low(v, nc.vector)
                v.wait_ge(sig_done, u + 1)
                nc.vector.scalar_tensor_tensor(out=gated[:, u % 2, :], in0=x1, scalar=b12[:, mb:mb + 1],
                                               in1=sig[:, u % 2, :], op0=ALU.add, op1=ALU.mult)\
                    .then_inc(gated_done, 1)
                v.wait_ge(gated_done, u + 1)
                wait(v, h_lo_done, u - 1)
                nc.vector.scalar_tensor_tensor(out=h[:, u % 2, :], in0=x2, scalar=b12[:, MB0 + mb:MB0 + mb + 1],
                                               in1=gated[:, u % 2, :], op0=ALU.add, op1=ALU.mult)\
                    .then_inc(h_done, 1)
            for k in range(ln.STEPS):
                ln.vector_first(v, k)
                if k < NT:
                    v.wait_ge(down_done, k + 1)
                    v.wait_ge(biased, k + 2)
                    nc.vector.scalar_tensor_tensor(out=x[:, k, :], in0=core.bank(4 + k % 2), scalar=0.5,
                                                   in1=x[:, k, :], op0=ALU.mult, op1=ALU.add).then_inc(added, 1)
                    v.wait_ge(added, k + 1)
                ln.vector(v, k)

        @block.scalar
        def _(act):
            def w_split(b):
                wait(act, w_in[b % 2], 16 * (b // 2))
                wait(act, up_done, NH * (b - 1) - 1)
                nc.scalar.activation(w[b % 2].hi[:], w[b % 2].raw[:], ACT.Copy).then_inc(w_hi_done, 1)

            def split(u):
                mb, th = units[u]
                act.wait_ge(h_done, u + 1)
                nc.scalar.activation(h_hi[:, mb, tok(th)], h[:, u % 2, :], ACT.Copy).then_inc(h_hi_done, 1)

            for u, (mb, th) in enumerate(units):
                if th == 0 and mb + 1 < MB0:
                    w_split(mb + 1)
                if u == 0:
                    act.wait_ge(bias_in, 16)
                if u == len(units) - 1:
                    prefetch.high(act)
                wait(act, up_done, u)
                wait(act, gated_done, u - 1)
                nc.scalar.activation(sig[:, u % 2, :], core.bank(2 * (u % 2)), ACT.Sigmoid,
                                     bias=b12[:, mb:mb + 1]).then_inc(sig_done, 1)
                if th == 0:
                    act.wait_ge(w3_in, 16)
                    nc.scalar.activation(w3_hi[:, mb, :], w3[:, mb, :], ACT.Copy).then_inc(w3_hi_done, 1)
                if u >= 1:
                    split(u - 1)
            split(len(units) - 1)
            for k in range(ln.STEPS):
                ln.scalar(act, k)

        @block.tensor
        def _(pe):
            for u, (mb, th) in list(enumerate(units))[1:]:
                wait(pe, w_lo_done, mb)
                wait(pe, h_done, u - 1)
                for part in range(2):
                    last = product(nc, core.bank(2 * (u % 2) + part), [
                        (w[mb % 2].parts((part * KB + k) * P), (xT.hi[:, k, tok(th)], xT.lo[:, k, tok(th)]))
                        for k in range(KB)])
                last.then_inc(up_done, 1)

            def down(k, blocks):
                s = slice(k * P, (k + 1) * P)
                return product(nc, core.bank(4 + k % 2), [
                    ((h_hi[:, m, s], h_lo[:, m, s]), (w3_hi[:, m, :], w3_lo[:, m, :])) for m in blocks],
                    start=blocks[0] == 0, stop=blocks[-1] == MB0 - 1)

            pe.wait_ge(w3_lo_done, MB0 - 1)
            pe.wait_ge(h_lo_done, NH * (MB0 - 2) + 1)
            for k in range(2):
                down(k, range(MB0 - 1))
            pe.wait_ge(w3_lo_done, MB0)
            for k in range(ln.STEPS):
                if k < NT:
                    pe.wait_ge(h_lo_done, NH * (MB0 - 1) + k * P // HALF + 1)
                    wait(pe, added, k - 1)
                    down(k, range(MB0 - 1 if k < 2 else 0, MB0)).then_inc(down_done, 1)
                ln.tensor(pe, k)


def qkv_block(core, ins, scratch):
    nc = core.nc
    with ExitStack() as ctx:
        def sb(name, shape, dt=F32):
            return ctx.enter_context(nc.sbuf_tensor(f"qkv_{name}", shape, dt))

        def sem(name):
            return core.semaphore(f"qkv_{name}")

        Q, K, V = range(3)
        UNITS = 8
        xT = core.ln
        w = [sb(f"w{t}", [P, KB, HALF]) for t in range(3)]
        w_hi = [sb(f"w{t}_hi", [P, KB, HALF], F32R) for t in range(3)]
        w_lo = [sb(f"w{t}_lo", [P, KB, HALF], F32R) for t in range(3)]
        res = [sb(f"res{i}", [P, HALF]) for i in range(4)]
        sq = sb("sq", [P, 2, HALF])
        acc = [sb(f"acc{t}", [P, TOK]) for t in (Q, K)]
        ones = sb("ones", [P, P])
        bo = sb("bo", [P, DM])
        ms, sd, r0, corr, rs = (sb(n, [P, 2, NT]) for n in ("ms", "sd", "r0", "corr", "rs"))
        diag = sb("diag", [P, NT, P])
        w_in = [sem(f"w_in{t}") for t in range(3)]
        w_hi_done, w_lo_done, proj_done, res_done = (sem(n) for n in
                                                     ("w_hi_done", "w_lo_done", "proj_done", "res_done"))
        stored = [sem(f"stored{i}") for i in range(4)]
        sq_done, acc_done, sums_done, ms_done, sd_done, rs_done, diag_done, spread_done, rms_done = (
            sem(n) for n in ("sq_done", "acc_done", "sums_done", "ms_done", "sd_done", "rs_done", "diag_done",
                             "spread_done", "rms_done"))
        k_in, q_in, bo_in = sem("k_in"), sem("q_in"), sem("bo_in")
        kn_done, k0_hi_done = sem("kn_done"), sem("k0_hi_done")
        AT_SUMS, AT_SPREAD = 1, 3
        block = core.open_block(ctx)
        weights = [ins["Wq"], ins["Wk"], ins["Wv"]]
        bias = [core.cols["bq"], core.cols["bk"]]

        def groups(eng, body):
            body(0)
            with eng.Fori(1, NGROUPS - 1) as g:
                body(g)
            body(NGROUPS - 1)

        def is_last(g):
            return isinstance(g, int) and g == NGROUPS - 1

        @block.sync
        def _(sp):
            def load(g, t):
                wait(sp, w_hi_done, (g - 1) * 3 + t + 1)
                wait(sp, w_lo_done, (g - 1) * 3 + t + 1)
                sp.dma_start(w[t][:], weights[t][bass.ds(g, 1)].rearrange("a p k n -> p (a k) n"))\
                    .then_inc(w_in[t], 16)

            load(0, Q)
            sp.dma_start(bo[:], ins["bo"].partition_broadcast(P)).then_inc(bo_in, 16)
            for n in core.cols:
                sp.dma_start(core.cols[n][:], ins[n]).then_inc(core.cols_in, 16)
            load(0, K)

            def body(g):
                for t in (Q, K, V):
                    if t == Q:
                        load(g, V)
                    elif not is_last(g):
                        load(g + 1, t - 1)
                    elif t == V:
                        for i in range(4):
                            sp.wait_ge(stored[i], 6 * 16)
                        sp.dma_start(core.k_raw[:], scratch["k"][0]).then_inc(k_in, 16)
                        sp.dma_start(core.q_raw[:], scratch["q"][0]).then_inc(q_in, 16)
                    for u in range(UNITS):
                        sp.wait_ge(res_done, g * 24 + t * UNITS + u + 1)
                        if t == V:
                            dst = scratch["v"][bass.ds(g * GROUP, GROUP), :, u, :].rearrange("h p d -> p h d")
                            src = res[u % 4][:].rearrange("p (h d) -> p h d", h=GROUP)
                        else:
                            dst = scratch["qk"[t]][bass.ds(g * GROUP + u // 2, 1), :,
                                                   (u % 2) * HALF:(u % 2 + 1) * HALF]\
                                .rearrange("a p n -> p (a n)")
                            src = res[u % 4][:]
                        sp.dma_start(dst, src).then_inc(stored[u % 4], 16)

            groups(sp, body)
            for i in range(4):
                sp.wait_ge(stored[i], NGROUPS * 6 * 16)
            sp.wait_ge(q_in, 16)

        @block.scalar
        def _(act):
            def split(n, t, g):
                act.wait_ge(w_in[t], (g + 1) * 16)
                wait(act, proj_done, (n - 2) * UNITS - 1)
                nc.scalar.activation(w_hi[t][:], w[t][:], ACT.Copy).then_inc(w_hi_done, 1)

            split(0, Q, 0)

            def body(g):
                for t in (Q, K, V):
                    n = g * 3 + t
                    if t < V:
                        split(n + 1, t + 1, g)
                    elif not is_last(g):
                        split(n + 1, Q, g + 1)
                    for u in range(UNITS):
                        if t == V:
                            continue
                        m = g * 16 + t * UNITS + u
                        act.wait_ge(res_done, n * UNITS + u + 1)
                        wait(act, acc_done, m + 2 - 1)
                        nc.scalar.activation(sq[:, u % 2, :], res[u % 4][:], ACT.Square).then_inc(sq_done, 1)

            groups(act, body)
            act.wait_ge(ms_done, 1)
            nc.scalar.activation(sd[:], ms[:], ACT.Sqrt).then_inc(sd_done, 1)
            act.wait_ge(kn_done, 1)
            nc.scalar.activation(core.first.hi[:], core.kn[:], ACT.Copy).then_inc(k0_hi_done, 1)

        @block.vector
        def _(v):
            def split(n, t):
                v.wait_ge(w_hi_done, n + 1)
                nc.vector.tensor_tensor(w_lo[t][:], w[t][:], w_hi[t][:], ALU.subtract).then_inc(w_lo_done, 1)

            def factors():
                v.wait_ge(sums_done, 1)
                nc.vector.tensor_scalar(ms[:], core.bank(6)[:, 0:2 * NT].rearrange("p (a t) -> p a t", a=2),
                                        1.0 / INNER, RMS_EPS, ALU.mult, ALU.add).then_inc(ms_done, 1)
                v.wait_ge(sd_done, 1)
                nc.vector.reciprocal(r0[:], sd[:]).then_inc(rs_done, 1)
                v.wait_ge(rs_done, 1)
                nc.vector.tensor_tensor(corr[:], ms[:], r0[:], ALU.mult).then_inc(rs_done, 1)
                v.wait_ge(rs_done, 2)
                nc.vector.tensor_tensor(corr[:], corr[:], r0[:], ALU.mult).then_inc(rs_done, 1)
                v.wait_ge(rs_done, 3)
                nc.vector.tensor_scalar(corr[:], corr[:], -0.5, 1.5, ALU.mult, ALU.add).then_inc(rs_done, 1)
                v.wait_ge(rs_done, 4)
                nc.vector.tensor_tensor(rs[:], r0[:], corr[:], ALU.mult).then_inc(rs_done, 1)
                v.wait_ge(rs_done, 5)
                nc.vector.tensor_scalar(core.rms[:, TOK:TOK + NT], rs[:, 0, :], float(HD) ** -0.5, None,
                                        ALU.mult).then_inc(rms_done, 1)
                nc.vector.tensor_tensor(diag[:], core.ident[:].unsqueeze(1).broadcast_to([P, NT, P]),
                                        rs[:, 1, :].unsqueeze(2).broadcast_to([P, NT, P]), ALU.mult)\
                    .then_inc(diag_done, 1)

            split(0, Q)
            v.wait_ge(core.cols_in, 16 * len(core.cols))

            def body(g):
                for t in (Q, K, V):
                    n = g * 3 + t
                    if t < V or not is_last(g):
                        split(n + 1, (t + 1) % 3)
                    for u in range(UNITS):
                        wait(v, proj_done, n * UNITS + u)
                        wait(v, stored[u % 4], (g * 6 + t * 2 + u // 4) * 16)
                        wait(v, sq_done, g * 16 + max(min(t * UNITS + u - 3, 16), 0))
                        if t == V:
                            nc.vector.tensor_copy(res[u % 4][:], core.bank(u % 4)).then_inc(res_done, 1)
                        else:
                            nc.vector.tensor_scalar(res[u % 4][:], core.bank(u % 4),
                                                    bias[t][:, bass.ds(g * GROUP + u // 2, 1)], None, ALU.add)\
                                .then_inc(res_done, 1)
                        if is_last(g) and t == V and u == AT_SUMS + 1:
                            factors()
                        if is_last(g) and t == V and u == AT_SPREAD + 1:
                            v.wait_ge(spread_done, 1)
                            nc.vector.tensor_copy(core.rms[:, 0:TOK], core.ps[2][:]).then_inc(rms_done, 1)
                            v.wait_ge(k_in, 16)
                            v.wait_ge(rms_done, 2)
                            nc.vector.scalar_tensor_tensor(out=core.kn[:], in0=core.k_raw[:],
                                                           scalar=core.cols["gk"][:, 0:1], in1=core.rms[:, 0:TOK],
                                                           op0=ALU.mult, op1=ALU.mult).then_inc(kn_done, 1)

            groups(v, body)

        @block.gpsimd
        def _(pool):
            nc.gpsimd.memset(ones[:], 1.0)
            for t in (Q, K):
                nc.gpsimd.memset(acc[t][:], 0.0).then_inc(acc_done, 1)
            pool.wait_ge(acc_done, 2)
            pool.wait_ge(bo_in, 16)
            for t in range(NT):
                nc.gpsimd.tensor_tensor(core.x[:, t, :], core.x[:, t, :], bo[:], ALU.add)

            def body(g):
                for t in (Q, K):
                    for u in range(UNITS):
                        m = g * 16 + t * UNITS + u
                        pool.wait_ge(sq_done, m + 1)
                        pool.wait_ge(acc_done, m + 2)
                        part = acc[t][:, (u % 2) * HALF:(u % 2 + 1) * HALF]
                        nc.gpsimd.tensor_tensor(part, part, sq[:, u % 2, :], ALU.add).then_inc(acc_done, 1)

            groups(pool, body)
            pool.wait_ge(k0_hi_done, 1)
            nc.gpsimd.tensor_tensor(core.first.lo[:], core.kn[:], core.first.hi[:], ALU.subtract)

        @block.tensor
        def _(pe):
            def sums():
                pe.wait_ge(acc_done, 2 + NGROUPS * 16)
                for a in (Q, K):
                    for t in range(NT):
                        last = nc.tensor.matmul(core.bank(6)[:, a * NT + t:a * NT + t + 1],
                                                acc[a][:, t * P:(t + 1) * P], ones[:, 0:1], start=True, stop=True)
                last.then_inc(sums_done, 1)

            def spread():
                pe.wait_ge(diag_done, 1)
                for th in range(NH):
                    last = nc.tensor.matmul(core.bank(4 + th), ones[:], diag[:, 4 * th:4 * th + 4, :],
                                            start=True, stop=True)
                last.then_inc(spread_done, 1)

            def body(g):
                for t in (Q, K, V):
                    n = g * 3 + t
                    start = isinstance(g, int) and g == 0 and t == Q
                    if not start:
                        pe.wait_ge(w_lo_done, n + 1)
                    for u in range(UNITS):
                        if start and u == FIRST * NH:
                            pe.wait_ge(w_lo_done, 1)
                        if start and u in (0, NH):
                            continue
                        wait(pe, res_done, n * UNITS + u - 3)
                        if t == V:
                            s = slice(u * P, (u + 1) * P)
                            pairs = [((xT.hi[:, k, s], xT.lo[:, k, s]), (w_hi[t][:, k, :], w_lo[t][:, k, :]))
                                     for k in range(KB)]
                        else:
                            c = slice(u // 2 * HD, (u // 2 + 1) * HD)
                            s = slice((u % 2) * HALF, (u % 2 + 1) * HALF)
                            pairs = [((w_hi[t][:, k, c], w_lo[t][:, k, c]) if not start or u >= FIRST * NH
                                      else core.first.parts((k * FIRST + u // NH) * HD),
                                      (xT.hi[:, k, s], xT.lo[:, k, s])) for k in range(KB)]
                        product(nc, core.bank(u % 4), pairs).then_inc(proj_done, 2 if start and u == NH - 1 else 1)
                        if is_last(g) and t == V and u == AT_SUMS:
                            sums()
                        if is_last(g) and t == V and u == AT_SPREAD:
                            spread()

            groups(pe, body)


def attention_block(core, ins, scratch, following, ahead):
    nc = core.nc
    x = core.x
    T_LAG, PV_LAG, OUT_LAG, WO_LAG = 2, 6, 10, 12
    BODY = 2 * NT
    STEPS = HEADS * NT
    with ExitStack() as ctx:
        def sb(name, shape, dt=F32):
            return ctx.enter_context(nc.sbuf_tensor(f"at_{name}", shape, dt))

        def sem(name):
            return core.semaphore(f"at_{name}")

        def pair(name, shape):
            return [(sb(f"{name}{i}_hi", shape, F32R), sb(f"{name}{i}_lo", shape, F32R)) for i in range(2)]

        k_raw, q_raw, v_raw = core.k_raw, core.q_raw, sb("v_raw", [P, NT, HD])
        o_raw = sb("o_raw", [P, DM])
        kn = core.kn
        k2, q2 = ([(xT[:, 2 * i, :], xT[:, 2 * i + 1, :]) for i in range(2)] for xT in (core.ln.hi, core.ln.lo))
        v2 = pair("v", [P, NT, HD])
        o2 = pair("o", [P, DM])
        pT2 = pair("pT", [P, NT, HALF])
        y2 = pair("y", [P, HALF])
        y = sb("y", [P, HALF])
        probs = [sb(f"probs{i}", [P, TOK]) for i in range(4)]
        maxes, nbias, sums, rsums = (sb(n, [P, 4]) for n in ("maxes", "nbias", "sums", "rsums"))
        k_in, q_in, v_in, o_in = (sem(f"{n}_in") for n in ("k", "q", "v", "o"))
        kn_done = sem("kn_done")
        k_hi, k_lo, q_hi, q_lo, v_hi, v_lo, o_hi, o_lo = (
            sem(f"{n}_done") for n in ("k_hi", "k_lo", "q_hi", "q_lo", "v_hi", "v_lo", "o_hi", "o_lo"))
        s_scores, s_max, s_bias, s_exp, s_rsum, s_norm = (
            sem(n) for n in ("scores_done", "max_done", "bias_done", "exp_done", "rsum_done", "norm_done"))
        s_T, s_pT_hi, s_pT_lo = sem("transposed"), sem("pT_hi_done"), sem("pT_lo_done")
        s_pv, s_y, s_y_hi, s_y_lo = sem("pv_done"), sem("y_done"), sem("y_hi_done"), sem("y_lo_done")
        s_wo, s_added = sem("wo_done"), sem("added")
        prefetch = Prefetch(core, ctx, "at", following)
        ln = LayerNorm(core, ctx, "at", (2, 3), prefetch, ahead)
        block = core.open_block(ctx)
        rk, rq = core.rms[:, 0:TOK], core.rms[:, TOK:TOK + NT]
        gq, gk, bv = core.cols["gq"], core.cols["gk"], core.cols["bv"]
        T_BANKS, PV_BANK, WO_BANK = core.ps[2], 6, 7

        def scores(l):
            return core.ps[l % 2]

        def steps(eng, step):
            for l in range(BODY):
                step(0, l)
            with eng.Fori(1, STEPS // BODY - 1) as i:
                for l in range(BODY):
                    step(i, l)
            for l in range(BODY):
                step(STEPS // BODY - 1, l)
            for l in range(WO_LAG):
                step(STEPS // BODY, l)

        def exists(i, l, lag=0):
            return not isinstance(i, int) or 0 <= BODY * i + l - lag < STEPS

        def last_heads(i):
            return isinstance(i, int) and i == STEPS // BODY - 1

        def final(i, l):
            k = BODY * i + l - WO_LAG - (HEADS - 1) * NT if isinstance(i, int) else -1
            return k if k >= 0 else None

        def lagging(i, l, lag):
            m = (l - lag) % BODY
            return (BODY // 4 * i + (l - lag) // 4), (m // 4) % 2, m // NT, m % 4

        def next_head(i, l):
            h = 2 * i + l // NT + 1
            return h, (l // NT + 1) % 2, not isinstance(h, int) or h < HEADS

        @block.sync
        def _(sp):
            def load(dst, src, h, arrived):
                sp.dma_start(dst, src[bass.ds(h, 1)].rearrange("a p n -> p (a n)")).then_inc(arrived, 16)

            def head(h):
                if not isinstance(h, int) or h >= 1:
                    wait(sp, kn_done, h - 1)
                    load(k_raw[:], scratch["k"], h, k_in)
                    wait(sp, q_lo, h)
                    load(q_raw[:], scratch["q"], h, q_in)
                wait(sp, v_lo, h)
                wait(sp, v_hi, h)
                load(v_raw[:].rearrange("p t d -> p (t d)"), scratch["v_flat"], h, v_in)
                wait(sp, o_lo, h)
                wait(sp, o_hi, h)
                load(o_raw[:], ins["Wo"], h, o_in)

            head(0)
            head(1)
            with sp.Fori(2, HEADS) as h:
                head(h)
            prefetch.load(sp)

        @block.gpsimd
        def _(pool):
            def part_lo(dst, a, b, done, count, arrived):
                pool.wait_ge(arrived, count)
                nc.gpsimd.tensor_tensor(dst, a, b, ALU.subtract).then_inc(done, 1)

            def k_part(h, hp):
                part_lo(k2[hp][1], kn[:], k2[hp][0], k_lo, h, k_hi)

            def v_part(h, hp):
                part_lo(v2[hp][1][:], v_raw[:], v2[hp][0][:], v_lo, h + 1, v_hi)

            def step(i, l):
                p = BODY * i + l
                if exists(i, l):
                    pool.wait_ge(s_rsum, p + 1)
                    nc.gpsimd.tensor_tensor(probs[l % 4][:], probs[l % 4][:],
                                            rsums[:, l % 4:l % 4 + 1].broadcast_to([P, TOK]), ALU.mult)\
                        .then_inc(s_norm, 1)
                h, hp, there = next_head(i, l)
                if l % NT == 1 and there:
                    k_part(h, hp)
                if l % NT == 7 and there:
                    v_part(h, hp)
                if l == 0 and isinstance(i, int) and i == 0:
                    v_part(0, 0)
                if l % NT == 5 and exists(i, l):
                    hh, par = 2 * i + l // NT, l // NT
                    part_lo(o2[par][1][:], o_raw[:], o2[par][0][:], o_lo, hh + 1, o_hi)
                if l % 4 == OUT_LAG % 4 and exists(i, l, OUT_LAG):
                    J, jp, _, _ = lagging(i, l, OUT_LAG)
                    part_lo(y2[jp][1][:], y[:], y2[jp][0][:], s_y_lo, J + 1, s_y_hi)
                if last_heads(i) and l == 12:
                    prefetch.low(pool, nc.gpsimd)
                if final(i, l) is not None:
                    ln.gpsimd(pool, final(i, l))

            steps(pool, step)
            for k in range(NT, ln.STEPS):
                ln.gpsimd(pool, k)

        @block.scalar
        def _(act):
            def k_split(h, hp):
                wait(act, kn_done, h)
                wait(act, s_scores, (h - 1) * NT)
                nc.scalar.activation(k2[hp][0], kn[:], ACT.Copy).then_inc(k_hi, 1)

            def v_part(h, hp):
                act.wait_ge(v_in, (h + 1) * 16)
                wait(act, s_pv, 2 * h - 2)
                nc.scalar.activation(v2[hp][0][:], v_raw[:], ACT.Copy).then_inc(v_hi, 1)

            nc.scalar.preload_act_table(ACT.Exp)

            def step(i, l):
                p = BODY * i + l
                if exists(i, l, T_LAG):
                    q = p - T_LAG
                    J, jp, _, w = lagging(i, l, T_LAG)
                    for b in range(2):
                        act.wait_ge(s_T, 2 * q + b + 1)
                        if w == 0 and b == 0:
                            wait(act, s_pv, J - 1)
                        nc.scalar.activation(
                            pT2[jp][0][:, 4 * b:4 * b + 4, w * P:(w + 1) * P],
                            T_BANKS[:, b * HALF:(b + 1) * HALF].rearrange("p (k n) -> p k n", k=4),
                            ACT.Copy).then_inc(s_pT_hi, 1)
                if exists(i, l):
                    act.wait_ge(s_bias, p + 1)
                    wait(act, s_T, 2 * (p - 4) + 2)
                    nc.scalar.activation(probs[l % 4][:], scores(l)[:], ACT.Exp, bias=nbias[:, l % 4:l % 4 + 1],
                                         scale=rq[:, l % NT:l % NT + 1], accum_out=sums[:, l % 4:l % 4 + 1])\
                        .then_inc(s_exp, 1)
                if l % 4 == OUT_LAG % 4 and exists(i, l, OUT_LAG):
                    J, jp, _, _ = lagging(i, l, OUT_LAG)
                    act.wait_ge(s_y, J + 1)
                    wait(act, s_wo, 4 * (J - 1))
                    nc.scalar.activation(y2[jp][0][:], y[:], ACT.Copy).then_inc(s_y_hi, 1)
                h, hp, there = next_head(i, l)
                if l % NT == 1 and there:
                    k_split(h, hp)
                if l % NT == 7 and there:
                    v_part(h, hp)
                if l == 0 and isinstance(i, int) and i == 0:
                    v_part(0, 0)
                if l % NT == 5 and exists(i, l):
                    hh, par = 2 * i + l // NT, l // NT
                    act.wait_ge(o_in, (hh + 1) * 16)
                    wait(act, s_wo, (hh - 1) * NT)
                    nc.scalar.activation(o2[par][0][:], o_raw[:], ACT.Copy).then_inc(o_hi, 1)
                if last_heads(i) and l == 12:
                    prefetch.high(act)
                if final(i, l) is not None:
                    ln.scalar(act, final(i, l))

            steps(act, step)
            for k in range(NT, ln.STEPS):
                ln.scalar(act, k)

        @block.vector
        def _(v):
            def k_part(h):
                v.wait_ge(k_in, h * 16)
                wait(v, k_lo, h - 1)
                nc.vector.scalar_tensor_tensor(out=kn[:], in0=k_raw[:], scalar=gk[:, bass.ds(h, 1)], in1=rk,
                                               op0=ALU.mult, op1=ALU.mult).then_inc(kn_done, 1)

            def q_high(h, hp):
                wait(v, q_in, h * 16)
                wait(v, s_scores, (h - 1) * NT)
                nc.vector.tensor_scalar(q2[hp][0], q_raw[:], gq[:, bass.ds(h, 1)], None, ALU.mult)\
                    .then_inc(q_hi, 1)

            def q_low(h, hp):
                v.wait_ge(q_hi, h + 1)
                nc.vector.scalar_tensor_tensor(out=q2[hp][1], in0=q_raw[:], scalar=gq[:, bass.ds(h, 1)],
                                               in1=q2[hp][0], op0=ALU.mult, op1=ALU.subtract).then_inc(q_lo, 1)

            q_high(0, 0)
            q_low(0, 0)

            def step(i, l):
                p = BODY * i + l
                if l % 4 == OUT_LAG % 4 and exists(i, l, OUT_LAG):
                    J, _, _, _ = lagging(i, l, OUT_LAG)
                    head = 2 * i + (l - OUT_LAG) // NT
                    v.wait_ge(s_pv, J + 1)
                    wait(v, s_y_lo, J)
                    nc.vector.tensor_scalar(y[:], core.bank(PV_BANK), bv[:, bass.ds(head, 1)], None, ALU.add)\
                        .then_inc(s_y, 1)
                if exists(i, l):
                    v.wait_ge(s_scores, p + 1)
                    nc.vector.reduce_max(maxes[:, l % 4:l % 4 + 1], scores(l)[:], AX.X).then_inc(s_max, 1)
                    v.wait_ge(s_max, p + 1)
                    nc.vector.tensor_scalar(nbias[:, l % 4:l % 4 + 1], maxes[:, l % 4:l % 4 + 1],
                                            rq[:, l % NT:l % NT + 1], -1.0, ALU.mult, ALU.mult).then_inc(s_bias, 1)
                if exists(i, l, T_LAG):
                    q = p - T_LAG
                    _, jp, _, w = lagging(i, l, T_LAG)
                    for b in range(2):
                        v.wait_ge(s_pT_hi, 2 * q + b + 1)
                        out = (slice(None), slice(4 * b, 4 * b + 4), slice(w * P, (w + 1) * P))
                        nc.vector.tensor_tensor(
                            pT2[jp][1][out], T_BANKS[:, b * HALF:(b + 1) * HALF].rearrange("p (k n) -> p k n", k=4),
                            pT2[jp][0][out], ALU.subtract).then_inc(s_pT_lo, 1)
                if exists(i, l):
                    v.wait_ge(s_exp, p + 1)
                    nc.vector.reciprocal(rsums[:, l % 4:l % 4 + 1], sums[:, l % 4:l % 4 + 1]).then_inc(s_rsum, 1)
                if exists(i, l, WO_LAG):
                    _, jp, _, w = lagging(i, l, WO_LAG)
                    tile = jp * 4 + w
                    if final(i, l) is not None:
                        ln.vector_first(v, final(i, l))
                    v.wait_ge(s_wo, p - WO_LAG + 1)
                    wait(v, s_added, p - WO_LAG)
                    nc.vector.tensor_tensor(x[:, tile, :], core.bank(WO_BANK), x[:, tile, :], ALU.add)\
                        .then_inc(s_added, 1)
                    if final(i, l) is not None:
                        v.wait_ge(s_added, STEPS - NT + final(i, l) + 1)
                        ln.vector(v, final(i, l))
                h, hp, there = next_head(i, l)
                if l % NT == 0 and there:
                    k_part(h)
                if l % NT == 3 and there:
                    q_high(h, hp)
                if l % NT == 4 and there:
                    q_low(h, hp)

            steps(v, step)
            for k in range(NT, ln.STEPS):
                ln.vector_first(v, k)
                ln.vector(v, k)

        @block.tensor
        def _(pe):
            def step(i, l):
                p = BODY * i + l
                if exists(i, l):
                    qt, hp = l % NT, l // NT
                    (qh, ql), (kh, kl) = q2[hp], k2[hp]
                    if isinstance(i, int) and 2 * i + hp == 0:
                        kh, kl = core.first.hi, core.first.lo
                    elif qt == 0:
                        pe.wait_ge(k_hi, 2 * i + hp)
                        pe.wait_ge(k_lo, 2 * i + hp)
                    if qt == 0:
                        pe.wait_ge(q_hi, 2 * i + hp + 1)
                        pe.wait_ge(q_lo, 2 * i + hp + 1)
                    wait(pe, s_exp, p - 1)
                    s = slice(qt * P, (qt + 1) * P)
                    for n in range(NH):
                        m = slice(n * HALF, (n + 1) * HALF)
                        last = product(nc, scores(l)[:, m], [((qh[:, s], ql[:, s]), (kh[:, m], kl[:, m]))])
                    last.then_inc(s_scores, 1)
                if exists(i, l, T_LAG):
                    q = p - T_LAG
                    pe.wait_ge(s_norm, q + 1)
                    for b in range(2):
                        wait(pe, s_pT_lo, 2 * (q - 1) + b + 1)
                        for k in range(4 * b, 4 * b + 4):
                            last = nc.tensor.transpose(T_BANKS[:, k * P:(k + 1) * P],
                                                       probs[(l - T_LAG) % 4][:, k * P:(k + 1) * P], core.ident[:])
                        last.then_inc(s_T, 1)
                if exists(i, l, WO_LAG):
                    J, jp, hp, w = lagging(i, l, WO_LAG)
                    if w == 0:
                        pe.wait_ge(s_y_lo, J + 1)
                        if jp == 0:
                            pe.wait_ge(o_lo, 2 * i + (l - WO_LAG) // NT + 1)
                    wait(pe, s_added, p - WO_LAG)
                    s = slice(w * P, (w + 1) * P)
                    product(nc, core.bank(WO_BANK), [((y2[jp][0][:, s], y2[jp][1][:, s]),
                                                      (o2[hp][0][:], o2[hp][1][:]))]).then_inc(s_wo, 1)
                if exists(i, l, PV_LAG):
                    J, jp, hp, c = lagging(i, l, PV_LAG)
                    if c == 0:
                        pe.wait_ge(s_pT_lo, 8 * J + 8)
                        wait(pe, s_y, J)
                        if jp == 0:
                            pe.wait_ge(v_lo, 2 * i + (l - PV_LAG) // NT + 1)
                    terms = []
                    for k in (2 * c, 2 * c + 1):
                        (vh, vl), (ph, pl) = v2[hp], pT2[jp]
                        terms += [(vh, ph, k), (vh, pl, k), (vl, ph, k)]
                    for n, (a, b, k) in enumerate(terms):
                        last = nc.tensor.matmul(core.bank(PV_BANK), a[:, k, :], b[:, k, :], start=(c == 0 and n == 0),
                                                stop=(c == 3 and n == len(terms) - 1))
                    if c == 3:
                        last.then_inc(s_pv, 1)
                if final(i, l) is not None:
                    pe.wait_ge(s_exp, STEPS)
                    ln.tensor(pe, final(i, l))

            steps(pe, step)
            for k in range(NT, ln.STEPS):
                ln.tensor(pe, k)


class Truncation:

    def __init__(self, core, ctx, tag):
        self.nc = nc = core.nc

        def sb(name):
            return ctx.enter_context(nc.sbuf_tensor(f"{tag}_{name}", [P, 2, HALF], F32))

        def sem(name):
            return core.semaphore(f"{tag}_{name}")

        self.clipped, self.mag, self.sign, self.near, self.over = (
            sb(n) for n in ("clipped", "magnitude", "sign", "nearest", "over"))
        self.s_clip, self.s_mag, self.s_sign, self.s_near, self.s_over, self.s_floor, self.s_out = (
            sem(n) for n in ("clip_done", "magnitude_done", "sign_done", "nearest_done", "over_done", "floor_done",
                             "trunc_done"))

    def clip(self, v, n):
        s = n % 2
        self.nc.vector.tensor_scalar(self.clipped[:, s, :], self.clipped[:, s, :], -QSCALE, QSCALE - 1,
                                     ALU.max, ALU.min).then_inc(self.s_clip, 1)

    def magnitude(self, act, n, scale=1.0):
        s = n % 2
        act.wait_ge(self.s_clip, n + 1)
        wait(act, self.s_out, n - 1)
        self.nc.scalar.activation(self.mag[:, s, :], self.clipped[:, s, :], ACT.Abs, scale=scale)\
            .then_inc(self.s_mag, 1)
        self.nc.scalar.activation(self.sign[:, s, :], self.clipped[:, s, :], ACT.Sign).then_inc(self.s_sign, 1)

    def nearest(self, v, n):
        s = n % 2
        v.wait_ge(self.s_mag, n + 1)
        wait(v, self.s_out, n - 1)
        self.nc.vector.tensor_scalar(self.near[:, s, :], self.mag[:, s, :], ROUND, ROUND, ALU.add, ALU.subtract)\
            .then_inc(self.s_near, 1)
        v.wait_ge(self.s_near, n + 1)
        self.nc.vector.tensor_tensor(self.over[:, s, :], self.near[:, s, :], self.mag[:, s, :], ALU.is_gt)\
            .then_inc(self.s_over, 1)

    def lower(self, engine, eng, n):
        s = n % 2
        eng.wait_ge(self.s_over, n + 1)
        engine.tensor_tensor(self.near[:, s, :], self.near[:, s, :], self.over[:, s, :], ALU.subtract)\
            .then_inc(self.s_floor, 1)

    def signed(self, engine, eng, n, out):
        s = n % 2
        eng.wait_ge(self.s_floor, n + 1)
        eng.wait_ge(self.s_sign, n + 1)
        engine.tensor_tensor(out, self.near[:, s, :], self.sign[:, s, :], ALU.mult).then_inc(self.s_out, 1)


def ffn1_block(core, ins, tag, following=None, ahead=None, out=None):
    nc = core.nc
    x, xT = core.x, core.ln
    with ExitStack() as ctx:
        def sb(name, shape, dt=F32):
            return ctx.enter_context(nc.sbuf_tensor(f"{tag}_{name}", shape, dt))

        def sem(name):
            return core.semaphore(f"{tag}_{name}")

        prefetch = Prefetch(core, ctx, tag, following) if out is None else None
        ln = LayerNorm(core, ctx, tag, (4, 5), prefetch, ahead, NT - 1) if out is None else None
        tr = Truncation(core, ctx, tag)
        w = [core.first, Chunk(nc, ctx, f"{tag}_w", raw=core.second_raw)]
        wd = [sb(f"wd{i}", [P, DM]) for i in range(2)]
        wd_hi, wd_lo = sb("wd_hi", [P, IB, DM], F32R), sb("wd_lo", [P, IB, DM], F32R)
        sig = sb("sig", [P, 2, HALF])
        silu = sb("silu", [P, 2, HALF])
        inter = sb("inter", [P, IB, TOK], F32R)
        q8 = sb("q8", [P, 2, HALF])
        w_in = [sem(f"w_in{i}") for i in range(2)]
        wd_in = [sem(f"wd_in{i}") for i in range(2)]
        w_hi_done, w_lo_done, wd_hi_done, wd_lo_done = (
            sem(n) for n in ("w_hi_done", "w_lo_done", "wd_hi_done", "wd_lo_done"))
        up_done, sig_done, silu_done, prod_done = (
            sem(n) for n in ("up_done", "sig_done", "silu_done", "prod_done"))
        down_done, added, stored = sem("down_done"), sem("added"), sem("stored")
        block = core.open_block(ctx)
        UP_UNITS = IB * NH

        def up_bank(n, part):
            return core.bank((FFN1_BANK + 2 * n) % 6 + part)

        LN_LAG = 1
        AFTER = LN_LAG + (ln.STEPS - NT if ln else 0)

        @block.sync
        def _(sp):
            for b in range(IB):
                if b >= 2:
                    wait(sp, w_lo_done, b - 2)
                    sp.dma_start(w[b % 2].raw[:], ins["wgu"][b]).then_inc(w_in[b % 2], 16)
                wait(sp, wd_lo_done, b - 1)
                sp.dma_start(wd[b % 2][:], ins["wdT"][b]).then_inc(wd_in[b % 2], 16)
            if out is None:
                sp.wait_ge(up_done, UP_UNITS - 1)
                sp.wait_ge(w_lo_done, IB - 1)
                prefetch.load(sp)
            else:
                for t in range(NT):
                    sp.wait_ge(added, t + 1)
                    sp.dma_start(out[t * P:(t + 1) * P, :], x[:, t, :]).then_inc(stored, 16)
                sp.wait_ge(stored, 16 * NT)

        @block.gpsimd
        def _(pool):
            for b in range(IB):
                pool.wait_ge(wd_hi_done, b + 1)
                nc.gpsimd.tensor_tensor(wd_lo[:, b, :], wd[b % 2][:], wd_hi[:, b, :], ALU.subtract)\
                    .then_inc(wd_lo_done, 1)
                for th in range(NH):
                    tr.lower(nc.gpsimd, pool, NH * b + th)
                    tr.signed(nc.gpsimd, pool, NH * b + th, inter[:, b, th * HALF:(th + 1) * HALF])
            for k in range(NT + AFTER):
                if ln and k >= LN_LAG:
                    ln.newton(pool, k - LN_LAG)
                if k < NT - 1:
                    wait(pool, added, k - 1)
                    tr.lower(nc.gpsimd, pool, UP_UNITS + k)
                if ln and k >= LN_LAG:
                    ln.variance(pool, k - LN_LAG)
                if k < NT - 1:
                    tr.signed(nc.gpsimd, pool, UP_UNITS + k, q8[:, k % 2, :])
                if k == 1 and ln:
                    prefetch.low(pool, nc.gpsimd)

        @block.scalar
        def _(act):
            def w_split(b):
                wait(act, w_in[b % 2], 16 * (b // 2))
                wait(act, up_done, NH * (b - 1) - 1)
                nc.scalar.activation(w[b % 2].hi[:], w[b % 2].raw[:], ACT.Copy).then_inc(w_hi_done, 1)

            for n in range(UP_UNITS + 1):
                if n < UP_UNITS:
                    b, th = n // NH, n % NH
                    if th == 0:
                        if b + 1 < IB:
                            w_split(b + 1)
                        act.wait_ge(wd_in[b % 2], 16 * (b // 2 + 1))
                        nc.scalar.activation(wd_hi[:, b, :], wd[b % 2][:], ACT.Copy).then_inc(wd_hi_done, 1)
                    wait(act, up_done, n)
                    wait(act, silu_done, n - 1)
                    nc.scalar.activation(sig[:, n % 2, :], up_bank(n, 0), ACT.Sigmoid, scale=1.0 / QSCALE)\
                        .then_inc(sig_done, 1)
                if n >= 1:
                    tr.magnitude(act, n - 1)
            if out is None:
                prefetch.high(act)
            for k in range(NT + AFTER):
                if ln and k >= LN_LAG:
                    ln.high(act, k - LN_LAG)
                if k < NT:
                    tr.magnitude(act, UP_UNITS + k, scale=QSCALE)
                if ln and k >= LN_LAG:
                    ln.root(act, k - LN_LAG)

        @block.vector
        def _(v):
            def w_split(b):
                v.wait_ge(w_hi_done, b)
                nc.vector.tensor_tensor(w[b % 2].lo[:], w[b % 2].raw[:], w[b % 2].hi[:], ALU.subtract)\
                    .then_inc(w_lo_done, 1)

            for n in range(UP_UNITS + 1):
                if n < UP_UNITS:
                    b, th = n // NH, n % NH
                    if th == 0 and b + 1 < IB:
                        w_split(b + 1)
                    v.wait_ge(sig_done, n + 1)
                    nc.vector.scalar_tensor_tensor(out=silu[:, n % 2, :], in0=up_bank(n, 0),
                                                   scalar=1.0 / QSCALE, in1=sig[:, n % 2, :],
                                                   op0=ALU.mult, op1=ALU.mult).then_inc(silu_done, 1)
                    v.wait_ge(silu_done, n + 1)
                    wait(v, tr.s_sign, n - 1)
                    nc.vector.tensor_tensor(tr.clipped[:, n % 2, :], up_bank(n, 1),
                                            silu[:, n % 2, :], ALU.mult).then_inc(prod_done, 1)
                    v.wait_ge(prod_done, n + 1)
                    tr.clip(v, n)
                if n >= 1:
                    tr.nearest(v, n - 1)

            def add(t):
                v.wait_ge(tr.s_out, UP_UNITS + t + 1)
                nc.vector.scalar_tensor_tensor(out=x[:, t, :], in0=q8[:, t % 2, :], scalar=0.5, in1=x[:, t, :],
                                               op0=ALU.mult, op1=ALU.add).then_inc(added, 1)

            for k in range(NT + AFTER):
                if k < NT:
                    v.wait_ge(down_done, k + 1)
                    wait(v, tr.s_sign, UP_UNITS + k - 1)
                    nc.vector.tensor_scalar(tr.clipped[:, k % 2, :], core.bank(6 + k % 2), -1.0,
                                            (QSCALE - 1) / QSCALE, ALU.max, ALU.min).then_inc(tr.s_clip, 1)
                if ln and k >= LN_LAG:
                    ln.vector_first(v, k - LN_LAG)
                    ln.normalise(v, k - LN_LAG)
                if k < NT:
                    tr.nearest(v, UP_UNITS + k)
                if k - LN_LAG in range(NT):
                    add(k - LN_LAG)
                    v.wait_ge(added, k - LN_LAG + 1)
                if k == NT - 1:
                    tr.lower(nc.vector, v, UP_UNITS + k)
                    tr.signed(nc.vector, v, UP_UNITS + k, q8[:, k % 2, :])
                if ln and k >= LN_LAG:
                    ln.moments(v, k - LN_LAG)

        @block.tensor
        def _(pe):
            for n in range(1, UP_UNITS):
                b, th = n // NH, n % NH
                s = slice(th * HALF, (th + 1) * HALF)
                wait(pe, w_lo_done, b)
                wait(pe, prod_done, n - 2)
                for part in range(2):
                    last = product(nc, up_bank(n, part), [
                        (w[b % 2].parts((part * KB + k) * P), (xT.hi[:, k, s], xT.lo[:, k, s]))
                        for k in range(KB)])
                last.then_inc(up_done, 1)
            def down(k, blocks):
                return product(nc, core.bank(6 + k % 2), [
                    ((inter[:, b, k * P:(k + 1) * P], None), (wd_hi[:, b, :], wd_lo[:, b, :])) for b in blocks],
                    start=blocks[0] == 0, stop=blocks[-1] == IB - 1)

            pe.wait_ge(wd_lo_done, IB - 1)
            pe.wait_ge(tr.s_out, NH * (IB - 2) + 1)
            for k in range(2):
                down(k, range(IB - 1))
            pe.wait_ge(wd_lo_done, IB)
            for k in range(NT + AFTER):
                if k < NT:
                    wait(pe, tr.s_clip, UP_UNITS + k - 1)
                    pe.wait_ge(tr.s_out, NH * (IB - 1) + k * P // HALF + 1)
                    down(k, range(IB - 1 if k < 2 else 0, IB)).then_inc(down_done, 1)
                if ln and k >= LN_LAG:
                    ln.tensor(pe, k - LN_LAG)


def retrieval_block(core, ins, following, ahead):
    nc = core.nc
    x, xT = core.x, core.ln
    with ExitStack() as ctx:
        def sb(name, shape, dt=F32):
            return ctx.enter_context(nc.sbuf_tensor(f"rt_{name}", shape, dt))

        def sem(name):
            return core.semaphore(f"rt_{name}")

        prefetch = Prefetch(core, ctx, "rt", following)
        ln = LayerNorm(core, ctx, "rt", (6, 7), prefetch, ahead)
        RING = 3
        TH = NT // NH
        raws = [core.first.raw, core.second_raw]
        w = [core.first] + [Chunk(nc, ctx, f"rt_w{i}", HEADW, raw=raws[i % 2]) for i in range(1, RING)]
        bq = sb("bq", [P, KVH])
        WO_RING = 3
        wo = [sb(f"wo{i}", [P, 2, DM]) for i in range(WO_RING)]
        wo_hi, wo_lo = sb("wo_hi", [P, KVH, DM], F32R), sb("wo_lo", [P, KVH, DM], F32R)
        sig, r = sb("sig", [P, 2, HALF]), sb("r", [P, 2, HALF])
        ret = sb("ret", [P, 2, TH, HD])
        den, rden = sb("den", [P, 2, TH]), sb("rden", [P, 2, TH])
        sig_hi, sig_lo = sb("sig_hi", [P, 2, HALF], F32R), sb("sig_lo", [P, 2, HALF], F32R)
        ret_hi, ret_lo = sb("ret_hi", [P, KVH, TOK], F32R), sb("ret_lo", [P, KVH, TOK], F32R)
        w_in = [sem(f"w_in{i}") for i in range(2)]
        bq_in, wo_in = sem("bq_in"), [sem(f"wo_in{i}") for i in range(WO_RING)]
        w_hi_done, w_lo_done = sem("w_hi_done"), sem("w_lo_done")
        wo_pairs, wo_summed, wo_hi_done, wo_lo_done = (
            sem(n) for n in ("wo_pairs", "wo_summed", "wo_hi_done", "wo_lo_done"))
        q_done, neg_done, er_done, sig_done, sig_hi_done, sig_lo_done = (
            sem(n) for n in ("q_done", "neg_done", "er_done", "sig_done", "sig_hi_done", "sig_lo_done"))
        nd_done, den_done, rden_done, ret_done, ret_T, ret_hi_done, ret_lo_done = (
            sem(n) for n in ("nd_done", "den_done", "rden_done", "ret_done", "ret_transposed", "ret_hi_done",
                             "ret_lo_done"))
        y_done, added = sem("y_done"), sem("added")
        block = core.open_block(ctx)
        UNITS = KVH * NH
        LAG = 2
        def tok(n):
            return slice(n % NH * HALF, (n % NH + 1) * HALF)

        def wo_sum(h):
            return wo[(2 * h + 1) % WO_RING][:, 0, :]

        def nd_bank(m, pair):
            return core.bank(2 + 2 * (m % 2) + pair).rearrange("p (t n) -> p t n", t=2)

        @block.sync
        def _(sp):
            sp.dma_start(bq[:], ins["bq1T"]).then_inc(bq_in, 16)
            for h in range(KVH):
                for p in (2 * h, 2 * h + 1):
                    wait(sp, wo_lo_done if (p - WO_RING) % 2 else wo_summed, (p - WO_RING) // 2 + 1)
                    sp.dma_start(wo[p % WO_RING][:], ins["wo1T"][h, p % 2 * 2:p % 2 * 2 + 2]
                                 .rearrange("g e n -> e g n")).then_inc(wo_in[p % WO_RING], 16)
                if h + 2 < KVH:
                    wait(sp, w_lo_done, h)
                    sp.dma_start(raws[h % 2][:, :HEADW], ins["heads"][h + 2]).then_inc(w_in[h % 2], 16)
            sp.wait_ge(nd_done, NH * (KVH - 1))
            sp.wait_ge(w_lo_done, KVH - 1)
            prefetch.load(sp)

        @block.gpsimd
        def _(pool):
            def w_low(h):
                i, raw = h % RING, raws[h % 2]
                pool.wait_ge(w_hi_done, h)
                nc.gpsimd.tensor_tensor(w[i].lo[:, :HEADW], raw[:, :HEADW], w[i].hi[:, :HEADW], ALU.subtract)\
                    .then_inc(w_lo_done, 1)

            w_low(1)
            for n in range(UNITS):
                h, th = n // NH, n % NH
                pool.wait_ge(sig_hi_done, n + 1)
                nc.gpsimd.tensor_tensor(sig_lo[:, n % 2, :], sig[:, n % 2, :], sig_hi[:, n % 2, :], ALU.subtract)\
                    .then_inc(sig_lo_done, 1)
                two = wo[n % WO_RING]
                pool.wait_ge(wo_in[n % WO_RING], 16 * (n // WO_RING + 1))
                nc.gpsimd.tensor_tensor(two[:, 0, :], two[:, 0, :], two[:, 1, :], ALU.add).then_inc(wo_pairs, 1)
                if th == 1 and h + 2 < KVH:
                    w_low(h + 2)
            prefetch.low(pool, nc.gpsimd)
            for k in range(ln.STEPS):
                ln.gpsimd(pool, k)

        @block.scalar
        def _(act):
            def w_split(h):
                wait(act, w_in[h % 2], 16 * (h // 2))
                wait(act, nd_done, NH * (h + 1 - RING))
                nc.scalar.activation(w[h % RING].hi[:, :HEADW], raws[h % 2][:, :HEADW], ACT.Copy)\
                    .then_inc(w_hi_done, 1)

            w_split(1)
            act.wait_ge(bq_in, 16)
            for n in range(UNITS + LAG + 1):
                if n < UNITS:
                    h, th = n // NH, n % NH
                    act.wait_ge(neg_done, n + 1)
                    nc.scalar.activation(sig[:, n % 2, :], sig[:, n % 2, :], ACT.Exp)
                    wait(act, sig_done, n - 1)
                    nc.scalar.activation(r[:, n % 2, :], core.bank(n % 2), ACT.Relu, bias=bq[:, h:h + 1])\
                        .then_inc(er_done, 1)
                m = n - LAG - 1
                if m >= 0:
                    act.wait_ge(ret_T, m + 1)
                    nc.scalar.activation(ret_hi[:, m // NH, tok(m)], core.bank(6 + m % 2), ACT.Copy)\
                        .then_inc(ret_hi_done, 1)
                if n < UNITS:
                    act.wait_ge(sig_done, n + 1)
                    wait(act, nd_done, n - 1)
                    nc.scalar.activation(sig_hi[:, n % 2, :], sig[:, n % 2, :], ACT.Copy).then_inc(sig_hi_done, 1)
                if n % NH == 1 and n > 1:
                    act.wait_ge(wo_summed, n // NH)
                    nc.scalar.activation(wo_hi[:, n // NH - 1, :], wo_sum(n // NH - 1), ACT.Copy).then_inc(wo_hi_done, 1)
                if n % NH == 1 and n // NH + 2 < KVH:
                    w_split(n // NH + 2)
            prefetch.high(act)
            for k in range(ln.STEPS):
                ln.scalar(act, k)

        @block.vector
        def _(v):
            v.wait_ge(bq_in, 16)
            for n in range(UNITS + LAG + 1):
                h, th = n // NH, n % NH
                if n < UNITS:
                    wait(v, q_done, n)
                    wait(v, sig_lo_done, n - 1)
                    nc.vector.tensor_scalar(sig[:, n % 2, :], core.bank(n % 2), bq[:, h:h + 1], 0.0,
                                            ALU.add, ALU.min).then_inc(neg_done, 1)
                m = n - LAG
                if 0 <= m < UNITS:
                    v.wait_ge(nd_done, m + 1)
                    for pair in range(2):
                        nc.vector.tensor_scalar_add(den[:, m % 2, 2 * pair:2 * pair + 2], nd_bank(m, pair)[:, :, HD],
                                                    RET_EPS).then_inc(den_done, 1)
                    v.wait_ge(den_done, 2 * m + 2)
                    nc.vector.reciprocal(rden[:, m % 2, :], den[:, m % 2, :]).then_inc(rden_done, 1)
                    v.wait_ge(rden_done, m + 1)
                    wait(v, ret_T, m - 1)
                    for pair in range(2):
                        two = slice(2 * pair, 2 * pair + 2)
                        nc.vector.tensor_tensor(ret[:, m % 2, two, :], nd_bank(m, pair)[:, :, 0:HD],
                                                rden[:, m % 2, two].unsqueeze(2).broadcast_to([P, 2, HD]), ALU.mult)\
                            .then_inc(ret_done, 1)
                if n < UNITS:
                    v.wait_ge(er_done, n + 1)
                    nc.vector.tensor_tensor(sig[:, n % 2, :], sig[:, n % 2, :], r[:, n % 2, :], ALU.add)\
                        .then_inc(sig_done, 1)
                m = n - LAG - 1
                if m >= 0:
                    v.wait_ge(ret_hi_done, m + 1)
                    nc.vector.tensor_tensor(ret_lo[:, m // NH, tok(m)], core.bank(6 + m % 2),
                                            ret_hi[:, m // NH, tok(m)], ALU.subtract).then_inc(ret_lo_done, 1)
                if th == 1 and 1 <= h <= KVH:
                    v.wait_ge(wo_hi_done, h)
                    nc.vector.tensor_tensor(wo_lo[:, h - 1, :], wo_sum(h - 1), wo_hi[:, h - 1, :], ALU.subtract)\
                        .then_inc(wo_lo_done, 1)
                if th == 0 and 1 <= h <= KVH:
                    v.wait_ge(wo_pairs, NH * h)
                    nc.vector.tensor_tensor(wo_sum(h - 1), wo[2 * (h - 1) % WO_RING][:, 0, :], wo_sum(h - 1),
                                            ALU.add).then_inc(wo_summed, 1)
            for k in range(ln.STEPS):
                ln.vector_first(v, k)
                if k < NT:
                    v.wait_ge(y_done, k + 1)
                    nc.vector.tensor_tensor(x[:, k, :], core.bank(k % 2), x[:, k, :], ALU.add)\
                        .then_inc(added, 1)
                    v.wait_ge(added, k + 1)
                ln.vector(v, k)

        @block.tensor
        def _(pe):
            def project(t, heads):
                s = slice(t * P, (t + 1) * P)
                return product(nc, core.bank(t % 2), [
                    ((ret_hi[:, h, s], ret_lo[:, h, s]), (wo_hi[:, h, :], wo_lo[:, h, :])) for h in heads],
                    start=heads[0] == 0, stop=heads[-1] == KVH - 1)

            def num_den(m):
                pe.wait_ge(sig_lo_done, m + 1)
                wait(pe, ret_done, 2 * (m - 1))
                for t in range(TH):
                    s = slice(t * P, (t + 1) * P)
                    last = product(nc, nd_bank(m, t // 2)[:, t % 2, 0:MZ], [
                        ((sig_hi[:, m % 2, s], sig_lo[:, m % 2, s]), w[m // NH % RING].parts(KB * HD, MZ))])
                last.then_inc(nd_done, 1)

            def back(m):
                pe.wait_ge(ret_done, 2 * m + 2)
                wait(pe, ret_lo_done, m - 1)
                for t in range(TH):
                    last = nc.tensor.transpose(core.bank(6 + m % 2)[:, t * P:(t + 1) * P], ret[:, m % 2, t, :],
                                               core.ident[:])
                last.then_inc(ret_T, 1)

            for n in range(UNITS):
                wait(pe, w_lo_done, n // NH)
                wait(pe, er_done, n - 1)
                if n == 0:
                    continue
                product(nc, core.bank(n % 2), [
                    (w[n // NH % RING].parts(k * HD), (xT.hi[:, k, tok(n)], xT.lo[:, k, tok(n)]))
                    for k in range(KB)]).then_inc(q_done, 1)
                if n >= LAG:
                    num_den(n - LAG)
                if n >= LAG + 1:
                    back(n - LAG - 1)
            ready, rest = list(range(KVH - 2)), [KVH - 2, KVH - 1]
            pe.wait_ge(wo_lo_done, KVH - 2)
            pe.wait_ge(ret_lo_done, NH * (KVH - 2))
            pe.wait_ge(er_done, UNITS)
            project(0, ready)
            num_den(UNITS - 2)
            back(UNITS - 3)
            project(1, ready)
            num_den(UNITS - 1)
            back(UNITS - 2)
            pe.wait_ge(wo_lo_done, KVH)
            for k in range(ln.STEPS):
                if k < NT:
                    pe.wait_ge(ret_lo_done, UNITS - NH + k * P // HALF + 1)
                    wait(pe, added, k - 1)
                    project(k, rest if k < 2 else ready + rest).then_inc(y_done, 1)
                if k == 0:
                    back(UNITS - 1)
                ln.tensor(pe, k)


def macaron(nc, ins, out):
    scratch = {n: nc.dram_tensor(f"scratch_{n}", [HEADS, P, TOK], F32).ap() for n in "qk"}
    v = nc.dram_tensor("scratch_v", [HEADS, P, NT, HD], F32).ap()
    scratch["v"] = v
    scratch["v_flat"] = v.rearrange("h p t d -> h p (t d)")
    with ExitStack() as ctx:
        core = Core(nc, ctx)
        wq_first = ins["Wq_first"].rearrange("p k n -> p (k n)")
        setup_block(core, ins, following=(ins["w12"][0], ins["w12"][1]), ahead=ffn0_first)
        ffn0_block(core, ins, "f0a", following=(wq_first,), ahead=qkv_first)
        with ExitStack() as attention:
            core.open_attention(attention)
            qkv_block(core, ins, scratch)
            attention_block(core, ins, scratch, following=(ins["w12"][0], ins["w12"][1]), ahead=ffn0_first)
        ffn0_block(core, ins, "f0b", following=(ins["wgu"][0], ins["wgu"][1]), ahead=ffn1_first)
        ffn1_block(core, ins, "f1a", following=(ins["heads"][0], ins["heads"][1]), ahead=retrieval_first)
        retrieval_block(core, ins, following=(ins["wgu"][0], ins["wgu"][1]), ahead=ffn1_first)
        ffn1_block(core, ins, "f1b", out=out)


def kernel(**inputs):
    import numpy as np
    import concourse.bacc as bacc
    from concourse.bass_utils import run_bass_kernel_spmd

    a = {n: np.asarray(v) for n, v in inputs.items()}
    c = np.ascontiguousarray

    def blocks(w, n=P):
        return c(w.reshape(-1, n, w.shape[1]).transpose(1, 0, 2))

    def chunks(w):
        return c(w.reshape(KB, P, -1, HALF).transpose(2, 1, 0, 3))

    def cols(b):
        return c(b.reshape(-1, P).T)

    def padded(w):
        z = np.zeros((IB * P, w.shape[1]), w.dtype)
        z[:w.shape[0]] = w
        return z

    def paired(u, w):
        u, w = (m.reshape(-1, P, KB, P) for m in (u, w))
        return c(np.stack([u, w], axis=1).transpose(0, 4, 1, 3, 2).reshape(-1, P, 2 * KB * P))

    wq1 = a["L1_attn_Wq"].reshape(KVH, REP, HD, KB, P)[:, 0].transpose(0, 3, 2, 1)
    arrays = {
        "x": c(a["L0_attn_hidden_states"].reshape(TOK, DM)),
        "w12": paired(a["L0_ffn_w12"][:M0], a["L0_ffn_w12"][M0:]), "b12T": cols(a["L0_ffn_b12"]),
        "w3T": blocks(a["L0_ffn_w3"].T), "b3": c(a["L0_ffn_b3"]),
        "Wq": chunks(a["L0_attn_Wq"]), "Wk": chunks(a["L0_attn_Wk"]), "Wv": chunks(a["L0_attn_Wv"]),
        "Wq_first": c(blocks(a["L0_attn_Wq"])[:, :, :CHUNK // KB]),
        "Wo": c(a["L0_attn_Wo"].reshape(HEADS, HD, DM)), "bo": c(a["L0_attn_bo"]),
        "bq": cols(a["L0_attn_bq"]), "bk": cols(a["L0_attn_bk"]), "bv": cols(a["L0_attn_bv"]),
        "gq": cols(a["L0_attn_gq"]), "gk": cols(a["L0_attn_gk"]),
        "wgu": paired(padded(a["L1_ffn_w_gate"]), padded(a["L1_ffn_w_up"])),
        "wdT": padded(a["L1_ffn_w_down"].T).reshape(IB, P, DM),
        "heads": c(np.concatenate([wq1.reshape(KVH, P, KB * HD), a["L1_attn_M"],
                                   a["L1_attn_z"][:, :, None], np.zeros((KVH, P, 1), np.float32)], axis=2)),
        "bq1T": cols(a["L1_attn_bq"].reshape(KVH, REP, HD)[:, 0].reshape(-1)),
        "wo1T": c(a["L1_attn_Wo"].T.reshape(KVH, REP, HD, DM)),
    }
    nc = bacc.Bacc("TRN2", target_bir_lowering=False, num_devices=1)
    ins = {n: nc.dram_tensor(f"in_{n}", v.shape, mybir.dt.from_np(v.dtype), kind="ExternalInput").ap()
           for n, v in arrays.items()}
    out = nc.dram_tensor("out_x", (TOK, DM), F32, kind="ExternalOutput").ap()
    macaron(nc, ins, out)
    r = run_bass_kernel_spmd(nc, [{f"in_{n}": v for n, v in arrays.items()}], core_ids=[0])
    return r.results[0]["out_x"].reshape(1, TOK, DM)
```
